# Optimizing a Trainium2 kernel written in Bass

```python
import numpy as np
import jax
import jax.numpy as jnp

def _softmax(x, axis=-1):
    return jax.nn.softmax(x, axis=axis)

def _gelu(x):
    return jax.nn.gelu(x, approximate=True)

def _silu(x):
    return jax.nn.silu(x)

def _sigmoid(x):
    return jax.nn.sigmoid(x)

def _layernorm(x, axis=-1, eps=1e-05):
    m = jnp.mean(x, axis=axis, keepdims=True)
    v = jnp.var(x, axis=axis, keepdims=True)
    return (x - m) / jnp.sqrt(v + eps)

def _scatter_add(tgt, idx, src, axis=0):
    return tgt.at[idx].add(src)

def _segment_sum(src, seg, n):
    return jax.ops.segment_sum(src, seg, n)
kernel_name = 'mk_adj_ffn_d1_adj_r2_87bd6e'

def setup_inputs(seed: int=0):
    np.random.seed(seed)
    _w = jnp.asarray

    def _rec_inputs():
        import jax
        import jax.numpy as jnp
        _gk = jax.random.key(seed)
        x = -0.0002928 + 1 * jax.random.normal(jax.random.fold_in(_gk, 1), (4096, 512), jnp.float32)
        _a = jax.random.bernoulli(jax.random.fold_in(_gk, 2), 0.000976562, (4096, 4096))
        _af = _a.astype(jnp.float32)
        adj = _af
        return (x, adj)
    x, adj = _rec_inputs()

    def _L0_gnn_setup():
        import jax, jax.numpy as jnp
        import numpy as np
        import math
        SENT_DIM = 512
        N_SENT = 2048
        key = jax.random.key(seed)
        ks = jax.random.split(key, 8)
        D = SENT_DIM
        s = 1.0 / math.sqrt(D)
        return {'sent_embed': jax.random.normal(ks[0], (N_SENT, D), dtype=jnp.float32), 'adj_tensor': jax.random.randint(ks[1], (N_SENT, N_SENT), 0, 2).astype(jnp.float32), 'W_q': jax.random.uniform(ks[2], (D, D), jnp.float32, -s, s), 'b_q': jax.random.uniform(ks[3], (D,), jnp.float32, -s, s), 'W_k': jax.random.uniform(ks[4], (D, D), jnp.float32, -s, s), 'b_k': jax.random.uniform(ks[5], (D,), jnp.float32, -s, s), 'W_v': jax.random.uniform(ks[6], (D, D), jnp.float32, -s, s), 'b_v': jax.random.uniform(ks[7], (D,), jnp.float32, -s, s)}
    _L0_gnn_all = _L0_gnn_setup()
    _L0_gnn_in = {k: v for k, v in _L0_gnn_all.items() if k in ('W_q', 'b_q', 'W_k', 'b_k', 'W_v', 'b_v')}
    del _L0_gnn_all

    def _L0_ffn_setup():
        import jax, jax.numpy as jnp
        import numpy as np
        from functools import partial
        DIM = 512
        LIGHT_HID = 256
        HEAVY_HID = 2048
        NUM_HEAVY = 512
        N_ITERS = 50
        K_ROUTE = 8.0
        EPS = 0.1

        def rms_norm(x, gamma):
            norm = jnp.linalg.norm(x, axis=-1, keepdims=True)
            normed = x / jnp.maximum(norm, 1e-12)
            return normed * x.shape[-1] ** 0.5 * gamma

        def ffn(x, gamma, w1, b1, w2, b2):
            h = rms_norm(x, gamma)
            h = jax.nn.gelu(h @ w1 + b1, approximate=False)
            return h @ w2 + b2

        def coor_descent_route(x, routing_token, num_tokens):
            s = jnp.einsum('bnd,d->bn', x, routing_token)
            constant = EPS * jnp.log(jnp.asarray(K_ROUTE, dtype=s.dtype))
            b0 = -jax.nn.relu(s)
            a0 = jnp.zeros((s.shape[0], 1), dtype=s.dtype)

            def step(carry, _):
                a_prev, b = carry
                a = constant - EPS * jax.nn.logsumexp((s + b) / EPS, axis=-1, keepdims=True)
                b = -jax.nn.relu(s + a)
                return ((a, b), None)
            (a, b), _ = jax.lax.scan(step, (a0, b0), None, length=N_ITERS)
            scores = jnp.exp((s + a + b) / EPS)
            sel_scores, sel_idx = jax.lax.top_k(scores, num_tokens)
            sel_scores = sel_scores + jax.lax.stop_gradient(1.0 - sel_scores)
            return (sel_scores, sel_idx)
        key = jax.random.key(seed)
        ks = jax.random.split(key, 12)

        def lin(k, fan_in, fan_out):
            lim = 1.0 / np.sqrt(fan_in)
            kw, kb = jax.random.split(k)
            w = jax.random.uniform(kw, (fan_in, fan_out), jnp.float32, -lim, lim)
            b = jax.random.uniform(kb, (fan_out,), jnp.float32, -lim, lim)
            return (w, b)
        x = jax.random.normal(ks[0], (4, 4096, DIM), jnp.float32)
        routing_token = jax.random.normal(ks[1], (DIM,), jnp.float32)
        gamma_light = jnp.ones((DIM,), jnp.float32)
        w1_l, b1_l = lin(ks[2], DIM, LIGHT_HID)
        w2_l, b2_l = lin(ks[3], LIGHT_HID, DIM)
        gamma_heavy = jnp.ones((DIM,), jnp.float32)
        w1_h, b1_h = lin(ks[4], DIM, HEAVY_HID)
        w2_h, b2_h = lin(ks[5], HEAVY_HID, DIM)
        return dict(x=x, routing_token=routing_token, gamma_light=gamma_light, w1_light=w1_l, b1_light=b1_l, w2_light=w2_l, b2_light=b2_l, gamma_heavy=gamma_heavy, w1_heavy=w1_h, b1_heavy=b1_h, w2_heavy=w2_h, b2_heavy=b2_h)
    _L0_ffn_all = _L0_ffn_setup()
    _L0_ffn_in = {k: v for k, v in _L0_ffn_all.items() if k in ('routing_token', 'gamma_light', 'w1_light', 'b1_light', 'w2_light', 'b2_light', 'gamma_heavy', 'w1_heavy', 'b1_heavy', 'w2_heavy', 'b2_heavy')}
    del _L0_ffn_all
    return {'x': x, 'adj': adj, 'L0_gnn_W_q': _L0_gnn_in['W_q'], 'L0_gnn_b_q': _L0_gnn_in['b_q'], 'L0_gnn_W_k': _L0_gnn_in['W_k'], 'L0_gnn_b_k': _L0_gnn_in['b_k'], 'L0_gnn_W_v': _L0_gnn_in['W_v'], 'L0_gnn_b_v': _L0_gnn_in['b_v'], 'L0_ffn_routing_token': _L0_ffn_in['routing_token'], 'L0_ffn_gamma_light': _L0_ffn_in['gamma_light'], 'L0_ffn_w1_light': _L0_ffn_in['w1_light'], 'L0_ffn_b1_light': _L0_ffn_in['b1_light'], 'L0_ffn_w2_light': _L0_ffn_in['w2_light'], 'L0_ffn_b2_light': _L0_ffn_in['b2_light'], 'L0_ffn_gamma_heavy': _L0_ffn_in['gamma_heavy'], 'L0_ffn_w1_heavy': _L0_ffn_in['w1_heavy'], 'L0_ffn_b1_heavy': _L0_ffn_in['b1_heavy'], 'L0_ffn_w2_heavy': _L0_ffn_in['w2_heavy'], 'L0_ffn_b2_heavy': _L0_ffn_in['b2_heavy']}

def reference(x, adj, L0_gnn_W_q, L0_gnn_b_q, L0_gnn_W_k, L0_gnn_b_k, L0_gnn_W_v, L0_gnn_b_v, L0_ffn_routing_token, L0_ffn_gamma_light, L0_ffn_w1_light, L0_ffn_b1_light, L0_ffn_w2_light, L0_ffn_b2_light, L0_ffn_gamma_heavy, L0_ffn_w1_heavy, L0_ffn_b1_heavy, L0_ffn_w2_heavy, L0_ffn_b2_heavy):
    import jax
    import jax.numpy as jnp

    def _L0_gnn_ref(sent_embed, adj_tensor, W_q, b_q, W_k, b_k, W_v, b_v):
        import jax, jax.numpy as jnp
        import numpy as np
        import math
        SENT_DIM = 512
        N_SENT = 2048
        q = sent_embed @ W_q.T + b_q
        k = sent_embed @ W_k.T + b_k
        v = sent_embed @ W_v.T + b_v
        scale = 1.0 / math.sqrt(sent_embed.shape[-1])
        z = scale * (q @ k.T)
        spare_z = z * adj_tensor
        spare_z = jnp.where(spare_z == 0.0, jnp.asarray(-10000.0, spare_z.dtype), spare_z)
        attn = jax.nn.softmax(spare_z, axis=1)
        out = attn @ v
        return jax.nn.relu(out)

    def _L0_ffn_ref(x, routing_token, gamma_light, w1_light, b1_light, w2_light, b2_light, gamma_heavy, w1_heavy, b1_heavy, w2_heavy, b2_heavy):
        import jax, jax.numpy as jnp
        import numpy as np
        from functools import partial
        DIM = 512
        LIGHT_HID = 256
        HEAVY_HID = 2048
        NUM_HEAVY = 512
        N_ITERS = 50
        K_ROUTE = 8.0
        EPS = 0.1

        def rms_norm(x, gamma):
            norm = jnp.linalg.norm(x, axis=-1, keepdims=True)
            normed = x / jnp.maximum(norm, 1e-12)
            return normed * x.shape[-1] ** 0.5 * gamma

        def ffn(x, gamma, w1, b1, w2, b2):
            h = rms_norm(x, gamma)
            h = jax.nn.gelu(h @ w1 + b1, approximate=False)
            return h @ w2 + b2

        def coor_descent_route(x, routing_token, num_tokens):
            s = jnp.einsum('bnd,d->bn', x, routing_token)
            constant = EPS * jnp.log(jnp.asarray(K_ROUTE, dtype=s.dtype))
            b0 = -jax.nn.relu(s)
            a0 = jnp.zeros((s.shape[0], 1), dtype=s.dtype)

            def step(carry, _):
                a_prev, b = carry
                a = constant - EPS * jax.nn.logsumexp((s + b) / EPS, axis=-1, keepdims=True)
                b = -jax.nn.relu(s + a)
                return ((a, b), None)
            (a, b), _ = jax.lax.scan(step, (a0, b0), None, length=N_ITERS)
            scores = jnp.exp((s + a + b) / EPS)
            sel_scores, sel_idx = jax.lax.top_k(scores, num_tokens)
            sel_scores = sel_scores + jax.lax.stop_gradient(1.0 - sel_scores)
            return (sel_scores, sel_idx)
        bsz = x.shape[0]
        light_out = ffn(x, gamma_light, w1_light, b1_light, w2_light, b2_light)
        sel_scores, sel_idx = coor_descent_route(x, routing_token, NUM_HEAVY)
        batch_range = jnp.arange(bsz)[:, None]
        routed = x[batch_range, sel_idx]
        routed_out = ffn(routed, gamma_heavy, w1_heavy, b1_heavy, w2_heavy, b2_heavy)
        routed_out = routed_out * sel_scores[..., None]
        heavy_out = jnp.zeros_like(x).at[batch_range, sel_idx].set(routed_out)
        return light_out + heavy_out
    x = x + _L0_gnn_ref(_layernorm(x, axis=-1), adj, L0_gnn_W_q, L0_gnn_b_q, L0_gnn_W_k, L0_gnn_b_k, L0_gnn_W_v, L0_gnn_b_v)
    x = x + _L0_ffn_ref(_layernorm(x, axis=-1)[None], L0_ffn_routing_token, L0_ffn_gamma_light, L0_ffn_w1_light, L0_ffn_b1_light, L0_ffn_w2_light, L0_ffn_b2_light, L0_ffn_gamma_heavy, L0_ffn_w1_heavy, L0_ffn_b1_heavy, L0_ffn_w2_heavy, L0_ffn_b2_heavy)[0]
    return x

_drawn_inputs = setup_inputs


def setup_inputs(seed=0):
    import zlib

    import numpy as np

    out = dict(_drawn_inputs(seed))
    spreads = {'L0_ffn_gamma_light': (1.0, 0.2), 'L0_ffn_gamma_heavy': (1.0, 0.6)}
    factors = {'L0_gnn_b_q': 8.0,
     'L0_gnn_b_k': 8.0,
     'L0_gnn_b_v': 2.956,
     'L0_ffn_b1_light': 6.267,
     'L0_ffn_b1_heavy': 8.0,
     'L0_ffn_b2_heavy': 8.0}
    for name, (base, spread) in spreads.items():
        noise = np.random.default_rng([zlib.crc32(name.encode()), seed]).standard_normal(out[name].shape)
        drawn = base * np.exp(spread * noise) if base else spread * noise
        out[name] = jnp.asarray(drawn.astype(out[name].dtype))
    for name, factor in factors.items():
        out[name] = (out[name] * factor).astype(out[name].dtype)
    return out
```

```python
from contextlib import ExitStack

import numpy as np

import concourse.bass as bass
from concourse import mybir

ALU = mybir.AluOpType
ACT = mybir.ActivationFunctionType
AX_X = mybir.AxisListType.X
F32 = mybir.dt.float32
F16 = mybir.dt.float16
I32 = mybir.dt.int32
U32 = mybir.dt.uint32

P = 128
N = 4096
D = 512
HL = 256
HH = 2048
ROUTED = 512
NT = N // P
KC = D // P
GROUP = 4
NG = NT // GROUP
YS = 64.0
MS = 1024.0
ZS = YS * YS
SCALE = 1.0 / (ZS * float(np.sqrt(D)))
MASKED = -10000.0 / SCALE
PS = 4096.0
EPS_LN = 1e-5


class Chain:

    def __init__(self, eng, sem):
        self.eng, self.sem, self.n, self.base = eng, sem, 0, 0

    def step(self, ins):
        self.n += 1
        ins.then_inc(self.sem, 1)
        self.eng.wait_ge(self.sem, self.base + self.n)


class Semaphores:

    def __init__(self, nc):
        self.nc, self.held = nc, []

    def __call__(self, name):
        self.held.append(self.nc.alloc_semaphore(name=name))
        return self.held[-1]

    def done(self):
        self.nc.all_engine_barrier()
        self.nc.clear_and_free_semaphores([h for h in self.held])
        self.nc.all_engine_barrier()
        self.held = []


def gnn_ffn_kernel(nc, x, adj, adj_t, wq, bq, wk, bk, wv_t, bv, rtok, gl, w1l, b1l, w2l, b2l,
                   gh, w1h, b1h, w2h, b2h, out):
    ytab = nc.dram_tensor("ytab", (N, 2 * D), F16).ap()
    qtab = nc.dram_tensor("qtab", (NT, P, KC * 2 * P), F16).ap()
    wtab = nc.dram_tensor("wtab", (10, P, 2 * 2048), F16).ap()
    x1tab = nc.dram_tensor("x1tab", (N, D), F32).ap()
    y2rows = nc.dram_tensor("y2rows", (N, D), F32).ap()
    y2ttab = nc.dram_tensor("y2ttab", (NT, P, KC * 2 * P), F16).ap()
    with ExitStack() as ctx:
        def sb(name, shape, dt, c=ctx):
            return c.enter_context(nc.sbuf_tensor(name, shape, dt))

        keep = {
            "cs": sb("cs", [P, NT], F32), "bvb": sb("bvb", [P, D], F32),
            "wv": sb("wv", [P, KC, 2, D], F16), "ident": sb("ident", [P, P], F32),
            "zeros": sb("zeros", [P, D], F16), "ident16": sb("ident16", [P, P], F16), "s": sb("s", [P, NT], F32),
            "valid": sb("valid", [P, NT, CH], F32), "index": sb("index", [P, NT, 2, CH], I32),
            "overflow": sb("overflow", [P, 1], I32), "nz": sb("nz", [P, NT, NT], F32), "ytot": sb("ytot", [P, D], F32), "ones16": sb("ones16", [P, P], F16),
        }
        sem = Semaphores(nc)
        split_weights(nc, keep, wk=wk, wq=wq, bq=bq, bk=bk, wv_t=wv_t, bv=bv, gl=gl, w1l=w1l, w2l=w2l,
                      gh=gh, w1h=w1h, w2h=w2h, wtab=wtab, sem=sem, x=x, ytab=ytab, qtab=qtab, adj_t=adj_t)
        list_neighbours(nc, keep, sem)
        sem.done()
        overflow = nc.values_load(keep["overflow"][0:1, 0:1], min_val=0, max_val=P)
        with nc.If(overflow == 0):
            attend_listed(nc, keep, x, adj_t, rtok, ytab, qtab, x1tab, y2rows, y2ttab, sem)
        sem.done()
        with nc.If(overflow > 0):
            attend_all(nc, keep, x, adj, rtok, ytab, qtab, x1tab, y2rows, y2ttab, sem)
        sem.done()
        feed_forward(nc, keep, y2ttab, x1tab, y2rows, wtab, b1l, b2l, b1h, b2h, out, sem)


def split_weights(nc, keep, wk, wq, bq, bk, wv_t, bv, gl, w1l, w2l, gh, w1h, w2h, wtab, sem, x, ytab, qtab, adj_t):
    with ExitStack() as ctx:
        def sb(name, shape, dt):
            return ctx.enter_context(nc.sbuf_tensor(name, shape, dt))

        def pb(name, shape, dt):
            return ctx.enter_context(nc.psum_tensor(name, shape, dt))

        m_hl = sb("m_hl", [P, KC, 2, D], F16)
        u_hl = sb("u_hl", [P, KC, 2], F16)
        w64 = sb("w64", [P, KC], F32)
        c0 = sb("c0", [P, 1], F32)
        zeros = keep["zeros"]

        loaded_v, loaded_b = sem("loaded_v"), sem("loaded_b")
        loaded_qk, raw_in = sem("loaded_qk"), [sem("raw_in0"), sem("raw_in1")]
        consts, scaled_done, high_done, low_done = sem("consts"), sem("scaled_done"), sem("high_done"), sem("low_done")
        split_out = [sem("split_out0"), sem("split_out1")]
        bq_ready, m_ready, m_copied, vec_ready, dve0 = sem("bq_ready"), sem("m_ready"), sem("m_copied"), sem("vec_ready"), sem("dve0")
        m_done = sem("m_done")
        pool0, wv_scaled, wv_high = sem("pool0"), sem("wv_scaled"), sem("wv_high")

        units = [(w1h[kc * P:(kc + 1) * P, :], 2048, (1, kc)) for kc in range(KC)]
        w2h_u = w2h.rearrange("(u c p) n -> u p c n", c=4, p=P)
        units += [(w2h_u[u], 2048, (2, 0)) for u in range(4)]
        units += [(w1l.rearrange("(c p) n -> p c n", p=P), 1024, None)]
        units += [(w2l.rearrange("(c p) n -> p c n", p=P), 1024, (2, 0))]

        with ExitStack() as pctx:
            def tmp(name, shape, dt):
                return pctx.enter_context(nc.sbuf_tensor(name, shape, dt))

            wq_sb, wk_sb = tmp("wq_sb", [P, KC, D], F32), tmp("wk_sb", [P, KC, D], F32)
            wv_sb = tmp("wv_sb", [P, KC, D], F32)
            bq_sb, bk_sb = tmp("bq_sb", [P, KC], F32), tmp("bk_sb", [P, KC], F32)
            bq_wide = tmp("bq_wide", [P, KC, P], F32)
            gl_sb, gh_sb = tmp("gl_sb", [P, KC], F32), tmp("gh_sb", [P, KC], F32)
            gains = tmp("gains", [P, 3, KC], F32)
            raw = tmp("raw", [P, 2, 2048], F32)
            scaled = tmp("scaled", [P, 2, 2048], F32)
            halves = tmp("halves", [P, 2, 2, 2048], F16)
            m32 = tmp("m32", [P, 2, D], F32)
            u32 = tmp("u32", [P, KC], F32)
            ps_m = [pctx.enter_context(nc.psum_tensor(f"ps_m{i}", [P, D], F32)) for i in range(2)]
            ps_v = pctx.enter_context(nc.psum_tensor("ps_v", [P, 16], F32))
            with nc.Block() as block:
                @block.sync
                def _(sp):
                    sp.dma_start(wq_sb[:, :, :], wq.rearrange("(c p) k -> p c k", p=P)).then_inc(loaded_qk, 16)
                    sp.dma_start(wk_sb[:, :, :], wk.rearrange("(c p) k -> p c k", p=P)).then_inc(loaded_qk, 16)
                    for t, s in ((bq_sb, bq), (bk_sb, bk), (gl_sb, gl), (gh_sb, gh)):
                        sp.dma_start(t[:, :], s.rearrange("(c p) -> p c", p=P),
                                     allow_slow_non_contiguous=True).then_inc(loaded_b, 16)
                    sp.dma_start(wv_sb[:, :, :], wv_t.rearrange("(c p) k -> p c k", p=P)).then_inc(loaded_v, 16)
                    sp.dma_start(keep["bvb"][:, :], bv.partition_broadcast(P)).then_inc(loaded_v, 16)
                    for n, (src, width, _) in enumerate(units):
                        if n >= 2:
                            sp.wait_ge(scaled_done, n - 1)
                        dst = raw[:, n % 2, 0:width]
                        if len(src.shape) == 3:
                            dst = dst.rearrange("p (c n) -> p c n", c=src.shape[1])
                        sp.dma_start(dst, src).then_inc(raw_in[n % 2], 16)
                    for i in range(2):
                        sp.wait_ge(split_out[i], 16 * (len(units) // 2))
                    sp.wait_ge(loaded_v, 32)

                @block.gpsimd
                def _(pool):
                    ch = Chain(pool, pool0)
                    ch.step(pool.memset(keep["ident"][:, :], 0.0))
                    pool.affine_select(out=keep["ident"][:, :], in_=keep["ident"][:, :], compare_op=ALU.not_equal,
                                       fill=1.0, base=0, pattern=[[-1, P]], channel_multiplier=1).then_inc(consts, 1)
                    pool.wait_ge(consts, 1)
                    pool.tensor_copy(keep["ident16"][:, :], keep["ident"][:, :])
                    pool.memset(keep["ones16"][:, :], 1.0).then_inc(consts, 1)
                    pool.memset(zeros[:, :], 0.0).then_inc(consts, 1)
                    for n, (_, width, _) in enumerate(units):
                        pool.wait_ge(high_done, n + 1)
                        pool.tensor_tensor(halves[:, n % 2, 1, 0:width], scaled[:, n % 2, 0:width],
                                           halves[:, n % 2, 0, 0:width], ALU.subtract).then_inc(low_done, 1)
                        pool.wait_ge(low_done, n + 1)
                        pool.dma_start(wtab[n].rearrange("p (h n) -> p h n", h=2)[:, :, 0:width],
                                       halves[:, n % 2, :, 0:width]).then_inc(split_out[n % 2], 16)

                @block.vector
                def _(dve):
                    ch = Chain(dve, dve0)
                    dve.wait_ge(loaded_b, 64)
                    dve.tensor_copy(bq_wide[:, :, :], bq_sb[:, :].unsqueeze(2).broadcast_to([P, KC, P])).then_inc(bq_ready, 1)
                    dve.tensor_scalar(gains[:, 0, :], gl_sb[:, :], YS, None, ALU.mult)
                    dve.tensor_scalar(gains[:, 1, :], gh_sb[:, :], YS, None, ALU.mult)
                    ch.step(dve.memset(gains[:, 2, :], YS))
                    dve.wait_ge(loaded_v, 32)
                    dve.tensor_scalar(wv_sb[:, :, :], wv_sb[:, :, :], YS, None, ALU.mult).then_inc(wv_scaled, 1)
                    dve.wait_ge(wv_high, 1)
                    dve.tensor_tensor(keep["wv"][:, :, 1, :], wv_sb[:, :, :], keep["wv"][:, :, 0, :], ALU.subtract)
                    for n, (_, width, g) in enumerate(units):
                        if n == 4:
                            for kc in range(KC):
                                dve.wait_ge(m_copied, 2 * kc + 2)
                                dve.tensor_tensor(m_hl[:, kc, 1, :], m32[:, kc % 2, :], m_hl[:, kc, 0, :],
                                                  ALU.subtract).then_inc(m_ready, 1)
                            dve.wait_ge(vec_ready, 1)
                            dve.tensor_scalar(w64[:, :], ps_v[:, 4:8], YS, None, ALU.mult)
                            dve.tensor_scalar(c0[:, :], ps_v[:, 8:9], ZS, None, ALU.mult)
                            ch.step(dve.tensor_scalar(u32[:, :], ps_v[:, 0:4], MS, None, ALU.mult))
                            ch.step(dve.tensor_copy(u_hl[:, :, 0], u32[:, :]))
                            ch.step(dve.tensor_tensor(u_hl[:, :, 1], u32[:, :], u_hl[:, :, 0], ALU.subtract))
                        dve.wait_ge(raw_in[n % 2], 16 * (n // 2 + 1))
                        if n >= 2:
                            dve.wait_ge(low_done, n - 1)
                        if g is None:
                            for kc in range(KC):
                                last = dve.tensor_scalar(scaled[:, n % 2, kc * HL:(kc + 1) * HL], raw[:, n % 2, kc * HL:(kc + 1) * HL],
                                                         gains[:, 0, kc:kc + 1], None, ALU.mult)
                            last.then_inc(scaled_done, 1)
                        else:
                            dve.tensor_scalar(scaled[:, n % 2, 0:width], raw[:, n % 2, 0:width],
                                              gains[:, g[0], g[1]:g[1] + 1], None, ALU.mult).then_inc(scaled_done, 1)

                @block.scalar
                def _(act):
                    def high(n):
                        width = units[n][1]
                        act.wait_ge(scaled_done, n + 1)
                        if n >= 2:
                            act.wait_ge(split_out[n % 2], 16 * (n // 2))
                        act.activation(halves[:, n % 2, 0, 0:width], scaled[:, n % 2, 0:width], ACT.Copy).then_inc(high_done, 1)

                    act.wait_ge(wv_scaled, 1)
                    act.activation(keep["wv"][:, :, 0, :], wv_sb[:, :, :], ACT.Copy).then_inc(wv_high, 1)
                    for n in range(4):
                        high(n)
                    for kc in range(KC):
                        act.wait_ge(m_done, kc + 1)
                        if kc >= 2:
                            act.wait_ge(m_ready, kc - 1)
                        act.activation(m32[:, kc % 2, :], ps_m[kc % 2][:, :], ACT.Copy, scale=MS).then_inc(m_copied, 1)
                        act.wait_ge(m_copied, 2 * kc + 1)
                        act.activation(m_hl[:, kc, 0, :], m32[:, kc % 2, :], ACT.Copy).then_inc(m_copied, 1)
                    for n in range(4, len(units)):
                        high(n)

                @block.tensor
                def _(pe):
                    pe.wait_ge(loaded_qk, 32)
                    for kc in range(KC):
                        if kc >= 2:
                            pe.wait_ge(m_copied, 2 * (kc - 1))
                        for d in range(KC):
                            last = pe.matmul(ps_m[kc % 2][:, :], wq_sb[:, d, kc * P:(kc + 1) * P], wk_sb[:, d, :],
                                             start=(d == 0), stop=(d == KC - 1))
                        last.then_inc(m_done, 1)
                    pe.wait_ge(loaded_b, 64)
                    pe.wait_ge(bq_ready, 1)
                    for kc in range(KC):
                        for d in range(KC):
                            pe.matmul(ps_v[:, kc:kc + 1], wq_sb[:, d, kc * P:(kc + 1) * P], bk_sb[:, d:d + 1],
                                      start=(d == 0), stop=(d == KC - 1))
                        for d in range(KC):
                            pe.matmul(ps_v[:, 4 + kc:5 + kc], wk_sb[:, d, kc * P:(kc + 1) * P], bq_sb[:, d:d + 1],
                                      start=(d == 0), stop=(d == KC - 1))
                    for d in range(KC):
                        last = pe.matmul(ps_v[:, 8:9], bq_wide[:, d, :], bk_sb[:, d:d + 1], start=(d == 0), stop=(d == KC - 1))
                    last.then_inc(vec_ready, 1)
        project_queries(nc, keep, m_hl, u_hl, w64, c0, zeros, x, ytab, qtab, adj_t, sem)


def project_queries(nc, keep, m_hl, u_hl, w64, c0, zeros, x, ytab, qtab, adj_t, sem):
    x_groups = x.rearrange("(g s p) d -> g p s d", s=GROUP, p=P)
    ytab_g = ytab.rearrange("(g s p) d -> g p s d", s=GROUP, p=P)
    qtab_g = qtab.rearrange("(g s) p n -> g p s n", s=GROUP)
    with ExitStack() as ctx:
        def sb(name, shape, dt):
            return ctx.enter_context(nc.sbuf_tensor(name, shape, dt))

        xg = sb("xg", [P, 2, GROUP, D], F32)
        stats = sb("stats", [P, 2, GROUP, 6], F32)
        mv = sb("mv", [P, 2, GROUP, 2], F32)
        half_pow = sb("half_pow", [P, 1], F32)
        var_eps = sb("var_eps", [P, 2, GROUP], F32)
        rstd = sb("rstd", [P, 2, GROUP], F32)
        y32 = sb("y32", [P, 2, GROUP, D], F32)
        y_rows = sb("y_rows", [P, 2, GROUP, 2, D], F16)
        y_t = sb("y_t", [P, 2, KC, 2, GROUP * P], F16)
        q32 = sb("q32", [P, 2, D], F32)
        q_hl = sb("q_hl", [P, 2, GROUP, KC, 2, P], F16)
        ps_t = [ctx.enter_context(nc.psum_tensor(f"ps_t{i}", [P, KC, P], F32)) for i in range(2)]
        ps_q = [ctx.enter_context(nc.psum_tensor(f"ps_q{i}", [P, GROUP * P], F32)) for i in range(2)]
        ps_c = [ctx.enter_context(nc.psum_tensor(f"ps_c{i}", [P, GROUP, 2], F32)) for i in range(2)]
        ps_y = ctx.enter_context(nc.psum_tensor("ps_y", [P, D], F32))

        adj_sb = sb("adj_sb", [P, 2, N], F32)
        c_part = sb("c_part", [P, 2, GROUP], F32)
        adj_t_tiles = adj_t.rearrange("(c p) i -> c p i", p=P)

        passed, passed_dve = sem("passed"), sem("passed_dve")
        xg_free, adj_free, rows_free, y32_free = sem("xg_free"), sem("adj_free"), sem("rows_free"), sem("y32_free")
        yt_free, rows_high, q_high = sem("yt_free"), sem("rows_high"), sem("q_high")
        adj_in = [sem("adj_in0"), sem("adj_in1")]
        x_in = [sem("x_in0"), sem("x_in1")]
        pow_ready = sem("pow_ready")
        dve1, pool1 = sem("dve1"), sem("pool1")
        var_ready, rstd_ready, y_ready, rows_ready = sem("var_ready"), sem("rstd_ready"), sem("y_ready"), sem("rows_ready")
        rows_out, q_out = [sem("rows_out0"), sem("rows_out1")], [sem("q_out0"), sem("q_out1")]
        t_ready, t_high, t_low = sem("t_ready"), sem("t_high"), sem("t_low")
        q_ready, q_biased, q_split = sem("q_ready"), sem("q_biased"), sem("q_split")
        c_ready, c_read, total_ready = sem("c_ready"), sem("c_read"), sem("total_ready")
        summed = sem("summed")
        HALVES = NG // 2

        with nc.Block() as block:
            @block.sync
            def _(sp):
                sp.sem_inc(xg_free, 2)
                sp.sem_inc(adj_free, 2)
                with sp.Fori(0, HALVES) as i:
                    for h in range(2):
                        g = i * 2 + h
                        sp.wait_ge(xg_free, g + 1)
                        sp.dma_start(xg[:, h], x_groups[bass.ds(g, 1)].rearrange("a p s d -> p (a s) d")).then_inc(x_in[h], 16)
                        for s in range(GROUP):
                            sp.wait_ge(adj_free, g * GROUP + (s + 1))
                            sp.dma_start(adj_sb[:, s % 2], adj_t_tiles[bass.ds(g * GROUP + s, 1)].rearrange("a p i -> p (a i)")
                                         ).then_inc(adj_in[s % 2], 16)
                for h in range(2):
                    sp.wait_ge(rows_out[h], 16 * HALVES)
                    sp.wait_ge(q_out[h], 16 * HALVES)

            @block.gpsimd
            def _(pool):
                pool.memset(half_pow[:, :], -0.5).then_inc(pow_ready, 1)
                pool.wait_ge(pow_ready, 1)
                pool.sem_inc(rows_free, 2)
                with pool.Fori(0, HALVES) as i:
                    for h in range(2):
                        g = i * 2 + h
                        pool.wait_ge(var_ready, g + 1)
                        pool.tensor_tensor(rstd[:, h], var_eps[:, h], half_pow[:, :].broadcast_to([P, GROUP]),
                                           ALU.pow).then_inc(rstd_ready, 1)
                        pool.wait_ge(rows_free, g + 1)
                        pool.wait_ge(rows_out[h], i * 16)
                        pool.wait_ge(y_ready, g * GROUP + GROUP)
                        pool.sem_inc(passed, 1)
                        pool.tensor_copy(y_rows[:, h, :, 0, :], y32[:, h]).then_inc(rows_high, 1)
                        pool.wait_ge(rows_high, g + 1)
                        pool.tensor_tensor(y_rows[:, h, :, 1, :], y32[:, h], y_rows[:, h, :, 0, :],
                                           ALU.subtract).then_inc(rows_ready, 1)
                        pool.wait_ge(rows_ready, g + 1)
                        pool.sem_inc(y32_free, 1)
                        pool.sem_inc(passed, 1)
                        pool.dma_start(ytab_g[bass.ds(g, 1)].rearrange("a p s d -> p (a s) d"),
                                       y_rows[:, h].rearrange("p s e d -> p s (e d)")).then_inc(rows_out[h], 16)
                        for k in range(KC):
                            pool.wait_ge(q_high, g * KC + (k + 1))
                            pool.tensor_tensor(q_hl[:, h, :, k, 1, :], q32[:, k % 2].rearrange("p (s t) -> p s t", s=GROUP),
                                               q_hl[:, h, :, k, 0, :], ALU.subtract).then_inc(q_split, 1)
                        pool.wait_ge(q_split, g * KC + KC)
                        pool.sem_inc(passed, 1)
                        pool.dma_start(qtab_g[bass.ds(g, 1)].rearrange("a p s n -> p (a s) n"),
                                       q_hl[:, h].rearrange("p s k e t -> p s (k e t)")).then_inc(q_out[h], 16)

            @block.vector
            def _(dve):
                ch = Chain(dve, dve1)
                dve.sem_inc(y32_free, 2)
                with dve.Fori(0, HALVES) as i:
                    for h in range(2):
                        g = i * 2 + h
                        ch.base = i * (2 * 3)
                        dve.wait_ge(x_in[h], i * 16 + 16)
                        for s in range(GROUP):
                            last = dve.bn_stats(stats[:, h, s], xg[:, h, s])
                        ch.step(last)
                        dve.sem_inc(passed_dve, 1)
                        for s in range(GROUP):
                            last = dve.bn_aggr(mv[:, h, s], stats[:, h, s])
                        ch.step(last)
                        dve.tensor_scalar(var_eps[:, h], mv[:, h, :, 1], EPS_LN, 1.0 / (YS * YS), ALU.add,
                                          ALU.mult).then_inc(var_ready, 1)
                        dve.wait_ge(rstd_ready, g + 1)
                        dve.wait_ge(y32_free, g + 1)
                        for s in range(GROUP):
                            last = dve.tensor_scalar(y32[:, h, s], xg[:, h, s], mv[:, h, s, 0:1], rstd[:, h, s:s + 1],
                                                     ALU.subtract, ALU.mult)
                            last.then_inc(y_ready, 1)
                        dve.wait_ge(y_ready, g * GROUP + GROUP)
                        dve.sem_inc(xg_free, 1)
                        for s in range(GROUP):
                            dve.wait_ge(t_high, g * GROUP + (s + 1))
                            dve.tensor_tensor(y_t[:, h, :, 1, s * P:(s + 1) * P], ps_t[s % 2][:, :, :],
                                              y_t[:, h, :, 0, s * P:(s + 1) * P], ALU.subtract).then_inc(t_low, 1)
                        dve.wait_ge(c_ready, g + 1)
                        ch.step(dve.tensor_scalar(c_part[:, h], ps_c[h][:, :, 0], ZS / (YS * MS), c0[:, 0:1], ALU.mult, ALU.add))
                        dve.scalar_tensor_tensor(keep["cs"][:, bass.ds(g * GROUP, GROUP)], ps_c[h][:, :, 1], ZS / (YS * MS),
                                                 c_part[:, h], ALU.mult, ALU.add).then_inc(c_read, 1)
                        for s in range(GROUP):
                            dve.wait_ge(adj_in[s % 2], g * 32 + 16 * (s // 2 + 1))
                            dve.tensor_reduce(keep["nz"][:, bass.ds(g * GROUP + s, 1), :].rearrange("p a t -> p (a t)"),
                                              adj_sb[:, s % 2].rearrange("p (t i) -> p t i", i=P), AX_X, ALU.max,
                                              apply_absolute_value=True).then_inc(adj_free, 1)
                dve.wait_ge(summed, 1)
                dve.tensor_copy(keep["ytot"][:, :], ps_y[:, :])

            @block.scalar
            def _(act):
                with act.Fori(0, HALVES) as i:
                    for h in range(2):
                        g = i * 2 + h
                        for s in range(GROUP):
                            act.wait_ge(t_ready, g * GROUP + (s + 1))
                            act.activation(y_t[:, h, :, 0, s * P:(s + 1) * P], ps_t[s % 2][:, :, :], ACT.Copy).then_inc(t_high, 1)
                        act.wait_ge(q_out[h], i * 16)
                        for k in range(KC):
                            act.wait_ge(q_ready, g * KC + (k + 1))
                            act.wait_ge(q_split, g * KC + max(k - 1, 0))
                            act.activation(q32[:, k % 2], ps_q[k % 2][:, :], ACT.Identity, bias=w64[:, k:k + 1],
                                           scale=1.0 / MS).then_inc(q_biased, 1)
                            act.wait_ge(q_biased, g * KC + (k + 1))
                            act.activation(q_hl[:, h, :, k, 0, :], q32[:, k % 2].rearrange("p (s t) -> p s t", s=GROUP),
                                           ACT.Copy).then_inc(q_high, 1)

            @block.tensor
            def _(pe):
                pe.matmul(ps_y[:, :], keep["ones16"][:, :], zeros[:, :], start=True, stop=False, skip_group_check=True)
                with pe.Fori(0, HALVES) as i:
                    for h in range(2):
                        g = i * 2 + h
                        for s in range(GROUP):
                            pe.wait_ge(y_ready, g * GROUP + (s + 1))
                            pe.wait_ge(t_low, g * GROUP + max(s - 1, 0))
                            for k in range(KC):
                                last = pe.transpose(ps_t[s % 2][:, k, :], y32[:, h, s, k * P:(k + 1) * P], keep["ident"][:, :])
                            last.then_inc(t_ready, 1)
                        pe.wait_ge(t_low, g * GROUP + GROUP)
                        pe.wait_ge(c_read, g)
                        for s in range(GROUP):
                            for k in range(KC):
                                pe.matmul(ps_c[h][:, s, :], y_t[:, h, k, 0, s * P:(s + 1) * P], u_hl[:, k, :],
                                          start=(k == 0), stop=False, skip_group_check=True)
                                last = pe.matmul(ps_c[h][:, s, 0:1], y_t[:, h, k, 1, s * P:(s + 1) * P], u_hl[:, k, 0:1],
                                                 start=False, stop=(k == KC - 1), skip_group_check=True)
                        last.then_inc(c_ready, 1)
                        pe.wait_ge(rows_ready, g + 1)
                        for s in range(GROUP):
                            for e in range(2):
                                last = pe.matmul(ps_y[:, :], keep["ones16"][:, :], y_rows[:, h, s, e, :], start=False,
                                                 stop=False, skip_group_check=True)
                        last.then_inc(rows_free, 1)
                        for k in range(KC):
                            pe.wait_ge(q_biased, g * KC + max(k - 1, 0))
                            for c in range(KC):
                                for a, b in ((0, 0), (0, 1), (1, 0)):
                                    last = pe.matmul(ps_q[k % 2][:, :], m_hl[:, c, a, k * P:(k + 1) * P], y_t[:, h, c, b, :],
                                                     start=(c == 0 and a == 0 and b == 0), stop=(c == KC - 1 and a == 1))
                            last.then_inc(q_ready, 1)
                pe.matmul(ps_y[0:P, 0:1], keep["ones16"][:, :], zeros[:, 0:1], start=False, stop=True, skip_group_check=True).then_inc(summed, 1)


SEGS = 4
SEG = N // SEGS
SLOTS = 160
CH = SEGS * SLOTS // P
LISTED = CH * P
RING = 4


def list_neighbours(nc, keep, sem):
    with ExitStack() as ctx:
        def sb(name, shape, dt):
            return ctx.enter_context(nc.sbuf_tensor(name, shape, dt))

        ramp = sb("ramp", [P, SEG // P], I32)
        ramp_f = sb("ramp_f", [P, SEG // P], F32)
        part = sb("part", [P, 1], I32)
        part_f = sb("part_f", [P, 1], F32)
        has = sb("has", [P, SEG // P, SEGS, NT], F32)
        local = sb("local", [P, SEG // P], F32)
        keys = sb("keys", [P, 2, SEG], F32)
        listed = sb("listed", [P, SLOTS], F32)
        turned = sb("turned", [P, SLOTS], F32)
        left = sb("left", [P, 8], F32)
        seg_base = sb("seg_base", [P, 1], F32)
        tile_no = sb("tile_no", [P, NT], I32)
        tile_f = sb("tile_f", [P, NT], F32)
        seg_i = sb("seg_i", [P, 1], I32)
        source = sb("source", [P, CH, NT], F32)
        row = sb("row", [P, CH, NT], F32)
        over = sb("over", [P, 1], F32)
        total = sb("total", [P, 1], F32)
        ps = [ctx.enter_context(nc.psum_tensor(f"ps_keys{i}", [P, 4, P], F32)) for i in range(2)]
        ps_over = ctx.enter_context(nc.psum_tensor("ps_over", [P, 1], F32))
        ones = sb("ones_f", [P, P], F32)

        iotas, dve2, key_ready, key_turned, over_ready, over_sum = (sem("iotas"), sem("dve2"), sem("key_ready"),
                                                                    sem("key_turned"), sem("over_ready"), sem("over_sum"))
        with nc.Block() as block:
            @block.gpsimd
            def _(pool):
                pool.iota(ramp[:, :], pattern=[[P, SEG // P]], base=0, channel_multiplier=0).then_inc(iotas, 1)
                pool.iota(part[:, :], pattern=[[0, 1]], base=0, channel_multiplier=1).then_inc(iotas, 1)
                pool.iota(tile_no[:, :], pattern=[[1, NT]], base=0, channel_multiplier=0).then_inc(iotas, 1)
                pool.memset(ones[:, :], 1.0).then_inc(iotas, 1)

            @block.vector
            def _(dve):
                ch = Chain(dve, dve2)
                dve.wait_ge(iotas, 4)
                dve.tensor_copy(part_f[:, :], part[:, :])
                dve.tensor_copy(tile_f[:, :], tile_no[:, :])
                dve.tensor_scalar(seg_i[:, :], part[:, :], 5, None, ALU.logical_shift_right)
                ch.step(dve.tensor_copy(ramp_f[:, :], ramp[:, :]))
                ch.step(dve.tensor_scalar(local[:, :], ramp_f[:, :], part_f[:, 0:1], -1.0, ALU.add, ALU.mult))
                ch.step(dve.tensor_copy(seg_base[:, :], seg_i[:, :]))
                ch.step(dve.tensor_scalar(seg_base[:, :], seg_base[:, :], 1.0, float(SEG), ALU.add, ALU.mult))
                ch.step(dve.tensor_scalar(local[:, :], local[:, :], float(SEG), None, ALU.add))
                for r in range(SEG // P):
                    last = dve.tensor_scalar(has[:, r], keep["nz"][:, r::SEG // P, :], 0.0, local[:, r:r + 1], ALU.not_equal, ALU.mult)
                last.then_inc(key_ready, 1)
                for b in range(2):
                    dve.wait_ge(key_turned, b + 1)
                    last = dve.tensor_copy(keys[:, 0, b * 512:(b + 1) * 512], ps[b][:, :, :].rearrange("p a j -> p (a j)"))
                ch.step(last)
                for n in range(SLOTS // 8):
                    ch.step(dve.max(listed[:, 8 * n:8 * n + 8], keys[:, n % 2, :]))
                    ch.step(dve.match_replace(keys[:, (n + 1) % 2, :], listed[:, 8 * n:8 * n + 8], keys[:, n % 2, :], 0.0))
                ch.step(dve.max(left[:, :], keys[:, (SLOTS // 8) % 2, :]))
                dve.tensor_scalar(over[:, :], left[:, 0:1], 0.0, None, ALU.is_gt).then_inc(over_ready, 1)
                ch.step(dve.transpose(turned[:, :], listed[:, :]))
                tv = turned[:, :].rearrange("p (c t) -> p c t", c=CH)
                dve.tensor_scalar(keep["valid"][:, :, :].rearrange("p t c -> p c t"), tv, 0.0, None, ALU.is_gt)
                ch.step(dve.tensor_scalar(source[:, :, :], tv, seg_base[:, 0:1], -1.0, ALU.subtract, ALU.mult))
                ch.step(dve.tensor_tensor(source[:, :, :], source[:, :, :],
                                          keep["valid"][:, :, :].rearrange("p t c -> p c t"), ALU.mult))
                dve.tensor_copy(keep["index"][:, :, 0, :].rearrange("p t c -> p c t"), source[:, :, :])
                ch.step(dve.tensor_scalar(row[:, :, :], source[:, :, :], float(NT), None, ALU.mult))
                ch.step(dve.tensor_tensor(row[:, :, :], row[:, :, :], tile_f[:, :].unsqueeze(1).broadcast_to([P, CH, NT]), ALU.add))
                dve.tensor_copy(keep["index"][:, :, 1, :].rearrange("p t c -> p c t"), row[:, :, :])
                dve.wait_ge(over_sum, 1)
                ch.step(dve.tensor_copy(keep["overflow"][:, :], ps_over[:, :]))

            @block.tensor
            def _(pe):
                pe.wait_ge(key_ready, 1)
                for r in range(SEG // P):
                    last = pe.transpose(ps[r // 4][:, r % 4, :], has[:, r].rearrange("p s t -> p (s t)"), keep["ident"][:, :])
                    if r % 4 == 3:
                        last.then_inc(key_turned, 1)
                pe.wait_ge(over_ready, 1)
                pe.matmul(ps_over[:, :], ones[:, :], over[:, :], start=True, stop=True).then_inc(over_sum, 1)


class Tile:

    def __init__(self, turn, k):
        self.t = turn * RING + k
        self.ring, self.par = k % RING, k % 2
        self.turn, self.pair = turn + k // RING, turn * (RING // 2) + k // 2


def wait(eng, sem, value):
    if not isinstance(value, int) or value > 0:
        eng.wait_ge(sem, value)


def pipeline(eng, stages):
    def step(turn, n):
        for stage, lag in stages:
            k = n + lag
            if turn is None and not 0 <= k < NT:
                continue
            stage(Tile(0 if turn is None else turn, k))

    first, turns = 3, (NT - 8) // RING
    for n in range(-2, first):
        step(None, n)
    with eng.Fori(0, turns) as turn:
        for u in range(RING):
            step(turn, first + u)
    for n in range(first + turns * RING, NT + 3):
        step(None, n)


class StageChain:

    def __init__(self, eng, sem, count):
        self.eng, self.sem, self.count = eng, sem, count

    def begin(self, tile):
        self.base, self.n = tile.t * self.count, 0

    def step(self, ins):
        self.n += 1
        ins.then_inc(self.sem, 1)
        self.eng.wait_ge(self.sem, self.base + self.n)

    def end(self):
        assert self.n == self.count, (self.n, self.count)


PASSES = ((0, 0), (0, 1), (1, 0))
A0 = 3
BANKS = ((0, A0), (A0, CH))


def attend_listed(nc, keep, x, adj_t, rtok, ytab, qtab, x1tab, y2rows, y2ttab, sem):
    adj_rows = adj_t.rearrange("j (t i) -> (j t) i", i=P)
    x_tiles = x.rearrange("(t p) d -> t p d", p=P)
    x1_tiles = x1tab.rearrange("(t p) d -> t p d", p=P)
    y2_tiles = y2rows.rearrange("(t p) d -> t p d", p=P)
    with ExitStack() as ctx:
        def sb(name, shape, dt):
            return ctx.enter_context(nc.sbuf_tensor(name, shape, dt))

        def pb(name, shape, dt):
            return ctx.enter_context(nc.psum_tensor(name, shape, dt))

        index_now = sb("index_now", [P, RING, 2, CH], I32)
        y_src = sb("y_src", [P, RING, CH, 2 * D], F16)
        a_src = sb("a_src", [P, RING, CH, P], F32)
        y_src_t = sb("y_src_t", [P, 2, 2 * KC, LISTED], F16)
        a_tok = sb("a_tok", [P, 2, LISTED], F32)
        q_t = sb("q_t", [P, 2, KC, 2, P], F16)
        prob = sb("prob", [P, 2, LISTED], F32)
        fill = sb("fill", [P, LISTED], F32)
        top, bias = sb("top", [P, 2, 1], F32), sb("bias", [P, 2, 1], F32)
        sum_e, one_e = sb("sum_e", [P, 2, 1], F32), sb("one_e", [P, 2, 1], F32)
        den, rden, rest = sb("den", [P, 2, 1], F32), sb("rden", [P, 2, 1], F32), sb("rest", [P, 2, 1], F32)
        masked = sb("masked", [P, 1], F32)
        minus_half = sb("minus_half", [P, 1], F32)
        prob_t = sb("prob_t", [P, 2, CH, 2, P], F16)
        mix = sb("mix", [P, 2, D], F32)
        mix_t = sb("mix_t", [P, 2, KC, 2, P], F16)
        x_tok = sb("x_tok", [P, 2, D], F32)
        val = sb("val", [P, D], F32)
        x1 = sb("x1", [P, 2, D], F32)
        stats2, mv2 = sb("stats2", [P, 2, 6], F32), sb("mv2", [P, 2, 2], F32)
        var2, rstd2 = sb("var2", [P, 2, 2], F32), sb("rstd2", [P, 2, 2], F32)
        alpha = sb("alpha", [P, 2, 1], F32)
        rt_row = sb("rt_row", [P, D], F32)
        rt_sum = sb("rt_sum", [P, 1], F32)
        dot_junk = sb("dot_junk", [P, D], F32)
        dot, off = sb("dot", [P, 2, 1], F32), sb("off", [P, 2, 1], F32)
        y2 = sb("y2", [P, 2, D], F32)
        y2_t = sb("y2_t", [P, 2, KC, 2, P], F16)

        turn_bank = [pb(f"turn_bank{b}", [P, 2 * KC, P], F16) for b in range(2)]
        z_bank = [pb(f"z_bank{b}", [P, D], F32) for b in range(2)]
        pa_bank = [pb(f"pa_bank{b}", [P, KC, P], F32) for b in range(2)]
        u_bank = pb("u_bank", [P, D], F32)
        o_bank = pb("o_bank", [P, D], F32)

        def sems(*names):
            return [sem(n) for n in names]

        y_in, a_in = [sem(f"y_in{r}") for r in range(RING)], [sem(f"a_in{r}") for r in range(RING)]
        q_in, xt_in = [sem(f"q_in{r}") for r in range(2)], [sem(f"xt_in{r}") for r in range(2)]
        x1_out, y2_out = [sem(f"x1_out{r}") for r in range(2)], [sem(f"y2_out{r}") for r in range(2)]
        y2t_out = [sem(f"y2t_out{r}") for r in range(2)]
        index_ready, a_masked, pow_done = sems("index_ready", "a_masked", "pow_done")
        passed, passed_dve = sems("passed2", "passed_dve2")
        setup, const_in, rt_ready = sems("setup", "const_in", "rt_ready")
        turn_full, turn_read = [sem(f"turn_full{b}") for b in range(2)], [sem(f"turn_read{b}") for b in range(2)]
        a_full, a_read, z_full, w_done = sems("a_full", "a_read", "z_full", "w_done")
        pt_full, pt_high, pt_low, pv_done = sems("pt_full", "pt_high", "pt_low", "pv_done")
        soft, top_ready, e_ready, prob_chain, prob_ready = sems("soft", "top_ready", "e_ready", "prob_chain", "prob_ready")
        mix_ready, mt_full, mt_high, mt_low, o_full = sems("mix_ready", "mt_full", "mt_high", "mt_low", "o_full")
        o_read, x1_ready, x1_chain, var_done, y2_ready = sems("o_read", "x1_ready", "x1_chain", "var_done", "y2_ready")
        route, s_ready, y2_full, y2_high, y2_low = sems("route", "s_ready", "y2_full", "y2_high", "y2_low")

        with nc.Block() as block:
            @block.sync
            def _(sp):
                sp.dma_start(rt_row[:, :], rtok.partition_broadcast(P)).then_inc(const_in, 16)

                def load_q(c):
                    wait(sp, z_full, 2 * (c.t - 1))
                    sp.dma_start(q_t[:, c.par].rearrange("p k e t -> p (k e t)"),
                                 qtab[bass.ds(c.t, 1)].rearrange("a p n -> p (a n)")).then_inc(q_in[c.par], 16)

                def load_x(c):
                    wait(sp, x1_ready, c.t - 1)
                    sp.dma_start(x_tok[:, c.par], x_tiles[bass.ds(c.t, 1)].rearrange("a p n -> p (a n)")
                                 ).then_inc(xt_in[c.par], 16)

                def store_y2t(c):
                    sp.wait_ge(y2_low, c.t + 1)
                    sp.dma_start(y2ttab[bass.ds(c.t, 1)].rearrange("a p n -> p (a n)"),
                                 y2_t[:, c.par].rearrange("p k e t -> p (k e t)")).then_inc(y2t_out[c.par], 16)

                def store_rows(c):
                    sp.wait_ge(x1_ready, c.t + 1)
                    sp.dma_start(x1_tiles[bass.ds(c.t, 1)].rearrange("a p n -> p (a n)"), x1[:, c.par]).then_inc(x1_out[c.par], 16)
                    sp.wait_ge(y2_ready, c.t + 1)
                    sp.dma_start(y2_tiles[bass.ds(c.t, 1)].rearrange("a p n -> p (a n)"), y2[:, c.par]).then_inc(y2_out[c.par], 16)

                pipeline(sp, [(load_q, 1), (load_x, 0), (store_y2t, -3), (store_rows, -2)])
                for b in range(2):
                    for s in (x1_out, y2_out, y2t_out):
                        sp.wait_ge(s[b], 16 * NT // 2)

            @block.gpsimd
            def _(pool):
                pool.memset(masked[:, :], MASKED).then_inc(setup, 1)
                pool.memset(minus_half[:, :], -0.5).then_inc(setup, 1)
                pool.wait_ge(setup, 2)

                def gather(c):
                    wait(pool, pv_done, c.t - 3)
                    wait(pool, a_full, 2 * (c.t - 3))
                    pool.sem_inc(passed, 1)
                    pool.tensor_copy(index_now[:, c.ring], keep["index"][:, bass.ds(c.t, 1)].rearrange("p a b c -> p (a b) c")
                                     ).then_inc(index_ready, 1)
                    pool.wait_ge(index_ready, c.t + 1)
                    pool.sem_inc(passed, 1)
                    for n in range(CH):
                        pool.indirect_dma_start(out=y_src[:, c.ring, n, :], out_offset=None, in_=ytab,
                                                in_offset=bass.IndirectOffsetOnAxis(ap=index_now[:, c.ring, 0, n:n + 1], axis=0)
                                                ).then_inc(y_in[c.ring], 16)
                    for n in range(CH):
                        pool.indirect_dma_start(out=a_src[:, c.ring, n, :], out_offset=None, in_=adj_rows,
                                                in_offset=bass.IndirectOffsetOnAxis(ap=index_now[:, c.ring, 1, n:n + 1], axis=0)
                                                ).then_inc(a_in[c.ring], 16)

                def mask_padding(c):
                    pool.wait_ge(a_in[c.ring], (c.turn + 1) * (16 * CH))
                    pool.tensor_tensor(a_src[:, c.ring], a_src[:, c.ring],
                                       keep["valid"][:, bass.ds(c.t, 1)].rearrange("p a c -> p (a c)").unsqueeze(2).broadcast_to([P, CH, P]),
                                       ALU.mult).then_inc(a_masked, 1)

                def powers(c):
                    pool.wait_ge(var_done, c.t + 1)
                    pool.tensor_tensor(rstd2[:, c.par], var2[:, c.par], minus_half[:, :].broadcast_to([P, 2]),
                                       ALU.pow).then_inc(pow_done, 1)

                pipeline(pool, [(mask_padding, 1), (gather, 2), (powers, -2)])

            @block.tensor
            def _(pe):
                ident, ident16 = keep["ident"], keep["ident16"]

                def turn_sources(c):
                    pe.wait_ge(y_in[c.ring], (c.turn + 1) * (16 * CH))
                    for n in range(CH):
                        b = n % 2
                        wait(pe, turn_read[b], c.t * (3 - b) + n // 2)
                        for m in range(2 * KC):
                            last = pe.transpose(turn_bank[b][:, m, :], y_src[:, c.ring, n, m * P:(m + 1) * P], ident16[:, :])
                        last.then_inc(turn_full[b], 1)
                    pe.wait_ge(a_masked, c.t + 1)
                    wait(pe, pt_low, 2 * (c.t - 1))
                    for b, (lo, hi) in enumerate(BANKS):
                        for n in range(lo, hi):
                            last = pe.transpose(pa_bank[b][:, n - lo, :], a_src[:, c.ring, n, :], ident[:, :])
                        last.then_inc(a_full, 1)

                def scores(c):
                    pe.wait_ge(q_in[c.par], (c.pair + 1) * 16)
                    pe.wait_ge(turn_read[0], c.t * 3 + 3)
                    pe.wait_ge(turn_read[1], c.t * 2 + 2)
                    for b, (lo, hi) in enumerate(BANKS):
                        wait(pe, (y2_low, mt_low)[b], c.t - (3, 1)[b])
                        for k in range(KC):
                            for e, f in PASSES:
                                last = pe.matmul(z_bank[b][:, 0:(hi - lo) * P], q_t[:, c.par, k, e, :],
                                                 y_src_t[:, c.par, f * KC + k, lo * P:hi * P],
                                                 start=(k == 0 and e + f == 0), stop=(k == KC - 1 and e == 1))
                        last.then_inc(z_full, 1)

                def turn_probs(c):
                    pe.wait_ge(prob_ready, c.t + 1)
                    pe.wait_ge(a_read, min(2 * c.t + 4, 2 * NT) if isinstance(c.t, int) else c.t * 2 + 4)
                    for b, (lo, hi) in enumerate(BANKS):
                        for n in range(lo, hi):
                            last = pe.transpose(pa_bank[b][:, n - lo, :], prob[:, c.par, n * P:(n + 1) * P], ident[:, :])
                        last.then_inc(pt_full, 1)

                def mix_sources(c):
                    pe.wait_ge(pt_low, c.t * 2 + 2)
                    wait(pe, mix_ready, c.t)
                    for n in range(CH):
                        for e, f in PASSES:
                            last = pe.matmul(u_bank[:, :], prob_t[:, c.par, n, e, :], y_src[:, c.ring, n, f * D:(f + 1) * D],
                                             start=(n == 0 and e + f == 0), stop=(n == CH - 1 and e == 1))
                    last.then_inc(pv_done, 1)

                def turn_mix(c):
                    pe.wait_ge(mix_ready, c.t + 1)
                    pe.wait_ge(w_done, min(2 * c.t + 4, 2 * NT) if isinstance(c.t, int) else c.t * 2 + 4)
                    for k in range(KC):
                        last = pe.transpose(z_bank[1][:, k * P:(k + 1) * P], mix[:, c.par, k * P:(k + 1) * P], ident[:, :])
                    last.then_inc(mt_full, 1)

                def values(c):
                    pe.wait_ge(mt_low, c.t + 1)
                    wait(pe, o_read, c.t)
                    for k in range(KC):
                        for e, f in PASSES:
                            last = pe.matmul(o_bank[:, :], mix_t[:, c.par, k, e, :], keep["wv"][:, k, f, :],
                                             start=(k == 0 and e + f == 0), stop=(k == KC - 1 and e == 1))
                    last.then_inc(o_full, 1)

                def turn_y2(c):
                    pe.wait_ge(y2_ready, c.t + 1)
                    pe.wait_ge(w_done, min(2 * c.t + 7, 2 * NT) if isinstance(c.t, int) else c.t * 2 + 7)
                    for k in range(KC):
                        last = pe.transpose(z_bank[0][:, k * P:(k + 1) * P], y2[:, c.par, k * P:(k + 1) * P], ident[:, :])
                    last.then_inc(y2_full, 1)

                pipeline(pe, [(scores, 0), (turn_probs, -1), (turn_sources, 1), (turn_y2, -3), (mix_sources, -1),
                              (values, -2), (turn_mix, -1)])

            def leave_turned(eng, c, n):
                b = n % 2
                eng.wait_ge(turn_full[b], c.t * (3 - b) + (n // 2 + 1))
                wait(eng, z_full, 2 * (c.t - 1))
                dst, src = y_src_t[:, c.par, :, n * P:(n + 1) * P], turn_bank[b][:, :, :]
                ins = eng.activation(dst, src, ACT.Copy) if eng is nc.scalar else eng.tensor_copy(dst, src)
                ins.then_inc(turn_read[b], 1)

            @block.scalar
            def _(act):
                act.wait_ge(setup, 2)

                def high_probs(c):
                    wait(act, pv_done, c.t - 1)
                    for b, (lo, hi) in enumerate(BANKS):
                        act.wait_ge(pt_full, c.t * 2 + (b + 1))
                        act.activation(prob_t[:, c.par, lo:hi, 0, :], pa_bank[b][:, 0:hi - lo, :], ACT.Copy).then_inc(pt_high, 1)

                def turned(c):
                    leave_turned(act, c, 0)
                    leave_turned(act, c, 1)

                def adjacency(c):
                    wait(act, w_done, 2 * (c.t - 1))
                    for b, (lo, hi) in enumerate(BANKS):
                        act.wait_ge(a_full, c.t * 2 + (b + 1))
                        act.activation(a_tok[:, c.par, lo * P:hi * P], pa_bank[b][:, 0:hi - lo, :].rearrange("p c t -> p (c t)"),
                                       ACT.Copy).then_inc(a_read, 1)

                def high_y2(c):
                    act.wait_ge(y2_full, c.t + 1)
                    wait(act, y2t_out[c.par], c.pair * 16)
                    act.activation(y2_t[:, c.par, :, 0, :], z_bank[0][:, :].rearrange("p (k t) -> p k t", k=KC), ACT.Copy
                                   ).then_inc(y2_high, 1)

                def exps(c):
                    act.wait_ge(top_ready, c.t + 1)
                    act.activation(one_e[:, c.par], masked[:, :], ACT.Exp, bias=bias[:, c.par], scale=SCALE).then_inc(e_ready, 1)
                    act.activation(prob[:, c.par], prob[:, c.par], ACT.Exp, bias=bias[:, c.par], scale=SCALE,
                                   accum_out=sum_e[:, c.par]).then_inc(e_ready, 1)

                def high_mix(c):
                    act.wait_ge(mt_full, c.t + 1)
                    wait(act, o_full, c.t - 1)
                    act.activation(mix_t[:, c.par, :, 0, :], z_bank[1][:, :].rearrange("p (k t) -> p k t", k=KC), ACT.Copy,
                                   scale=1.0 / PS).then_inc(mt_high, 1)

                pipeline(act, [(high_probs, -1), (turned, 1), (adjacency, 1), (high_y2, -3), (exps, 0), (high_mix, -1)])

            @block.vector
            def _(dve):
                dve.wait_ge(const_in, 16)
                dve.tensor_reduce(rt_sum[:, :], rt_row[:, :], AX_X, ALU.add).then_inc(rt_ready, 1)
                dve.wait_ge(rt_ready, 1)
                softs, probs, rows = StageChain(dve, soft, 2), StageChain(dve, prob_chain, 4), StageChain(dve, x1_chain, 3)
                routes = StageChain(dve, route, 3)

                def low_probs(c):
                    for b, (lo, hi) in enumerate(BANKS):
                        dve.wait_ge(pt_high, c.t * 2 + (b + 1))
                        dve.tensor_tensor(prob_t[:, c.par, lo:hi, 1, :], pa_bank[b][:, 0:hi - lo, :], prob_t[:, c.par, lo:hi, 0, :],
                                          ALU.subtract).then_inc(pt_low, 1)

                def weigh(c):
                    wait(dve, pt_full, 2 * (c.t - 1))
                    for b, (lo, hi) in enumerate(BANKS):
                        dve.wait_ge(z_full, c.t * 2 + (b + 1))
                        dve.wait_ge(a_read, c.t * 2 + (b + 1))
                        dve.scalar_tensor_tensor(prob[:, c.par, lo * P:hi * P], z_bank[b][:, 0:(hi - lo) * P],
                                                 keep["cs"][:, bass.ds(c.t, 1)], a_tok[:, c.par, lo * P:hi * P],
                                                 ALU.add, ALU.mult).then_inc(w_done, 1)

                def turned(c):
                    for n in range(2, CH):
                        leave_turned(dve, c, n)

                def low_y2(c):
                    dve.wait_ge(y2_high, c.t + 1)
                    dve.tensor_tensor(y2_t[:, c.par, :, 1, :], z_bank[0][:, :].rearrange("p (k t) -> p k t", k=KC),
                                      y2_t[:, c.par, :, 0, :], ALU.subtract).then_inc(y2_low, 1)

                def maxima(c):
                    softs.begin(c)
                    dve.wait_ge(w_done, c.t * 2 + 2)
                    softs.step(dve.tensor_scalar(fill[:, :], prob[:, c.par], 0.0, MASKED, ALU.is_equal, ALU.mult))
                    dve.sem_inc(passed_dve, 1)
                    softs.step(dve.tensor_tensor_reduce(out=prob[:, c.par], in0=prob[:, c.par], in1=fill[:, :], scale=1.0,
                                                        scalar=MASKED, op0=ALU.add, op1=ALU.max, accum_out=top[:, c.par]))
                    dve.tensor_scalar(bias[:, c.par], top[:, c.par], -SCALE, float(np.log(PS)), ALU.mult, ALU.add).then_inc(top_ready, 1)
                    softs.end()

                def mixed(c):
                    dve.wait_ge(pv_done, c.t + 1)
                    wait(dve, mt_full, c.t - 1)
                    dve.scalar_tensor_tensor(mix[:, c.par], keep["ytot"][:, :], rest[:, c.par], u_bank[:, :],
                                             ALU.mult, ALU.add).then_inc(mix_ready, 1)

                def normalise(c):
                    probs.begin(c)
                    dve.wait_ge(e_ready, c.t * 2 + 2)
                    probs.step(dve.tensor_scalar(den[:, c.par], sum_e[:, c.par], 1.0 / PS, None, ALU.mult))
                    probs.step(dve.scalar_tensor_tensor(den[:, c.par], one_e[:, c.par], (N - LISTED) / PS, den[:, c.par],
                                                        ALU.mult, ALU.add))
                    probs.step(dve.reciprocal(rden[:, c.par], den[:, c.par]))
                    probs.step(dve.tensor_tensor(rest[:, c.par], one_e[:, c.par], rden[:, c.par], ALU.mult))
                    dve.tensor_scalar(prob[:, c.par], prob[:, c.par], one_e[:, c.par], rden[:, c.par], ALU.subtract,
                                      ALU.mult).then_inc(prob_ready, 1)
                    probs.end()

                def residual(c):
                    rows.begin(c)
                    dve.wait_ge(o_full, c.t + 1)
                    dve.scalar_tensor_tensor(val[:, :], o_bank[:, :], 1.0 / ZS, keep["bvb"][:, :], ALU.mult, ALU.add
                                             ).then_inc(o_read, 1)
                    dve.wait_ge(o_read, c.t + 1)
                    dve.wait_ge(xt_in[c.par], (c.pair + 1) * 16)
                    wait(dve, x1_out[c.par], c.pair * 16)
                    dve.scalar_tensor_tensor(x1[:, c.par], val[:, :], 0.0, x_tok[:, c.par], ALU.max, ALU.add).then_inc(x1_ready, 1)
                    dve.wait_ge(x1_ready, c.t + 1)
                    rows.step(dve.bn_stats(stats2[:, c.par], x1[:, c.par]))
                    dve.sem_inc(passed_dve, 1)
                    rows.step(dve.bn_aggr(mv2[:, c.par], stats2[:, c.par]))
                    dve.tensor_scalar(var2[:, c.par, 0:1], mv2[:, c.par, 1:2], 1.0 / (YS * YS), None, ALU.mult)
                    rows.step(dve.tensor_scalar(var2[:, c.par, 1:2], mv2[:, c.par, 1:2], EPS_LN, 1.0 / (YS * YS), ALU.add, ALU.mult))
                    dve.sem_inc(var_done, 1)
                    rows.end()

                def low_mix(c):
                    dve.wait_ge(mt_high, c.t + 1)
                    dve.scalar_tensor_tensor(mix_t[:, c.par, :, 1, :], z_bank[1][:, :].rearrange("p (k t) -> p k t", k=KC),
                                             1.0 / PS, mix_t[:, c.par, :, 0, :], ALU.mult, ALU.subtract).then_inc(mt_low, 1)

                def norms(c):
                    routes.begin(c)
                    dve.wait_ge(pow_done, c.t + 1)
                    routes.step(dve.scalar_tensor_tensor(alpha[:, c.par], rstd2[:, c.par, 1:2], float(np.sqrt(D)) * 1e12,
                                                         rstd2[:, c.par, 0:1], ALU.mult, ALU.min))
                    wait(dve, y2_out[c.par], c.pair * 16)
                    wait(dve, y2_full, c.t - 1)
                    dve.tensor_scalar(y2[:, c.par], x1[:, c.par], mv2[:, c.par, 0:1], alpha[:, c.par], ALU.subtract,
                                      ALU.mult).then_inc(y2_ready, 1)
                    routes.step(dve.tensor_tensor_reduce(out=dot_junk[:, :], in0=x1[:, c.par], in1=rt_row[:, :], scale=1.0,
                                                         scalar=0.0, op0=ALU.mult, op1=ALU.add, accum_out=dot[:, c.par]))
                    routes.step(dve.scalar_tensor_tensor(off[:, c.par], mv2[:, c.par, 0:1], rt_sum[:, 0:1], dot[:, c.par],
                                                         ALU.mult, ALU.subtract))
                    dve.tensor_scalar(keep["s"][:, bass.ds(c.t, 1)], off[:, c.par], rstd2[:, c.par, 1:2], -1.0 / YS,
                                      ALU.mult, ALU.mult).then_inc(s_ready, 1)
                    routes.end()

                pipeline(dve, [(low_probs, -1), (weigh, 0), (turned, 1), (low_y2, -3), (maxima, 0), (mixed, -1),
                               (normalise, 0), (residual, -2), (low_mix, -1), (norms, -2)])


BANK = 512
PIECES = N // BANK


def attend_all(nc, keep, x, adj, rtok, ytab, qtab, x1tab, y2rows, y2ttab, sem):
    x_tiles = x.rearrange("(t p) d -> t p d", p=P)
    adj_tiles = adj.rearrange("(t p) j -> t p j", p=P)
    x1_tiles = x1tab.rearrange("(t p) d -> t p d", p=P)
    y2_tiles = y2rows.rearrange("(t p) d -> t p d", p=P)
    with ExitStack() as ctx:
        def sb(name, shape, dt):
            return ctx.enter_context(nc.sbuf_tensor(name, shape, dt))

        def pb(name, shape, dt):
            return ctx.enter_context(nc.psum_tensor(name, shape, dt))

        def sems(*names):
            return [sem(n) for n in names]

        ya = sb("all_y", [P, NT, 2 * D], F16)
        ya_t = sb("all_y_t", [P, 2 * KC, N], F16)
        adj_sb = sb("all_adj", [P, 2, BANK], F32)
        q_t = sb("all_q_t", [P, KC, 2, P], F16)
        prob = sb("all_prob", [P, N], F32)
        fill = sb("all_fill", [P, BANK], F32)
        tops, top, bias = sb("all_tops", [P, PIECES], F32), sb("all_top", [P, 1], F32), sb("all_bias", [P, 1], F32)
        sum_e, den, rden = sb("all_sum_e", [P, 1], F32), sb("all_den", [P, 1], F32), sb("all_rden", [P, 1], F32)
        minus_half = sb("all_minus_half", [P, 1], F32)
        prob_t = sb("all_prob_t", [P, 2, 4, 2, P], F16)
        mix, mix_t = sb("all_mix", [P, D], F32), sb("all_mix_t", [P, KC, 2, P], F16)
        x_tok, x1, y2 = sb("all_x_tok", [P, D], F32), sb("all_x1", [P, D], F32), sb("all_y2", [P, D], F32)
        stats, mv = sb("all_stats", [P, 6], F32), sb("all_mv", [P, 2], F32)
        var, rstd = sb("all_var", [P, 2], F32), sb("all_rstd", [P, 2], F32)
        alpha, dot, off = sb("all_alpha", [P, 1], F32), sb("all_dot", [P, 1], F32), sb("all_off", [P, 1], F32)
        rt_row, rt_sum = sb("all_rt_row", [P, D], F32), sb("all_rt_sum", [P, 1], F32)
        y2_t = sb("all_y2_t", [P, KC, 2, P], F16)
        z_bank = [pb(f"all_z_bank{b}", [P, BANK], F32) for b in range(2)]
        p_bank = [pb(f"all_p_bank{b}", [P, 4, P], F32) for b in range(2)]
        turn_bank = [pb(f"all_turn_bank{b}", [P, 2 * KC, P], F16) for b in range(2)]
        u_bank, o_bank = pb("all_u_bank", [P, D], F32), pb("all_o_bank", [P, D], F32)

        ya_in, rt_in, half_ready, rt_ready = sems("all_y_in", "all_rt_in", "all_half_ready", "all_rt_ready")
        turned, left = sems("all_turned", "all_left")
        adj_in = [sem("all_adj_in0"), sem("all_adj_in1")]
        q_in, x_in, x1_out, y2_out, y2t_out = sems("all_q_in", "all_x_in", "all_x1_out", "all_y2_out", "all_y2t_out")
        scored, weighed, adj_free, masking, top_ready = sems("all_scored", "all_weighed", "all_adj_free", "all_masking", "all_top_ready")
        e_ready, prob_ready, p_full, p_high, p_low, p_used = sems("all_e_ready", "all_prob_ready", "all_p_full",
                                                                   "all_p_high", "all_p_low", "all_p_used")
        mix_ready, mt_full, mt_high, mt_low, o_full = sems("all_mix_ready", "all_mt_full", "all_mt_high", "all_mt_low", "all_o_full")
        x1_ready, tail, var_done, pow_done, y2_ready = sems("all_x1_ready", "all_tail", "all_var_done", "all_pow_done", "all_y2_ready")
        y2_full, y2_high, y2_low, carried = sems("all_y2_full", "all_y2_high", "all_y2_low", "all_carried")

        with nc.Block() as block:
            @block.sync
            def _(sp):
                sp.dma_start(rt_row[:, :], rtok.partition_broadcast(P)).then_inc(rt_in, 16)
                sp.dma_start(ya[:, :, :], ytab.rearrange("(c p) d -> p c d", p=P)).then_inc(ya_in, 16)
                sp.sem_inc(adj_free, 2)
                with sp.Fori(0, NT) as t:
                    sp.wait_ge(scored, t * PIECES)
                    sp.dma_start(q_t[:, :, :, :].rearrange("p k e t -> p (k e t)"),
                                 qtab[bass.ds(t, 1)].rearrange("a p n -> p (a n)")).then_inc(q_in, 16)
                    sp.wait_ge(x1_ready, t)
                    sp.dma_start(x_tok[:, :], x_tiles[bass.ds(t, 1)].rearrange("a p n -> p (a n)")).then_inc(x_in, 16)
                    for b in range(PIECES):
                        sp.wait_ge(adj_free, t * PIECES + (b + 1))
                        sp.dma_start(adj_sb[:, b % 2], adj_tiles[bass.ds(t, 1), :, b * BANK:(b + 1) * BANK]
                                     .rearrange("a p n -> p (a n)")).then_inc(adj_in[b % 2], 16)
                    sp.wait_ge(x1_ready, t + 1)
                    sp.dma_start(x1_tiles[bass.ds(t, 1)].rearrange("a p n -> p (a n)"), x1[:, :]).then_inc(x1_out, 16)
                    sp.wait_ge(y2_ready, t + 1)
                    sp.dma_start(y2_tiles[bass.ds(t, 1)].rearrange("a p n -> p (a n)"), y2[:, :]).then_inc(y2_out, 16)
                    sp.wait_ge(y2_low, t + 1)
                    sp.dma_start(y2ttab[bass.ds(t, 1)].rearrange("a p n -> p (a n)"),
                                 y2_t[:, :, :, :].rearrange("p k e t -> p (k e t)")).then_inc(y2t_out, 16)
                for s in (x1_out, y2_out, y2t_out):
                    sp.wait_ge(s, 16 * NT)

            @block.gpsimd
            def _(pool):
                pool.memset(minus_half[:, :], -0.5).then_inc(half_ready, 1)
                pool.wait_ge(half_ready, 1)
                with pool.Fori(0, NT) as t:
                    pool.wait_ge(var_done, t + 1)
                    pool.tensor_tensor(rstd[:, :], var[:, :], minus_half[:, :].broadcast_to([P, 2]), ALU.pow).then_inc(pow_done, 1)

            @block.tensor
            def _(pe):
                ident, ident16 = keep["ident"], keep["ident16"]
                pe.wait_ge(ya_in, 16)
                with pe.Fori(0, NT // 2) as i:
                    for h in range(2):
                        pe.wait_ge(left, i * 2)
                        for m in range(2 * KC):
                            last = pe.transpose(turn_bank[h][:, m, :],
                                                ya[:, bass.ds(i * 2 + h, 1), m * P:(m + 1) * P].rearrange("p a n -> p (a n)"),
                                                ident16[:, :])
                        last.then_inc(turned, 1)
                pe.wait_ge(left, NT)
                with pe.Fori(0, NT) as t:
                    pe.wait_ge(q_in, t * 16 + 16)
                    pe.wait_ge(y2_low, t)
                    for b in range(PIECES):
                        pe.wait_ge(weighed, t * PIECES + max(b - 1, 0))
                        for k in range(KC):
                            for e, f in PASSES:
                                last = pe.matmul(z_bank[b % 2][:, :], q_t[:, k, e, :], ya_t[:, f * KC + k, b * BANK:(b + 1) * BANK],
                                                 start=(k == 0 and e + f == 0), stop=(k == KC - 1 and e == 1))
                        last.then_inc(scored, 1)
                    pe.wait_ge(prob_ready, t + 1)
                    for g in range(PIECES):
                        pe.wait_ge(p_low, t * PIECES + g)
                        for n in range(4):
                            last = pe.transpose(p_bank[g % 2][:, n, :], prob[:, (4 * g + n) * P:(4 * g + n + 1) * P], ident[:, :])
                        last.then_inc(p_full, 1)
                        pe.wait_ge(p_low, t * PIECES + (g + 1))
                        for n in range(4):
                            for e, f in PASSES:
                                last = pe.matmul(u_bank[:, :], prob_t[:, g % 2, n, e, :], ya[:, 4 * g + n, f * D:(f + 1) * D],
                                                 start=(g + n + e + f == 0), stop=(g == PIECES - 1 and n == 3 and e == 1))
                        last.then_inc(p_used, 1)
                    pe.wait_ge(mix_ready, t + 1)
                    for k in range(KC):
                        last = pe.transpose(z_bank[1][:, k * P:(k + 1) * P], mix[:, k * P:(k + 1) * P], ident[:, :])
                    last.then_inc(mt_full, 1)
                    pe.wait_ge(mt_low, t + 1)
                    for k in range(KC):
                        for e, f in PASSES:
                            last = pe.matmul(o_bank[:, :], mix_t[:, k, e, :], keep["wv"][:, k, f, :],
                                             start=(k == 0 and e + f == 0), stop=(k == KC - 1 and e == 1))
                    last.then_inc(o_full, 1)
                    pe.wait_ge(y2_ready, t + 1)
                    for k in range(KC):
                        last = pe.transpose(z_bank[0][:, k * P:(k + 1) * P], y2[:, k * P:(k + 1) * P], ident[:, :])
                    last.then_inc(y2_full, 1)

            @block.scalar
            def _(act):
                with act.Fori(0, NT) as t:
                    act.wait_ge(top_ready, t + 1)
                    act.activation(prob[:, :], prob[:, :], ACT.Exp, bias=bias[:, :], scale=SCALE, accum_out=sum_e[:, :]
                                   ).then_inc(e_ready, 1)
                    for g in range(PIECES):
                        act.wait_ge(p_full, t * PIECES + (g + 1))
                        act.wait_ge(p_used, t * PIECES + max(g - 1, 0))
                        act.activation(prob_t[:, g % 2, :, 0, :], p_bank[g % 2][:, :, :], ACT.Copy).then_inc(p_high, 1)
                    act.wait_ge(mt_full, t + 1)
                    act.activation(mix_t[:, :, 0, :], z_bank[1][:, :].rearrange("p (k t) -> p k t", k=KC), ACT.Copy,
                                   scale=1.0 / PS).then_inc(mt_high, 1)
                    act.wait_ge(y2_full, t + 1)
                    act.wait_ge(y2t_out, t * 16)
                    act.activation(y2_t[:, :, 0, :], z_bank[0][:, :].rearrange("p (k t) -> p k t", k=KC), ACT.Copy
                                   ).then_inc(y2_high, 1)

            @block.vector
            def _(dve):
                dve.wait_ge(rt_in, 16)
                dve.tensor_reduce(rt_sum[:, :], rt_row[:, :], AX_X, ALU.add).then_inc(rt_ready, 1)
                dve.wait_ge(rt_ready, 1)
                with dve.Fori(0, NT // 2) as i:
                    for h in range(2):
                        dve.wait_ge(turned, i * 2 + (h + 1))
                        dve.tensor_copy(ya_t[:, :, bass.ds(i * (2 * P) + h * P, P)], turn_bank[h][:, :, :]).then_inc(left, 1)
                with dve.Fori(0, NT) as t:
                    masks = Chain(dve, masking)
                    masks.base = t * (2 * PIECES + 1)
                    dve.wait_ge(p_full, t * PIECES)
                    for b in range(PIECES):
                        piece = prob[:, b * BANK:(b + 1) * BANK]
                        dve.wait_ge(scored, t * PIECES + (b + 1))
                        dve.wait_ge(adj_in[b % 2], t * (8 * PIECES) + 16 * (b // 2 + 1))
                        dve.scalar_tensor_tensor(piece, z_bank[b % 2][:, :], keep["cs"][:, bass.ds(t, 1)], adj_sb[:, b % 2],
                                                 ALU.add, ALU.mult).then_inc(weighed, 1)
                        dve.wait_ge(weighed, t * PIECES + (b + 1))
                        dve.sem_inc(adj_free, 1)
                        masks.step(dve.tensor_scalar(fill[:, :], piece, 0.0, MASKED, ALU.is_equal, ALU.mult))
                        dve.sem_inc(carried, 1)
                        masks.step(dve.tensor_tensor_reduce(out=piece, in0=piece, in1=fill[:, :], scale=1.0, scalar=MASKED,
                                                            op0=ALU.add, op1=ALU.max, accum_out=tops[:, b:b + 1]))
                    masks.step(dve.tensor_reduce(top[:, :], tops[:, :], AX_X, ALU.max))
                    dve.tensor_scalar(bias[:, :], top[:, :], -SCALE, float(np.log(PS)), ALU.mult, ALU.add).then_inc(top_ready, 1)
                    ch = Chain(dve, tail)
                    ch.base = t * 10
                    dve.wait_ge(e_ready, t + 1)
                    ch.step(dve.tensor_scalar(den[:, :], sum_e[:, :], 1.0 / PS, None, ALU.mult))
                    ch.step(dve.reciprocal(rden[:, :], den[:, :]))
                    dve.tensor_scalar(prob[:, :], prob[:, :], rden[:, :], None, ALU.mult).then_inc(prob_ready, 1)
                    for g in range(PIECES):
                        dve.wait_ge(p_high, t * PIECES + (g + 1))
                        dve.tensor_tensor(prob_t[:, g % 2, :, 1, :], p_bank[g % 2][:, :, :], prob_t[:, g % 2, :, 0, :],
                                          ALU.subtract).then_inc(p_low, 1)
                    dve.wait_ge(p_used, t * PIECES + PIECES)
                    dve.tensor_copy(mix[:, :], u_bank[:, :]).then_inc(mix_ready, 1)
                    dve.wait_ge(mt_high, t + 1)
                    dve.scalar_tensor_tensor(mix_t[:, :, 1, :], z_bank[1][:, :].rearrange("p (k t) -> p k t", k=KC),
                                             1.0 / PS, mix_t[:, :, 0, :], ALU.mult, ALU.subtract).then_inc(mt_low, 1)
                    dve.wait_ge(o_full, t + 1)
                    dve.wait_ge(x1_out, t * 16)
                    ch.step(dve.scalar_tensor_tensor(x1[:, :], o_bank[:, :], 1.0 / ZS, keep["bvb"][:, :], ALU.mult, ALU.add))
                    dve.wait_ge(x_in, t * 16 + 16)
                    dve.scalar_tensor_tensor(x1[:, :], x1[:, :], 0.0, x_tok[:, :], ALU.max, ALU.add).then_inc(x1_ready, 1)
                    dve.wait_ge(x1_ready, t + 1)
                    ch.step(dve.bn_stats(stats[:, :], x1[:, :]))
                    dve.sem_inc(carried, 1)
                    ch.step(dve.bn_aggr(mv[:, :], stats[:, :]))
                    dve.tensor_scalar(var[:, 0:1], mv[:, 1:2], 1.0 / (YS * YS), None, ALU.mult)
                    ch.step(dve.tensor_scalar(var[:, 1:2], mv[:, 1:2], EPS_LN, 1.0 / (YS * YS), ALU.add, ALU.mult))
                    dve.sem_inc(var_done, 1)
                    dve.wait_ge(pow_done, t + 1)
                    ch.step(dve.scalar_tensor_tensor(alpha[:, :], rstd[:, 1:2], float(np.sqrt(D)) * 1e12, rstd[:, 0:1],
                                                     ALU.mult, ALU.min))
                    dve.wait_ge(y2_out, t * 16)
                    dve.tensor_scalar(y2[:, :], x1[:, :], mv[:, 0:1], alpha[:, :], ALU.subtract, ALU.mult).then_inc(y2_ready, 1)
                    ch.step(dve.tensor_tensor_reduce(out=fill[:, :], in0=x1[:, :], in1=rt_row[:, :], scale=1.0, scalar=0.0,
                                                     op0=ALU.mult, op1=ALU.add, accum_out=dot[:, :]))
                    ch.step(dve.scalar_tensor_tensor(off[:, :], mv[:, 0:1], rt_sum[:, 0:1], dot[:, :], ALU.mult, ALU.subtract))
                    ch.step(dve.tensor_scalar(keep["s"][:, bass.ds(t, 1)], off[:, :], rstd[:, 1:2], -1.0 / YS, ALU.mult, ALU.mult))
                    dve.wait_ge(y2_high, t + 1)
                    dve.tensor_tensor(y2_t[:, :, 1, :], z_bank[0][:, :].rearrange("p (k t) -> p k t", k=KC), y2_t[:, :, 0, :],
                                      ALU.subtract).then_inc(y2_low, 1)
                    dve.wait_ge(y2_low, t + 1)


K_ROUTE = 8.0
EPS_ROUTE = 0.1
RECENTRE = 12
CAP = 76.0
UNDERFLOW = -87.33654
LN_SHIFT = 50
LATE_STEPS = 2


def feed_forward(nc, keep, ytab2t, x1tab, y2rows, wtab, b1l, b2l, b1h, b2h, out, sem):
    out_tiles = out.rearrange("(t p) d -> t p d", p=P)
    x1_tiles = x1tab.rearrange("(t p) d -> t p d", p=P)
    y2t_groups = ytab2t.rearrange("(g s) p n -> g p s n", s=GROUP)
    with ExitStack() as ctx:
        def sb(name, shape, dt):
            return ctx.enter_context(nc.sbuf_tensor(name, shape, dt))

        def sems(*names):
            return [sem(n) for n in names]

        w1l_sb, w2l_sb = sb("w1l_sb", [P, 2, KC, HL], F16), sb("w2l_sb", [P, 2, HL // P, D], F16)
        w1h_sb = sb("w1h_sb", [P, KC, 2, HH], F16)
        w2h_sb = sb("w2h_sb", [P, HH // P // 4, 2, 4, D], F16)
        b1l_sb, b1h_sb = sb("b1l_sb", [P, HL // P], F32), sb("b1h_sb", [P, HH // P], F32)
        b2l_row, b2h_row = sb("b2l_row", [P, D], F32), sb("b2h_row", [P, D], F32)
        score = sb("score", [P, NT], F32)
        ones = sb("ones_c", [P, P], F32)
        threshold = sb("threshold", [P, 1], I32)
        w_in, b_in, heavy_in = sems("w_in", "b_in", "heavy_in")

        hidden_ctx = ExitStack()
        hid = hidden_ctx.enter_context(nc.sbuf_tensor("hid", [P, HL // P, N], F32))
        with ExitStack() as c1:
            def tmp(name, shape, dt):
                return c1.enter_context(nc.sbuf_tensor(name, shape, dt))

            y_in_t = tmp("y_in_t", [P, 2, GROUP, KC, 2, P], F16)
            eighths = tmp("eighths", [P, P], F32)
            logits = tmp("logits", [P, NT + 1], F32)
            args, weights = tmp("args", [P, NT + 1], F32), tmp("weights", [P, NT + 1], F32)
            part, centre, s_top, s_part = (tmp(n, [P, 1], F32) for n in ("part_sum", "centre", "s_top", "s_part"))
            junk, log_a, low = tmp("junk", [P, NT], F32), tmp("log_a", [P, 1], F32), tmp("low", [P, NT], F32)
            ps_h = [c1.enter_context(nc.psum_tensor(f"ps_h{i}", [P, GROUP * P], F32)) for i in range(4)]
            ps_a = c1.enter_context(nc.psum_tensor("ps_a", [P, 1], F32))
            g_in, g_free = [sem("g_in0"), sem("g_in1")], sem("g_free")
            c1_const, top_in, top_out, h_full, h_read = sems("c1_const", "top_in", "top_out", "h_full", "h_read")
            dve3, args_ready, exp_ready, part_ready, sum_ready, log_ready = sems(
                "dve3", "args_ready", "exp_ready", "part_ready", "sum_ready", "log_ready")
            alpha_ready, final_ready = sems("alpha_ready", "final_ready")
            TURNS = NG // 2

            with nc.Block() as block:
                @block.sync
                def _(sp):
                    wv = wtab.rearrange("u p (h n) -> u p h n", h=2)
                    sp.dma_start(w1l_sb[:, :, :, :].rearrange("p h c n -> p h (c n)"), wv[8][:, :, 0:KC * HL]).then_inc(w_in, 16)
                    sp.dma_start(w2l_sb[:, :, :, :].rearrange("p h c n -> p h (c n)"), wv[9][:, :, 0:HL // P * D]).then_inc(w_in, 16)
                    sp.dma_start(b1l_sb[:, :], b1l.rearrange("(c p) -> p c", p=P), allow_slow_non_contiguous=True).then_inc(b_in, 16)
                    sp.dma_start(b1h_sb[:, :], b1h.rearrange("(c p) -> p c", p=P), allow_slow_non_contiguous=True).then_inc(b_in, 16)
                    sp.dma_start(b2l_row[:, :], b2l.partition_broadcast(P)).then_inc(b_in, 16)
                    sp.dma_start(b2h_row[:, :], b2h.partition_broadcast(P)).then_inc(b_in, 16)
                    sp.sem_inc(g_free, 2)
                    with sp.Fori(0, TURNS) as i:
                        for h in range(2):
                            sp.wait_ge(g_free, i * 2 + (h + 1))
                            sp.dma_start(y_in_t[:, h].rearrange("p s k e t -> p s (k e t)"),
                                         y2t_groups[bass.ds(i * 2 + h, 1)].rearrange("a p s n -> p (a s) n")).then_inc(g_in[h], 16)
                    for k in range(KC):
                        sp.dma_start(w1h_sb[:, k], wv[k]).then_inc(heavy_in, 16)
                        sp.dma_start(w2h_sb[:, k].rearrange("p h c n -> p h (c n)"), wv[KC + k]).then_inc(heavy_in, 16)

                @block.gpsimd
                def _(pool):
                    pool.memset(eighths[:, :], 1.0 / K_ROUTE).then_inc(c1_const, 1)
                    pool.memset(ones[:, :], 1.0).then_inc(c1_const, 1)
                    pool.wait_ge(top_in, 1)
                    pool.partition_all_reduce(s_top[:, :], s_part[:, :], P, bass.bass_isa.ReduceOp.max).then_inc(top_out, 1)

                @block.vector
                def _(dve):
                    ch = Chain(dve, dve3)
                    ch.step(dve.tensor_copy(logits[:, 0:NT], keep["s"][:, :]))
                    dve.memset(logits[:, NT:NT + 1], 0.0)
                    dve.tensor_reduce(s_part[:, :], keep["s"][:, :], AX_X, ALU.max).then_inc(top_in, 1)
                    dve.wait_ge(top_out, 1)
                    ch.step(dve.tensor_copy(low[:, 0:1], s_part[:, :]))

                    def recentre(turn):
                        ch.step(dve.tensor_tensor(centre[:, :], logits[:, NT:NT + 1], s_top[:, :], ALU.min))
                        ch.step(dve.tensor_scalar(args[:, :], logits[:, :], centre[:, :], 1.0 / EPS_ROUTE, ALU.subtract, ALU.mult))
                        dve.tensor_scalar(args[:, :], args[:, :], CAP, None, ALU.min).then_inc(args_ready, 1)
                        dve.wait_ge(exp_ready, turn + 1)

                    def descend(done, count, first):
                        for n in range(count):
                            if n > 0:
                                dve.wait_ge(sum_ready, done + n)
                            a = weights[:, NT:NT + 1] if n == 0 else ps_a[:, :]
                            dve.tensor_scalar(junk[:, :], weights[:, 0:NT], a, None, ALU.min, ALU.add,
                                              accum_out=part[:, :]).then_inc(part_ready, 1)

                    def take_log(turn, done):
                        dve.wait_ge(log_ready, turn + 1)
                        ch.step(dve.tensor_scalar(log_a[:, :], log_a[:, :], LN_SHIFT * float(np.log(2.0)), EPS_ROUTE, ALU.add, ALU.mult))
                        ch.step(dve.tensor_tensor(logits[:, NT:NT + 1], log_a[:, :], centre[:, :], ALU.add))

                    base = ch.n
                    with dve.Fori(0, TURNS) as i:
                        ch.base, ch.n = i * 4 + base, 0
                        recentre(i)
                        descend(i * RECENTRE, RECENTRE, False)
                        take_log(i, i * RECENTRE)
                    ch.base, ch.n = 0, base + 4 * TURNS
                    recentre(TURNS)
                    descend(TURNS * RECENTRE, LATE_STEPS, False)
                    take_log(TURNS, TURNS * RECENTRE)
                    ch.step(dve.tensor_scalar(args[:, 0:NT], keep["s"][:, :], logits[:, NT:NT + 1], None, ALU.subtract))
                    ch.step(dve.tensor_scalar(low[:, :], args[:, 0:NT], 0.0, None, ALU.max))
                    ch.step(dve.tensor_tensor(args[:, 0:NT], args[:, 0:NT], low[:, :], ALU.subtract))
                    ch.step(dve.tensor_scalar(args[:, 0:NT], args[:, 0:NT], 1.0 / EPS_ROUTE, None, ALU.mult))
                    ch.step(dve.tensor_scalar(low[:, :], args[:, 0:NT], UNDERFLOW, None, ALU.is_ge))
                    dve.sem_inc(final_ready, 1)
                    dve.wait_ge(exp_ready, TURNS + 2)
                    dve.tensor_tensor(score[:, :], weights[:, 0:NT], low[:, :], ALU.mult)

                @block.scalar
                def _(act):
                    act.wait_ge(b_in, 64)

                    def leave_hidden(g, h):
                        for c in range(HL // P):
                            act.wait_ge(h_full, g * 2 + (c + 1))
                            act.activation(hid[:, c, bass.ds(g * (GROUP * P), GROUP * P)], ps_h[2 * h + c][:, :], ACT.Identity,
                                           bias=b1l_sb[:, c:c + 1], scale=1.0 / ZS).then_inc(h_read, 1)
                        act.sem_inc(g_free, 1)

                    def exps(turn):
                        act.wait_ge(args_ready, turn + 1)
                        act.activation(weights[:, :], args[:, :], ACT.Exp).then_inc(exp_ready, 1)

                    def logs(turn, done):
                        act.wait_ge(sum_ready, done)
                        act.activation(log_a[:, :], ps_a[:, :], ACT.Ln, scale=2.0 ** -LN_SHIFT).then_inc(log_ready, 1)

                    with act.Fori(0, TURNS) as i:
                        exps(i)
                        for h in range(2):
                            leave_hidden(i * 2 + h, h)
                        logs(i, i * RECENTRE + RECENTRE)
                    exps(TURNS)
                    logs(TURNS, TURNS * RECENTRE + LATE_STEPS)
                    act.wait_ge(final_ready, 1)
                    act.activation(weights[:, 0:NT], args[:, 0:NT], ACT.Exp).then_inc(exp_ready, 1)

                @block.tensor
                def _(pe):
                    pe.wait_ge(w_in, 32)
                    pe.wait_ge(c1_const, 2)

                    def total(done):
                        pe.wait_ge(part_ready, done + 1)
                        pe.matmul(ps_a[:, :], eighths[:, :], part[:, :], start=True, stop=True).then_inc(sum_ready, 1)

                    with pe.Fori(0, TURNS) as i:
                        for h in range(2):
                            g = i * 2 + h
                            pe.wait_ge(g_in[h], i * 16 + 16)
                            pe.wait_ge(h_read, i * 4)
                            units = [(c, k, e, f) for c in range(HL // P) for k in range(KC) for e, f in PASSES]
                            for n, (c, k, e, f) in enumerate(units):
                                last = pe.matmul(ps_h[2 * h + c][:, :], w1l_sb[:, e, k, c * P:(c + 1) * P],
                                                 y_in_t[:, h, :, k, f, :], start=(k == 0 and e + f == 0), stop=(k == KC - 1 and e == 1))
                                if k == KC - 1 and e == 1:
                                    last.then_inc(h_full, 1)
                                if n % 4 == 3:
                                    total(i * RECENTRE + (h * RECENTRE // 2 + n // 4))
                    for n in range(LATE_STEPS):
                        total(TURNS * RECENTRE + n)

        with ExitStack() as c2:
            def tmp(name, shape, dt):
                return c2.enter_context(nc.sbuf_tensor(name, shape, dt))

            act_h = tmp("act_h", [P, 2, HL // P, P], F32)
            act_hl = tmp("act_hl", [P, 2, HL // P, 2, P], F16)
            x1_in_sb = tmp("x1_in_sb", [P, 2, D], F32)
            sum_b = tmp("sum_b", [P, 2, D], F32)
            res = tmp("res", [P, 2, D], F32)
            bit, cand, met = tmp("bit", [P, 1], I32), tmp("cand", [P, 1], I32), tmp("met", [P, 1], I32)
            junk2, count = tmp("junk2", [P, NT], F32), tmp("count", [P, 1], F32)
            ps_o = [c2.enter_context(nc.psum_tensor(f"ps_o{i}", [P, D], F32)) for i in range(2)]
            ps_n = c2.enter_context(nc.psum_tensor("ps_n", [P, 1], F32))
            x1_in, res_out = [sem("x1_in0"), sem("x1_in1")], [sem("res_out0"), sem("res_out1")]
            gelu_ready, act_high, act_low, o2_full, o2_read, res_ready = sems(
                "gelu_ready", "act_high", "act_low", "o2_full", "o2_read", "res_ready")
            search, counted, totalled, x1_free = sems("search", "counted", "totalled", "x1_free")
            PAIRS = NT // 2
            passed3, passed4 = sems("passed3", "passed4")

            with nc.Block() as block:
                @block.sync
                def _(sp):
                    sp.sem_inc(x1_free, 2)
                    with sp.Fori(0, PAIRS) as i:
                        for h in range(2):
                            t = i * 2 + h
                            sp.wait_ge(x1_free, t + 1)
                            sp.dma_start(x1_in_sb[:, h], x1_tiles[bass.ds(t, 1)].rearrange("a p n -> p (a n)")).then_inc(x1_in[h], 16)
                    for h in range(2):
                        sp.wait_ge(res_out[h], 16 * PAIRS)

                @block.gpsimd
                def _(pool):
                    with pool.Fori(0, PAIRS) as i:
                        for h in range(2):
                            pool.wait_ge(res_ready, i * 2 + (h + 1))
                            pool.sem_inc(passed3, 1)
                            pool.dma_start(out_tiles[bass.ds(i * 2 + h, 1)].rearrange("a p n -> p (a n)"), res[:, h]
                                           ).then_inc(res_out[h], 16)

                @block.scalar
                def _(act):
                    with act.Fori(0, PAIRS) as i:
                        for h in range(2):
                            t = i * 2 + h
                            act.wait_ge(act_low, i * 2)
                            act.activation(act_h[:, h], hid[:, :, bass.ds(t * P, P)], ACT.Gelu).then_inc(gelu_ready, 1)
                            act.wait_ge(gelu_ready, t + 1)
                            act.wait_ge(o2_full, i * 2)
                            act.activation(act_hl[:, h, :, 0, :], act_h[:, h], ACT.Copy, scale=YS).then_inc(act_high, 1)

                @block.vector
                def _(dve):
                    ch = Chain(dve, search)
                    dve.memset(bit[:, :], 1 << 29)
                    ch.step(dve.memset(threshold[:, :], 0))
                    with dve.Fori(0, PAIRS) as i:
                        ch.base, ch.n = i * 8 + 1, 0
                        for h in range(2):
                            t = i * 2 + h
                            ch.step(dve.tensor_tensor(cand[:, :], threshold[:, :], bit[:, :], ALU.bitwise_or))
                            dve.tensor_scalar(junk2[:, :], score[:, :], cand[:, :].bitcast(F32), None, ALU.is_ge, ALU.add,
                                              accum_out=count[:, :]).then_inc(counted, 1)
                            ch.step(dve.tensor_single_scalar(bit[:, :], bit[:, :], 1, ALU.logical_shift_right))
                            dve.wait_ge(act_high, t + 1)
                            dve.scalar_tensor_tensor(act_hl[:, h, :, 1, :], act_h[:, h], YS, act_hl[:, h, :, 0, :],
                                                     ALU.mult, ALU.subtract).then_inc(act_low, 1)
                            dve.wait_ge(totalled, t + 1)
                            ch.step(dve.tensor_scalar(met[:, :], ps_n[:, :], float(ROUTED), None, ALU.is_ge))
                            dve.sem_inc(passed4, 1)
                            ch.step(dve.copy_predicated(threshold[:, :], met[:, :], cand[:, :]))
                            dve.wait_ge(x1_in[h], i * 16 + 16)
                            dve.tensor_tensor(sum_b[:, h], x1_in_sb[:, h], b2l_row[:, :], ALU.add).then_inc(x1_free, 1)
                            dve.wait_ge(x1_free, t + 3)
                            dve.wait_ge(o2_full, t + 1)
                            dve.wait_ge(res_out[h], i * 16)
                            dve.scalar_tensor_tensor(res[:, h], ps_o[h][:, :], 1.0 / ZS, sum_b[:, h], ALU.mult, ALU.add
                                                     ).then_inc(res_ready, 1)

                @block.tensor
                def _(pe):
                    with pe.Fori(0, PAIRS) as i:
                        for h in range(2):
                            t = i * 2 + h
                            pe.wait_ge(counted, t + 1)
                            pe.matmul(ps_n[:, :], ones[:, :], count[:, :], start=True, stop=True).then_inc(totalled, 1)
                            pe.wait_ge(act_low, t + 1)
                            pe.wait_ge(res_ready, i * 2)
                            for c in range(HL // P):
                                for e, f in PASSES:
                                    last = pe.matmul(ps_o[h][:, :], act_hl[:, h, c, e, :], w2l_sb[:, f, c, :],
                                                     start=(c == 0 and e + f == 0), stop=(c == 1 and e == 1))
                            last.then_inc(o2_full, 1)

        hidden_ctx.close()
        route_and_heavy(nc, keep, score, threshold, ones, y2rows, w1h_sb, w2h_sb, b1h_sb, b2h_row, heavy_in, out, sem)


def route_and_heavy(nc, keep, score, threshold, ones, y2rows, w1h_sb, w2h_sb, b1h_sb, b2h_row, heavy_in, out, sem):
    B = ROUTED // P
    HC = HH // P
    with ExitStack() as ctx:
        def sb(name, shape, dt):
            return ctx.enter_context(nc.sbuf_tensor(name, shape, dt))

        def sems(*names):
            return [sem(n) for n in names]

        before = sb("before", [P, P], F32)
        above, level = sb("above", [P, NT], F32), sb("level", [P, NT], F32)
        run = sb("run", [P, 2, NT], F32)
        need, n_above = sb("need", [P, 1], F32), sb("n_above", [P, 1], F32)
        place, taken = sb("place", [P, NT], F32), sb("taken", [P, NT], F32)
        slots_i, slots = sb("slots_i", [P, ROUTED], I32), sb("slots", [P, ROUTED], F16)
        slots_f = sb("slots_f", [P, ROUTED], F32)
        gain = sb("gain", [P, NT], F32)
        facts = sb("facts", [P, NT, 4], F16)
        p_i, t_i = sb("p_i", [P, 1], I32), sb("t_i", [P, NT], I32)
        hot = sb("hot", [P, 2, ROUTED], F16)
        found = sb("found", [P, B, 4], F32)
        token_f, token, gains = sb("token_f", [P, B], F32), sb("token", [P, B], I32), sb("gains_r", [P, B], F32)
        y_rt = sb("y_rt", [P, B, D], F32)
        y_rt_t = sb("y_rt_t", [P, KC, 2, ROUTED], F16)
        base = sb("base", [P, B, D], F32)
        g32 = sb("g32", [P, 2, ROUTED], F32)
        g_hl = sb("g_hl", [P, HC, 2, ROUTED], F16)
        fin = sb("fin", [P, B, D], F32)
        ps_w = ctx.enter_context(nc.psum_tensor("ps_w", [P, 3, NT], F32))
        ps_f = ctx.enter_context(nc.psum_tensor("ps_f", [P, B, 4], F32))
        ps_r = [ctx.enter_context(nc.psum_tensor(f"ps_r{i}", [P, KC, P], F32)) for i in range(2)]
        ps_u = [ctx.enter_context(nc.psum_tensor(f"ps_u{i}", [P, D], F32)) for i in range(4)]

        tri_ready, iota2, dve4, sel_ready, prefix_ready = sems("tri_ready", "iota2", "dve4", "sel_ready", "prefix_ready")
        hot_ready, facts_ready, found_ready, token_ready = sems("hot_ready", "facts_ready", "found_ready", "token_ready")
        hot_used = sem("hot_used")
        rows_in = [sem(f"rows_in{b}") for b in range(B)]
        base_in, r_full, r_high, r_low, u_full, u_act, u_high, u_low = sems(
            "base_in", "r_full", "r_high", "r_low", "u_full", "u_act", "u_high", "u_low")
        d_full, d_read, fin_ready, fin_out = sems("d_full", "d_read", "fin_ready", "fin_out")

        with nc.Block() as block:
            @block.gpsimd
            def _(pool):
                pool.memset(before[:, :], 1.0).then_inc(tri_ready, 1)
                pool.wait_ge(tri_ready, 1)
                pool.affine_select(out=before[:, :], in_=before[:, :], compare_op=ALU.is_gt, fill=0.0, base=0,
                                   pattern=[[1, P]], channel_multiplier=-1).then_inc(tri_ready, 1)
                pool.iota(slots_i[:, :], pattern=[[1, ROUTED]], base=0, channel_multiplier=0).then_inc(iota2, 1)
                pool.iota(p_i[:, :], pattern=[[0, 1]], base=0, channel_multiplier=1).then_inc(iota2, 1)
                pool.iota(t_i[:, :], pattern=[[1, NT]], base=0, channel_multiplier=0).then_inc(iota2, 1)
                pool.wait_ge(token_ready, 1)
                for b in range(B):
                    pool.indirect_dma_start(out=y_rt[:, b, :], out_offset=None, in_=y2rows,
                                            in_offset=bass.IndirectOffsetOnAxis(ap=token[:, b:b + 1], axis=0)).then_inc(rows_in[b], 16)
                for b in range(B):
                    pool.indirect_dma_start(out=base[:, b, :], out_offset=None, in_=out,
                                            in_offset=bass.IndirectOffsetOnAxis(ap=token[:, b:b + 1], axis=0)).then_inc(base_in, 16)
                for b in range(B):
                    pool.wait_ge(fin_ready, b + 1)
                    pool.indirect_dma_start(out=out, out_offset=bass.IndirectOffsetOnAxis(ap=token[:, b:b + 1], axis=0),
                                            in_=fin[:, b, :], in_offset=None).then_inc(fin_out, 16)
                pool.wait_ge(fin_out, 16 * B)

            @block.vector
            def _(dve):
                ch = Chain(dve, dve4)
                level_f = threshold[:, :].bitcast(F32)
                dve.wait_ge(iota2, 3)
                dve.tensor_copy(slots[:, :], slots_i[:, :])
                dve.tensor_copy(facts[:, :, 0], p_i[:, :].broadcast_to([P, NT]))
                dve.tensor_copy(facts[:, :, 1], t_i[:, :])
                dve.tensor_scalar(above[:, :], score[:, :], level_f, None, ALU.is_gt)
                ch.step(dve.tensor_scalar(gain[:, :], score[:, :], -1.0, 1.0, ALU.mult, ALU.add))
                ch.step(dve.tensor_tensor(gain[:, :], gain[:, :], score[:, :], ALU.add))
                ch.step(dve.tensor_copy(facts[:, :, 2], gain[:, :]))
                ch.step(dve.tensor_tensor(facts[:, :, 3], gain[:, :], facts[:, :, 2], ALU.subtract))
                ch.step(dve.tensor_scalar(level[:, :], score[:, :], level_f, None, ALU.is_equal))
                dve.sem_inc(sel_ready, 1)

                def running(n):
                    dve.wait_ge(prefix_ready, n)
                    ch.step(dve.memset(run[:, 0, 0:1], 0.0))
                    ch.step(dve.tensor_copy(run[:, 0, 1:NT], ps_w[:, 1, 0:NT - 1]))
                    src, d = 0, 1
                    while d < NT:
                        ch.step(dve.tensor_copy(run[:, 1 - src, 0:d], run[:, src, 0:d]))
                        ch.step(dve.tensor_tensor(run[:, 1 - src, d:NT], run[:, src, d:NT], run[:, src, 0:NT - d], ALU.add))
                        src, d = 1 - src, 2 * d
                    ch.step(dve.tensor_tensor(place[:, :], run[:, src, :], ps_w[:, 0, :], ALU.add))

                running(1)
                ch.step(dve.tensor_reduce(n_above[:, :], ps_w[:, 2, :], AX_X, ALU.add))
                ch.step(dve.tensor_scalar(need[:, :], n_above[:, :], -1.0, float(ROUTED), ALU.mult, ALU.add))
                ch.step(dve.tensor_scalar(place[:, :], place[:, :], need[:, :], None, ALU.is_lt))
                ch.step(dve.tensor_tensor(place[:, :], place[:, :], level[:, :], ALU.mult))
                ch.step(dve.tensor_tensor(taken[:, :], place[:, :], above[:, :], ALU.add))
                dve.sem_inc(sel_ready, 1)
                running(2)
                ch.step(dve.tensor_scalar(place[:, :], place[:, :], 1.0, None, ALU.add))
                ch.step(dve.tensor_tensor(place[:, :], place[:, :], taken[:, :], ALU.mult))
                ch.step(dve.tensor_scalar(place[:, :], place[:, :], 1.0, None, ALU.subtract))
                dve.sem_inc(facts_ready, 1)
                with dve.Fori(0, NT // 2) as i:
                    for h in range(2):
                        dve.wait_ge(hot_used, i * 2)
                        dve.tensor_scalar(hot[:, h], slots[:, :], place[:, bass.ds(i * 2 + h, 1)], None, ALU.is_equal
                                          ).then_inc(hot_ready, 1)
                dve.wait_ge(found_ready, 1)
                ch.step(dve.tensor_copy(found[:, :, :], ps_f[:, :, :]))
                ch.step(dve.scalar_tensor_tensor(token_f[:, :], found[:, :, 1], float(P), found[:, :, 0], ALU.mult, ALU.add))
                dve.tensor_tensor(gains[:, :], found[:, :, 2], found[:, :, 3], ALU.add)
                dve.tensor_copy(token[:, :], token_f[:, :]).then_inc(token_ready, 1)
                for b in range(B):
                    dve.wait_ge(r_high, b + 1)
                    dve.tensor_tensor(y_rt_t[:, :, 1, b * P:(b + 1) * P], ps_r[b % 2][:, :, :],
                                      y_rt_t[:, :, 0, b * P:(b + 1) * P], ALU.subtract).then_inc(r_low, 1)
                for c in range(HC):
                    dve.wait_ge(u_act, c + 1)
                    dve.tensor_scalar(g_hl[:, c, 0, :], g32[:, c % 2], YS, None, ALU.mult).then_inc(u_high, 1)
                    dve.wait_ge(u_high, c + 1)
                    dve.scalar_tensor_tensor(g_hl[:, c, 1, :], g32[:, c % 2], YS, g_hl[:, c, 0, :], ALU.mult,
                                             ALU.subtract).then_inc(u_low, 1)
                dve.wait_ge(base_in, 16 * B)
                for b in range(B):
                    dve.wait_ge(d_full, b + 1)
                    dve.scalar_tensor_tensor(fin[:, b], ps_u[b][:, :], 1.0 / ZS, b2h_row[:, :], ALU.mult, ALU.add
                                             ).then_inc(d_read, 1)
                    dve.wait_ge(d_read, b + 1)
                    dve.scalar_tensor_tensor(fin[:, b], fin[:, b], gains[:, b:b + 1], base[:, b], ALU.mult, ALU.add
                                             ).then_inc(fin_ready, 1)

            @block.scalar
            def _(act):
                for b in range(B):
                    act.wait_ge(r_full, b + 1)
                    act.activation(y_rt_t[:, :, 0, b * P:(b + 1) * P], ps_r[b % 2][:, :, :], ACT.Copy).then_inc(r_high, 1)
                for c in range(HC):
                    act.wait_ge(u_full, c + 1)
                    if c >= 2:
                        act.wait_ge(u_low, c - 1)
                    act.activation(g32[:, c % 2], ps_u[c % 4][:, :], ACT.Gelu, bias=b1h_sb[:, c:c + 1], scale=1.0 / ZS
                                   ).then_inc(u_act, 1)

            @block.tensor
            def _(pe):
                pe.wait_ge(tri_ready, 2)
                for n, m in ((1, level), (2, taken)):
                    pe.wait_ge(sel_ready, n)
                    pe.matmul(ps_w[:, 0, :], before[:, :], m[:, :], start=True, stop=True)
                    pe.matmul(ps_w[:, 1, :], ones[:, :], m[:, :], start=True, stop=True)
                    pe.matmul(ps_w[:, 2, :], ones[:, :], above[:, :], start=True, stop=True).then_inc(prefix_ready, 1)
                pe.wait_ge(facts_ready, 1)
                pe.matmul(ps_f[:, :, :].rearrange("p b n -> p (b n)"), keep["ones16"][:, :], keep["zeros"][:, 0:4 * B],
                          start=True, stop=False, skip_group_check=True)
                with pe.Fori(0, NT // 2) as i:
                    for h in range(2):
                        pe.wait_ge(hot_ready, i * 2 + (h + 1))
                        for b in range(B):
                            last = pe.matmul(ps_f[:, b, :], hot[:, h, b * P:(b + 1) * P],
                                             facts[:, bass.ds(i * 2 + h, 1), :].rearrange("p a n -> p (a n)"),
                                             start=False, stop=False, skip_group_check=True)
                        last.then_inc(hot_used, 1)
                pe.matmul(ps_f[:, 0, 0:1], keep["ones16"][:, :], keep["zeros"][:, 0:1], start=False, stop=True,
                          skip_group_check=True).then_inc(found_ready, 1)
                for b in range(B):
                    pe.wait_ge(rows_in[b], 16)
                    if b >= 2:
                        pe.wait_ge(r_low, b - 1)
                    for k in range(KC):
                        last = pe.transpose(ps_r[b % 2][:, k, :], y_rt[:, b, k * P:(k + 1) * P], keep["ident"][:, :])
                    last.then_inc(r_full, 1)
                pe.wait_ge(r_low, B)
                pe.wait_ge(heavy_in, 16 * 2 * KC)
                for c in range(HC):
                    if c >= 4:
                        pe.wait_ge(u_act, c - 3)
                    for k in range(KC):
                        for e, f in PASSES:
                            last = pe.matmul(ps_u[c % 4][:, :], w1h_sb[:, k, e, c * P:(c + 1) * P], y_rt_t[:, k, f, :],
                                             start=(k == 0 and e + f == 0), stop=(k == KC - 1 and e == 1))
                    last.then_inc(u_full, 1)
                pe.wait_ge(u_low, HC)
                pe.wait_ge(u_act, HC)
                for b in range(B):
                    for c in range(HC):
                        for e, f in PASSES:
                            last = pe.matmul(ps_u[b][:, :], g_hl[:, c, e, b * P:(b + 1) * P], w2h_sb[:, c // 4, f, c % 4, :],
                                             start=(c == 0 and e + f == 0), stop=(c == HC - 1 and e == 1))
                    last.then_inc(d_full, 1)


_INS = ["x", "adj", "adj_t", "L0_gnn_W_q", "L0_gnn_b_q", "L0_gnn_W_k", "L0_gnn_b_k", "L0_gnn_W_v_t", "L0_gnn_b_v",
        "L0_ffn_routing_token", "L0_ffn_gamma_light", "L0_ffn_w1_light", "L0_ffn_b1_light", "L0_ffn_w2_light",
        "L0_ffn_b2_light", "L0_ffn_gamma_heavy", "L0_ffn_w1_heavy", "L0_ffn_b1_heavy", "L0_ffn_w2_heavy",
        "L0_ffn_b2_heavy"]


def build(nc, shapes):
    args = [nc.dram_tensor(f"in_{n}", tuple(shapes[n]), F32, kind="ExternalInput").ap() for n in _INS]
    args.append(nc.dram_tensor("out_0", (N, D), F32, kind="ExternalOutput").ap())
    gnn_ffn_kernel(nc, *args)


def kernel(**inputs):
    import concourse.bacc as _bacc
    from concourse.bass_utils import run_bass_kernel_spmd as _run

    inputs = {k: np.asarray(v) for k, v in inputs.items()}
    inputs["adj_t"] = inputs["adj"].T
    inputs["L0_gnn_W_v_t"] = inputs["L0_gnn_W_v"].T
    arrays = {f"in_{n}": np.ascontiguousarray(inputs[n]) for n in _INS}
    nc = _bacc.Bacc("TRN2", target_bir_lowering=False, num_devices=1)
    build(nc, {n: inputs[n].shape for n in _INS})
    r = _run(nc, [arrays], core_ids=[0])
    return r.results[0]["out_0"]
```

```python
from contextlib import ExitStack

import numpy as np

import concourse.bass as bass
from concourse import mybir

ALU = mybir.AluOpType
ACT = mybir.ActivationFunctionType
AX_X = mybir.AxisListType.X
F32 = mybir.dt.float32
F16 = mybir.dt.float16
I32 = mybir.dt.int32
U32 = mybir.dt.uint32

P = 128
N = 4096
D = 512
HL = 256
HH = 2048
ROUTED = 512
NT = N // P
KC = D // P
GROUP = 4
NG = NT // GROUP
YS = 64.0
MS = 1024.0
ZS = YS * YS
SCALE = 1.0 / (ZS * float(np.sqrt(D)))
MASKED = -10000.0 / SCALE
PS = 4096.0
EPS_LN = 1e-5


class Chain:

    def __init__(self, eng, sem):
        self.eng, self.sem, self.n, self.base = eng, sem, 0, 0

    def step(self, ins):
        self.n += 1
        ins.then_inc(self.sem, 1)
        self.eng.wait_ge(self.sem, self.base + self.n)


class Semaphores:

    def __init__(self, nc):
        self.nc, self.held = nc, []

    def __call__(self, name):
        self.held.append(self.nc.alloc_semaphore(name=name))
        return self.held[-1]

    def done(self):
        self.nc.all_engine_barrier()
        self.nc.clear_and_free_semaphores([h for h in self.held])
        self.nc.all_engine_barrier()
        self.held = []


def gnn_ffn_kernel(nc, x, adj, adj_t, wq, bq, wk, bk, wv_t, bv, rtok, gl, w1l, b1l, w2l, b2l,
                   gh, w1h, b1h, w2h, b2h, out):
    ytab = nc.dram_tensor("ytab", (N, 2 * D), F16).ap()
    qtab = nc.dram_tensor("qtab", (NT, P, KC * 2 * P), F16).ap()
    x1tab = nc.dram_tensor("x1tab", (N, D), F32).ap()
    y2rows = nc.dram_tensor("y2rows", (N, D), F32).ap()
    y2ttab = nc.dram_tensor("y2ttab", (NT, P, KC * 2 * P), F16).ap()
    with ExitStack() as ctx:
        def sb(name, shape, dt, c=ctx):
            return c.enter_context(nc.sbuf_tensor(name, shape, dt))

        keep = {
            "cs": sb("cs", [P, NT], F32), "bvb": sb("bvb", [P, D], F32),
            "wv": sb("wv", [P, KC, 2, D], F16), "ident": sb("ident", [P, P], F32),
            "zeros": sb("zeros", [P, D], F16), "ident16": sb("ident16", [P, P], F16), "s": sb("s", [P, NT], F32),
            "index": sb("index", [P, NT, 2, CH], I32),
            "overflow": sb("overflow", [P, 1], I32), "nz": sb("nz", [P, NT, NT], F32), "ytot": sb("ytot", [P, D], F32), "ones16": sb("ones16", [P, P], F16),
            "ramp": sb("ramp", [P, SEG // P], I32), "part": sb("part", [P, 1], I32), "tile_no": sb("tile_no", [P, NT], I32),
            "place_i": sb("place_i", [P, SEG], I32), "ones": sb("ones_f", [P, P], F32),
            "w1l": sb("w1l_hl", [P, 2, KC, HL], F16), "w2l": sb("w2l_hl", [P, 2, HL // P, D], F16),
            "b1l": sb("b1l_sb", [P, HL // P], F32), "b1h": sb("b1h_sb", [P, HH // P], F32),
            "b2l": sb("b2l_row", [P, D], F32), "b2h": sb("b2h_row", [P, D], F32), "gain_h": sb("gain_h", [P, KC], F32),
        }
        sem = Semaphores(nc)
        q_out = split_weights(nc, keep, wk=wk, wq=wq, bq=bq, bk=bk, wv_t=wv_t, bv=bv, gl=gl, w1l=w1l, w2l=w2l,
                      gh=gh, b1l=b1l, b2l=b2l, b1h=b1h, b2h=b2h, sem=sem, x=x, ytab=ytab, qtab=qtab, adj_t=adj_t)
        list_neighbours(nc, keep, q_out, sem)
        sem.done()
        overflow = nc.values_load(keep["overflow"][0:1, 0:1], min_val=0, max_val=P)
        with nc.If(overflow == 0):
            attend_listed(nc, keep, x, adj_t, rtok, ytab, qtab, x1tab, y2rows, y2ttab, sem)
        sem.done()
        with nc.If(overflow > 0):
            attend_all(nc, keep, x, adj, rtok, ytab, qtab, x1tab, y2rows, y2ttab, sem)
        sem.done()
        feed_forward(nc, keep, y2ttab, x1tab, y2rows, w1h, w2h, out, sem)


def split_weights(nc, keep, wk, wq, bq, bk, wv_t, bv, gl, w1l, w2l, gh, b1l, b2l, b1h, b2h, sem, x, ytab, qtab, adj_t):
    with ExitStack() as ctx:
        def sb(name, shape, dt):
            return ctx.enter_context(nc.sbuf_tensor(name, shape, dt))

        def pb(name, shape, dt):
            return ctx.enter_context(nc.psum_tensor(name, shape, dt))

        xg = sb("xg", [P, 2, GROUP, D], F32)
        adj_sb = sb("adj_sb", [P, GROUP, N], F32)
        q_out = [sem("q_out0"), sem("q_out1")]
        x_in, adj_in = [sem("x_in0"), sem("x_in1")], [sem(f"adj_in{s}") for s in range(GROUP)]
        m_hl = sb("m_hl", [P, KC, 2, D], F16)
        u_hl = sb("u_hl", [P, KC, 2], F16)
        w64 = sb("w64", [P, KC], F32)
        c0 = sb("c0", [P, 1], F32)
        zeros = keep["zeros"]

        loaded_v, loaded_b = sem("loaded_v"), sem("loaded_b")
        loaded_qk, consts = sem("loaded_qk"), sem("consts")
        light_in, light_scaled, light_high = sem("light_in"), sem("light_scaled"), sem("light_high")
        bq_ready, m_ready, m_copied, vec_ready, dve0 = sem("bq_ready"), sem("m_ready"), sem("m_copied"), sem("vec_ready"), sem("dve0")
        m_done = sem("m_done")
        pool0, wv_scaled, wv_high = sem("pool0"), sem("wv_scaled"), sem("wv_high")

        with ExitStack() as pctx:
            def tmp(name, shape, dt):
                return pctx.enter_context(nc.sbuf_tensor(name, shape, dt))

            wq_sb, wk_sb = tmp("wq_sb", [P, KC, D], F32), tmp("wk_sb", [P, KC, D], F32)
            wv_sb = tmp("wv_sb", [P, KC, D], F32)
            bq_sb, bk_sb = tmp("bq_sb", [P, KC], F32), tmp("bk_sb", [P, KC], F32)
            bq_wide = tmp("bq_wide", [P, KC, P], F32)
            gl_sb, gh_sb = tmp("gl_sb", [P, KC], F32), tmp("gh_sb", [P, KC], F32)
            gain_l = tmp("gain_l", [P, KC], F32)
            w1l_raw, w2l_raw = tmp("w1l_raw", [P, KC, HL], F32), tmp("w2l_raw", [P, HL // P, D], F32)
            m32 = tmp("m32", [P, 2, D], F32)
            u32 = tmp("u32", [P, KC], F32)
            ps_m = [pctx.enter_context(nc.psum_tensor(f"ps_m{i}", [P, D], F32)) for i in range(2)]
            ps_v = pctx.enter_context(nc.psum_tensor("ps_v", [P, 16], F32))
            with nc.Block() as block:
                @block.sync
                def _(sp):
                    sp.dma_start(wq_sb[:, :, :], wq.rearrange("(c p) k -> p c k", p=P)).then_inc(loaded_qk, 16)
                    sp.dma_start(wk_sb[:, :, :], wk.rearrange("(c p) k -> p c k", p=P)).then_inc(loaded_qk, 16)
                    for t, s in ((bq_sb, bq), (bk_sb, bk), (gl_sb, gl), (gh_sb, gh)):
                        sp.dma_start(t[:, :], s.rearrange("(c p) -> p c", p=P),
                                     allow_slow_non_contiguous=True).then_inc(loaded_b, 16)
                    sp.dma_start(wv_sb[:, :, :], wv_t.rearrange("(c p) k -> p c k", p=P)).then_inc(loaded_v, 16)
                    sp.dma_start(keep["bvb"][:, :], bv.partition_broadcast(P)).then_inc(loaded_v, 16)
                    for t, s in ((keep["b1l"], b1l), (keep["b1h"], b1h)):
                        sp.dma_start(t[:, :], s.rearrange("(c p) -> p c", p=P),
                                     allow_slow_non_contiguous=True).then_inc(loaded_v, 16)
                    for t, s in ((keep["b2l"], b2l), (keep["b2h"], b2h)):
                        sp.dma_start(t[:, :], s.partition_broadcast(P)).then_inc(loaded_v, 16)
                    sp.dma_start(w1l_raw[:, :, :], w1l.rearrange("(c p) n -> p c n", p=P)).then_inc(light_in, 16)
                    sp.dma_start(w2l_raw[:, :, :], w2l.rearrange("(c p) n -> p c n", p=P)).then_inc(light_in, 16)
                    for g in range(2):
                        sp.dma_start(xg[:, g], x[g * GROUP * P:(g + 1) * GROUP * P, :].rearrange("(s p) d -> p s d", p=P)
                                     ).then_inc(x_in[g], 16)
                    for s in range(GROUP):
                        sp.dma_start(adj_sb[:, s], adj_t[s * P:(s + 1) * P, :]).then_inc(adj_in[s], 16)

                @block.gpsimd
                def _(pool):
                    ch = Chain(pool, pool0)
                    ch.step(pool.memset(keep["ident"][:, :], 0.0))
                    pool.affine_select(out=keep["ident"][:, :], in_=keep["ident"][:, :], compare_op=ALU.not_equal,
                                       fill=1.0, base=0, pattern=[[-1, P]], channel_multiplier=1).then_inc(consts, 1)
                    pool.wait_ge(consts, 1)
                    pool.tensor_copy(keep["ident16"][:, :], keep["ident"][:, :])
                    pool.memset(keep["ones16"][:, :], 1.0).then_inc(consts, 1)
                    pool.memset(zeros[:, :], 0.0).then_inc(consts, 1)
                    pool.iota(keep["ramp"][:, :], pattern=[[P, SEG // P]], base=0, channel_multiplier=0).then_inc(consts, 1)
                    pool.iota(keep["part"][:, :], pattern=[[0, 1]], base=0, channel_multiplier=1).then_inc(consts, 1)
                    pool.iota(keep["tile_no"][:, :], pattern=[[1, NT]], base=0, channel_multiplier=0).then_inc(consts, 1)
                    pool.iota(keep["place_i"][:, :], pattern=[[-1, SEG]], base=SEG, channel_multiplier=0).then_inc(consts, 1)
                    pool.memset(keep["ones"][:, :], 1.0).then_inc(consts, 1)

                @block.vector
                def _(dve):
                    ch = Chain(dve, dve0)
                    dve.wait_ge(loaded_b, 64)
                    dve.tensor_copy(bq_wide[:, :, :], bq_sb[:, :].unsqueeze(2).broadcast_to([P, KC, P])).then_inc(bq_ready, 1)
                    dve.tensor_scalar(keep["gain_h"][:, :], gh_sb[:, :], YS, None, ALU.mult)
                    ch.step(dve.tensor_scalar(gain_l[:, :], gl_sb[:, :], YS, None, ALU.mult))
                    dve.wait_ge(loaded_v, 96)
                    dve.tensor_scalar(wv_sb[:, :, :], wv_sb[:, :, :], YS, None, ALU.mult).then_inc(wv_scaled, 1)
                    dve.wait_ge(light_in, 32)
                    for kc in range(KC):
                        dve.tensor_scalar(w1l_raw[:, kc, :], w1l_raw[:, kc, :], gain_l[:, kc:kc + 1], None, ALU.mult)
                    dve.tensor_scalar(w2l_raw[:, :, :], w2l_raw[:, :, :], YS, None, ALU.mult).then_inc(light_scaled, 1)
                    dve.wait_ge(wv_high, 1)
                    dve.tensor_tensor(keep["wv"][:, :, 1, :], wv_sb[:, :, :], keep["wv"][:, :, 0, :], ALU.subtract)
                    dve.wait_ge(light_high, 2)
                    dve.tensor_tensor(keep["w1l"][:, 1], w1l_raw[:, :, :], keep["w1l"][:, 0], ALU.subtract)
                    dve.tensor_tensor(keep["w2l"][:, 1], w2l_raw[:, :, :], keep["w2l"][:, 0], ALU.subtract)
                    for kc in range(KC):
                        dve.wait_ge(m_copied, 2 * kc + 2)
                        dve.tensor_tensor(m_hl[:, kc, 1, :], m32[:, kc % 2, :], m_hl[:, kc, 0, :],
                                          ALU.subtract).then_inc(m_ready, 1)
                    dve.wait_ge(vec_ready, 1)
                    dve.tensor_scalar(w64[:, :], ps_v[:, 4:8], YS, None, ALU.mult)
                    dve.tensor_scalar(c0[:, :], ps_v[:, 8:9], ZS, None, ALU.mult)
                    ch.step(dve.tensor_scalar(u32[:, :], ps_v[:, 0:4], MS, None, ALU.mult))
                    ch.step(dve.tensor_copy(u_hl[:, :, 0], u32[:, :]))
                    ch.step(dve.tensor_tensor(u_hl[:, :, 1], u32[:, :], u_hl[:, :, 0], ALU.subtract))

                @block.scalar
                def _(act):
                    act.wait_ge(wv_scaled, 1)
                    act.activation(keep["wv"][:, :, 0, :], wv_sb[:, :, :], ACT.Copy).then_inc(wv_high, 1)
                    act.wait_ge(light_scaled, 1)
                    act.activation(keep["w1l"][:, 0], w1l_raw[:, :, :], ACT.Copy).then_inc(light_high, 1)
                    act.activation(keep["w2l"][:, 0], w2l_raw[:, :, :], ACT.Copy).then_inc(light_high, 1)
                    for kc in range(KC):
                        act.wait_ge(m_done, kc + 1)
                        if kc >= 2:
                            act.wait_ge(m_ready, kc - 1)
                        act.activation(m32[:, kc % 2, :], ps_m[kc % 2][:, :], ACT.Copy, scale=MS).then_inc(m_copied, 1)
                        act.wait_ge(m_copied, 2 * kc + 1)
                        act.activation(m_hl[:, kc, 0, :], m32[:, kc % 2, :], ACT.Copy).then_inc(m_copied, 1)

                @block.tensor
                def _(pe):
                    pe.wait_ge(loaded_qk, 32)
                    for kc in range(KC):
                        if kc >= 2:
                            pe.wait_ge(m_copied, 2 * (kc - 1))
                        for d in range(KC):
                            last = pe.matmul(ps_m[kc % 2][:, :], wq_sb[:, d, kc * P:(kc + 1) * P], wk_sb[:, d, :],
                                             start=(d == 0), stop=(d == KC - 1))
                        last.then_inc(m_done, 1)
                    pe.wait_ge(loaded_b, 64)
                    pe.wait_ge(bq_ready, 1)
                    for kc in range(KC):
                        for d in range(KC):
                            pe.matmul(ps_v[:, kc:kc + 1], wq_sb[:, d, kc * P:(kc + 1) * P], bk_sb[:, d:d + 1],
                                      start=(d == 0), stop=(d == KC - 1))
                        for d in range(KC):
                            pe.matmul(ps_v[:, 4 + kc:5 + kc], wk_sb[:, d, kc * P:(kc + 1) * P], bq_sb[:, d:d + 1],
                                      start=(d == 0), stop=(d == KC - 1))
                    for d in range(KC):
                        last = pe.matmul(ps_v[:, 8:9], bq_wide[:, d, :], bk_sb[:, d:d + 1], start=(d == 0), stop=(d == KC - 1))
                    last.then_inc(vec_ready, 1)
        project_queries(nc, keep, m_hl, u_hl, w64, c0, zeros, x, xg, x_in, ytab, qtab, adj_t, adj_sb, adj_in, q_out, sem)
        return q_out


def project_queries(nc, keep, m_hl, u_hl, w64, c0, zeros, x, xg, x_in, ytab, qtab, adj_t, adj_sb, adj_in, q_out, sem):
    x_groups = x.rearrange("(g s p) d -> g p s d", s=GROUP, p=P)
    ytab_g = ytab.rearrange("(g s p) d -> g p s d", s=GROUP, p=P)
    qtab_g = qtab.rearrange("(g s) p n -> g p s n", s=GROUP)
    with ExitStack() as ctx:
        def sb(name, shape, dt):
            return ctx.enter_context(nc.sbuf_tensor(name, shape, dt))

        stats = sb("stats", [P, 2, GROUP, 6], F32)
        mv = sb("mv", [P, 2, GROUP, 2], F32)
        half_pow = sb("half_pow", [P, 1], F32)
        var_eps = sb("var_eps", [P, 2, GROUP], F32)
        rstd = sb("rstd", [P, 2, GROUP], F32)
        y32 = sb("y32", [P, 2, GROUP, D], F32)
        y_rows = sb("y_rows", [P, 2, GROUP, 2, D], F16)
        y_t = sb("y_t", [P, 2, KC, 2, GROUP * P], F16)
        q32 = sb("q32", [P, 2, D], F32)
        q_hl = sb("q_hl", [P, 2, GROUP, KC, 2, P], F16)
        ps_t = [ctx.enter_context(nc.psum_tensor(f"ps_t{i}", [P, KC, P], F32)) for i in range(2)]
        ps_q = [ctx.enter_context(nc.psum_tensor(f"ps_q{i}", [P, GROUP * P], F32)) for i in range(2)]
        ps_c = [ctx.enter_context(nc.psum_tensor(f"ps_c{i}", [P, GROUP, 2], F32)) for i in range(2)]
        ps_y = ctx.enter_context(nc.psum_tensor("ps_y", [P, D], F32))

        c_part = sb("c_part", [P, 2, GROUP], F32)
        adj_t_tiles = adj_t.rearrange("(c p) i -> c p i", p=P)

        passed, passed_dve, passed_act = sem("passed"), sem("passed_dve"), sem("passed_act")
        xg_used, scanned, rows_free, y32_free = sem("xg_used"), sem("scanned"), sem("rows_free"), sem("y32_free")
        yt_free, rows_high, q_high = sem("yt_free"), sem("rows_high"), sem("q_high")
        pow_ready = sem("pow_ready")
        dve1, pool1 = sem("dve1"), sem("pool1")
        var_ready, rstd_ready, y_ready, rows_ready = sem("var_ready"), sem("rstd_ready"), sem("y_ready"), sem("rows_ready")
        rows_out = [sem("rows_out0"), sem("rows_out1")]
        t_ready, t_high, t_low = sem("t_ready"), sem("t_high"), sem("t_low")
        q_ready, q_biased, q_split = sem("q_ready"), sem("q_biased"), sem("q_split")
        c_ready, c_read, total_ready = sem("c_ready"), sem("c_read"), sem("total_ready")
        summed = sem("summed")
        HALVES = NG // 2

        with nc.Block() as block:
            @block.sync
            def _(sp):
                def load_x(g):
                    sp.wait_ge(xg_used, g - 1)
                    sp.dma_start(xg[:, h], x_groups[bass.ds(g, 1)].rearrange("a p s d -> p (a s) d")).then_inc(x_in[h], 16)

                def load_adjacency(g):
                    for s in range(GROUP):
                        sp.wait_ge(scanned, g * GROUP - GROUP + (s + 1))
                        sp.dma_start(adj_sb[:, s], adj_t_tiles[bass.ds(g * GROUP + s, 1)].rearrange("a p i -> p (a i)")
                                     ).then_inc(adj_in[s], 16)

                with sp.Fori(0, HALVES - 1) as i:
                    for h in range(2):
                        load_x(i * 2 + (2 + h))
                        load_adjacency(i * 2 + (1 + h))
                load_adjacency(NG - 1)
                sp.sem_inc(x_in[0], 16)
                sp.wait_ge(rows_out[0], 16 * HALVES + 16)
                sp.wait_ge(rows_out[1], 16 * HALVES + 16)

            @block.gpsimd
            def _(pool):
                pool.memset(half_pow[:, :], -0.5).then_inc(pow_ready, 1)
                pool.wait_ge(pow_ready, 1)
                def power(g, h):
                    pool.wait_ge(var_ready, g + 1)
                    pool.tensor_tensor(rstd[:, h], var_eps[:, h], half_pow[:, :].broadcast_to([P, GROUP]),
                                       ALU.pow).then_inc(rstd_ready, 1)

                power(0, 0)
                with pool.Fori(0, HALVES) as i:
                    for h in range(2):
                        g = i * 2 + h
                        pool.wait_ge(rows_high, g + 1)
                        pool.tensor_tensor(y_rows[:, h, :, 1, :], y32[:, h], y_rows[:, h, :, 0, :],
                                           ALU.subtract).then_inc(rows_ready, 1)
                        pool.wait_ge(rows_ready, g + 1)
                        pool.sem_inc(y32_free, 1)
                        power(g + 1, 1 - h)
                        for k in range(KC):
                            pool.wait_ge(q_high, g * KC + (k + 1))
                            pool.tensor_tensor(q_hl[:, h, :, k, 1, :], q32[:, k % 2].rearrange("p (s t) -> p s t", s=GROUP),
                                               q_hl[:, h, :, k, 0, :], ALU.subtract).then_inc(q_split, 1)

            @block.vector
            def _(dve):
                ch = Chain(dve, dve1)
                dve.sem_inc(y32_free, 2)
                def scan(g, s):
                    dve.wait_ge(adj_in[s], g * 16 + 16)
                    dve.tensor_reduce(keep["nz"][:, bass.ds(g * GROUP + s, 1), :].rearrange("p a t -> p (a t)"),
                                      adj_sb[:, s].rearrange("p (t i) -> p t i", i=P), AX_X, ALU.max,
                                      apply_absolute_value=True).then_inc(scanned, 1)

                def statistics(g, h):
                    dve.wait_ge(x_in[h], g // 2 * 16 + 16 if isinstance(g, int) else g * 8 + (16 - 8 * h))
                    for s in range(GROUP):
                        last = dve.bn_stats(stats[:, h, s], xg[:, h, s])
                    ch.step(last)
                    dve.sem_inc(passed_dve, 1)
                    for s in range(GROUP):
                        last = dve.bn_aggr(mv[:, h, s], stats[:, h, s])
                    ch.step(last)
                    dve.tensor_scalar(var_eps[:, h], mv[:, h, :, 1], EPS_LN, 1.0 / (YS * YS), ALU.add,
                                      ALU.mult).then_inc(var_ready, 1)

                statistics(0, 0)
                with dve.Fori(0, HALVES) as i:
                    for h in range(2):
                        g = i * 2 + h
                        ch.base, ch.n = i * (2 * 3) + 2, 3 * h
                        dve.wait_ge(rstd_ready, g + 1)
                        dve.wait_ge(y32_free, g + 1)
                        for s in range(GROUP):
                            last = dve.tensor_scalar(y32[:, h, s], xg[:, h, s], mv[:, h, s, 0:1], rstd[:, h, s:s + 1],
                                                     ALU.subtract, ALU.mult)
                            last.then_inc(y_ready, 1)
                        dve.wait_ge(y_ready, g * GROUP + GROUP)
                        dve.sem_inc(xg_used, 1)
                        scan(g, 0)
                        statistics(g + 1, 1 - h)
                        for s in range(GROUP):
                            if s % 2 == 0:
                                scan(g, 1 + s // 2)
                            dve.wait_ge(t_high, g * GROUP + (s + 1))
                            dve.tensor_tensor(y_t[:, h, :, 1, s * P:(s + 1) * P], ps_t[s % 2][:, :, :],
                                              y_t[:, h, :, 0, s * P:(s + 1) * P], ALU.subtract).then_inc(t_low, 1)
                        scan(g, 3)
                        dve.wait_ge(c_ready, g + 1)
                        ch.step(dve.tensor_scalar(c_part[:, h], ps_c[h][:, :, 0], ZS / (YS * MS), c0[:, 0:1], ALU.mult, ALU.add))
                        dve.scalar_tensor_tensor(keep["cs"][:, bass.ds(g * GROUP, GROUP)], ps_c[h][:, :, 1], ZS / (YS * MS),
                                                 c_part[:, h], ALU.mult, ALU.add).then_inc(c_read, 1)
                dve.wait_ge(summed, 1)
                dve.tensor_copy(keep["ytot"][:, :], ps_y[:, :])

            @block.scalar
            def _(act):
                act.sem_inc(rows_free, 2)
                for h in range(2):
                    act.sem_inc(q_out[h], 16)
                    act.sem_inc(rows_out[h], 16)
                with act.Fori(0, HALVES) as i:
                    for h in range(2):
                        g = i * 2 + h
                        act.wait_ge(rows_free, g + 1)
                        act.wait_ge(rows_out[h], i * 16 + 16)
                        act.wait_ge(y_ready, g * GROUP + GROUP)
                        act.activation(y_rows[:, h, :, 0, :], y32[:, h], ACT.Copy).then_inc(rows_high, 1)
                        for s in range(GROUP):
                            act.wait_ge(t_ready, g * GROUP + (s + 1))
                            act.activation(y_t[:, h, :, 0, s * P:(s + 1) * P], ps_t[s % 2][:, :, :], ACT.Copy).then_inc(t_high, 1)
                        act.wait_ge(rows_ready, g + 1)
                        act.sem_inc(passed_act, 1)
                        act.dma_start(ytab_g[bass.ds(g, 1)].rearrange("a p s d -> p (a s) d"),
                                      y_rows[:, h].rearrange("p s e d -> p s (e d)")).then_inc(rows_out[h], 16)
                        act.wait_ge(q_out[h], i * 16 + 16)
                        for k in range(KC):
                            act.wait_ge(q_ready, g * KC + (k + 1))
                            if k >= 2:
                                act.wait_ge(q_split, g * KC + (k - 1))
                            act.activation(q32[:, k % 2], ps_q[k % 2][:, :], ACT.Identity, bias=w64[:, k:k + 1],
                                           scale=1.0 / MS).then_inc(q_biased, 1)
                            act.wait_ge(q_biased, g * KC + (k + 1))
                            act.activation(q_hl[:, h, :, k, 0, :], q32[:, k % 2].rearrange("p (s t) -> p s t", s=GROUP),
                                           ACT.Copy).then_inc(q_high, 1)
                        act.wait_ge(q_split, g * KC + KC)
                        act.sem_inc(passed_act, 1)
                        act.dma_start(qtab_g[bass.ds(g, 1)].rearrange("a p s n -> p (a s) n"),
                                      q_hl[:, h].rearrange("p s k e t -> p s (k e t)")).then_inc(q_out[h], 16)

            @block.tensor
            def _(pe):
                pe.matmul(ps_y[:, :], keep["ones16"][:, :], zeros[:, :], start=True, stop=False, skip_group_check=True)
                with pe.Fori(0, HALVES) as i:
                    for h in range(2):
                        g = i * 2 + h
                        for s in range(GROUP):
                            pe.wait_ge(y_ready, g * GROUP + (s + 1))
                            if s >= 2:
                                pe.wait_ge(t_low, g * GROUP + (s - 1))
                            for k in range(KC):
                                last = pe.transpose(ps_t[s % 2][:, k, :], y32[:, h, s, k * P:(k + 1) * P], keep["ident"][:, :])
                            last.then_inc(t_ready, 1)
                        pe.wait_ge(t_low, g * GROUP + GROUP)
                        for s in range(GROUP):
                            for k in range(KC):
                                pe.matmul(ps_c[h][:, s, :], y_t[:, h, k, 0, s * P:(s + 1) * P], u_hl[:, k, :],
                                          start=(k == 0), stop=False, skip_group_check=True)
                                last = pe.matmul(ps_c[h][:, s, 0:1], y_t[:, h, k, 1, s * P:(s + 1) * P], u_hl[:, k, 0:1],
                                                 start=False, stop=(k == KC - 1), skip_group_check=True)
                        last.then_inc(c_ready, 1)
                        pe.wait_ge(rows_ready, g + 1)
                        for s in range(GROUP):
                            for e in range(2):
                                last = pe.matmul(ps_y[:, :], keep["ones16"][:, :], y_rows[:, h, s, e, :], start=False,
                                                 stop=False, skip_group_check=True)
                        last.then_inc(rows_free, 1)
                        for k in range(KC):
                            if k >= 2:
                                pe.wait_ge(q_biased, g * KC + (k - 1))
                            for c in range(KC):
                                for a, b in ((0, 0), (0, 1), (1, 0)):
                                    last = pe.matmul(ps_q[k % 2][:, :], m_hl[:, c, a, k * P:(k + 1) * P], y_t[:, h, c, b, :],
                                                     start=(c == 0 and a == 0 and b == 0), stop=(c == KC - 1 and a == 1))
                            last.then_inc(q_ready, 1)
                        pe.wait_ge(q_biased, g * KC + KC)
                        pe.wait_ge(c_read, g + 1)
                pe.matmul(ps_y[0:P, 0:1], keep["ones16"][:, :], zeros[:, 0:1], start=False, stop=True, skip_group_check=True).then_inc(summed, 1)


SEGS = 4
SEG = N // SEGS
SLOTS = 160
CH = SEGS * SLOTS // P
LISTED = CH * P
RING = 4


EVEN = 1024


def window(rank):
    p = 1.0 - (1.0 - 1.0 / EVEN) ** P
    spread = 5.0 * np.sqrt(1.0 - p) / p
    lo, hi = rank / p - spread * np.sqrt(rank), (rank + 8) / p + spread * np.sqrt(rank + 8)
    return max(0, int(lo)), min(SEG, int(hi) + 1)


def list_neighbours(nc, keep, q_out, sem):
    with ExitStack() as ctx:
        def sb(name, shape, dt):
            return ctx.enter_context(nc.sbuf_tensor(name, shape, dt))

        ramp, part, tile_no, place_i, ones = (keep[n] for n in ("ramp", "part", "tile_no", "place_i", "ones"))
        ramp_f = sb("ramp_f", [P, SEG // P], F32)
        part_f = sb("part_f", [P, 1], F32)
        has = sb("has", [P, SEG // P, SEGS, NT], F32)
        local = sb("local", [P, SEG // P], F32)
        keys = sb("keys", [P, SEG], F32)
        place_f = sb("place_f", [P, SEG], F32)
        unlisted, free = sb("unlisted", [P, SEG], F32), sb("free", [P, 8], F32)
        pad = sb("pad", [P, SLOTS], F32)
        listed = sb("listed", [P, SLOTS], F32)
        turned = sb("turned", [P, SLOTS], F32)
        left = sb("left", [P, 8], F32)
        seg_base = sb("seg_base", [P, 1], F32)
        tile_f = sb("tile_f", [P, NT], F32)
        seg_i = sb("seg_i", [P, 1], I32)
        source = sb("source", [P, CH, NT], F32)
        row = sb("row", [P, CH, NT], F32)
        over = sb("over", [P, 1], F32)
        total = sb("total", [P, 1], F32)
        ps = [ctx.enter_context(nc.psum_tensor(f"ps_keys{i}", [P, 4, P], F32)) for i in range(2)]
        ps_over = ctx.enter_context(nc.psum_tensor("ps_over", [P, 1], F32))

        dve2, key_ready, key_turned, over_ready, over_sum = (sem("dve2"), sem("key_ready"),
                                                                    sem("key_turned"), sem("over_ready"), sem("over_sum"))
        with nc.Block() as block:
            @block.sync
            def _(sp):
                for h in range(2):
                    sp.wait_ge(q_out[h], 16 * (NG // 2 + 1))

            @block.vector
            def _(dve):
                ch = Chain(dve, dve2)
                dve.tensor_copy(part_f[:, :], part[:, :])
                dve.tensor_copy(tile_f[:, :], tile_no[:, :])
                dve.tensor_scalar(seg_i[:, :], part[:, :], 5, None, ALU.logical_shift_right)
                ch.step(dve.tensor_copy(ramp_f[:, :], ramp[:, :]))
                ch.step(dve.tensor_scalar(local[:, :], ramp_f[:, :], part_f[:, 0:1], -1.0, ALU.add, ALU.mult))
                ch.step(dve.tensor_copy(seg_base[:, :], seg_i[:, :]))
                ch.step(dve.tensor_scalar(seg_base[:, :], seg_base[:, :], 1.0, float(SEG), ALU.add, ALU.mult))
                ch.step(dve.tensor_scalar(local[:, :], local[:, :], float(SEG), None, ALU.add))
                for r in range(SEG // P):
                    last = dve.tensor_scalar(has[:, r], keep["nz"][:, r::SEG // P, :], 0.0, local[:, r:r + 1], ALU.not_equal, ALU.mult)
                last.then_inc(key_ready, 1)
                dve.tensor_copy(place_f[:, :], place_i[:, :])
                for b in range(2):
                    dve.wait_ge(key_turned, b + 1)
                    last = dve.tensor_copy(keys[:, b * 512:(b + 1) * 512], ps[b][:, :, :].rearrange("p a j -> p (a j)"))
                ch.step(last)
                ch.step(dve.scalar_tensor_tensor(unlisted[:, :], keys[:, :], 0.0, place_f[:, :], ALU.is_equal, ALU.mult))
                ch.step(dve.max(free[:, :], unlisted[:, :]))
                for n in range(SLOTS // 8):
                    lo, hi = window(8 * n)
                    ch.step(dve.max(listed[:, 8 * n:8 * n + 8], keys[:, lo:hi]))
                    ch.step(dve.match_replace(keys[:, lo:hi], listed[:, 8 * n:8 * n + 8], keys[:, lo:hi], 0.0))
                ch.step(dve.max(left[:, :], keys[:, :]))
                dve.tensor_scalar(over[:, :], left[:, 0:1], 0.0, None, ALU.is_gt).then_inc(over_ready, 1)
                ch.step(dve.tensor_scalar(pad[:, :], listed[:, :], 0.0, free[:, 0:1], ALU.is_equal, ALU.mult))
                ch.step(dve.tensor_tensor(listed[:, :], listed[:, :], pad[:, :], ALU.add))
                ch.step(dve.transpose(turned[:, :], listed[:, :]))
                tv = turned[:, :].rearrange("p (c t) -> p c t", c=CH)
                ch.step(dve.tensor_scalar(source[:, :, :], tv, seg_base[:, 0:1], -1.0, ALU.subtract, ALU.mult))
                dve.tensor_copy(keep["index"][:, :, 0, :].rearrange("p t c -> p c t"), source[:, :, :])
                ch.step(dve.tensor_scalar(row[:, :, :], source[:, :, :], float(NT), None, ALU.mult))
                ch.step(dve.tensor_tensor(row[:, :, :], row[:, :, :], tile_f[:, :].unsqueeze(1).broadcast_to([P, CH, NT]), ALU.add))
                dve.tensor_copy(keep["index"][:, :, 1, :].rearrange("p t c -> p c t"), row[:, :, :])
                dve.wait_ge(over_sum, 1)
                ch.step(dve.tensor_copy(keep["overflow"][:, :], ps_over[:, :]))

            @block.tensor
            def _(pe):
                pe.wait_ge(key_ready, 1)
                for r in range(SEG // P):
                    last = pe.transpose(ps[r // 4][:, r % 4, :], has[:, r].rearrange("p s t -> p (s t)"), keep["ident"][:, :])
                    if r % 4 == 3:
                        last.then_inc(key_turned, 1)
                pe.wait_ge(over_ready, 1)
                pe.matmul(ps_over[:, :], ones[:, :], over[:, :], start=True, stop=True).then_inc(over_sum, 1)


class Tile:

    def __init__(self, turn, k):
        self.t = turn * RING + k
        self.ring, self.par = k % RING, k % 2
        self.turn, self.pair = turn + k // RING, turn * (RING // 2) + k // 2


def wait(eng, sem, value):
    if not isinstance(value, int) or value > 0:
        eng.wait_ge(sem, value)


def pipeline(eng, stages):
    def step(turn, n):
        for stage, lag in stages:
            k = n + lag
            if turn is None and not 0 <= k < NT:
                continue
            stage(Tile(0 if turn is None else turn, k))

    first, turns = 5, (NT - 8) // RING
    for n in range(-2, first):
        step(None, n)
    with eng.Fori(0, turns) as turn:
        for u in range(RING):
            step(turn, first + u)
    for n in range(first + turns * RING, NT + 3):
        step(None, n)


class StageChain:

    def __init__(self, eng, sem, count):
        self.eng, self.sem, self.count = eng, sem, count

    def begin(self, tile):
        self.base, self.n = tile.t * self.count, 0

    def step(self, ins):
        self.n += 1
        ins.then_inc(self.sem, 1)
        self.eng.wait_ge(self.sem, self.base + self.n)

    def end(self):
        assert self.n == self.count, (self.n, self.count)


PASSES = ((0, 0), (0, 1), (1, 0))
A0 = 3
ACT_TURNS, DVE_TURNS = (0, 2, 4), (1, 3)
BANKS = ((0, A0), (A0, CH))


def attend_listed(nc, keep, x, adj_t, rtok, ytab, qtab, x1tab, y2rows, y2ttab, sem):
    adj_rows = adj_t.rearrange("j (t i) -> (j t) i", i=P)
    x_tiles = x.rearrange("(t p) d -> t p d", p=P)
    x1_tiles = x1tab.rearrange("(t p) d -> t p d", p=P)
    y2_tiles = y2rows.rearrange("(t p) d -> t p d", p=P)
    with ExitStack() as ctx:
        def sb(name, shape, dt):
            return ctx.enter_context(nc.sbuf_tensor(name, shape, dt))

        def pb(name, shape, dt):
            return ctx.enter_context(nc.psum_tensor(name, shape, dt))

        index_now = sb("index_now", [P, RING, 2, CH], I32)
        y_src = sb("y_src", [P, RING, CH, 2 * D], F16)
        a_src = sb("a_src", [P, RING, CH, P], F32)
        y_src_t = sb("y_src_t", [P, 2, 2 * KC, LISTED], F16)
        a_tok = sb("a_tok", [P, 2, LISTED], F32)
        q_t = sb("q_t", [P, 2, KC, 2, P], F16)
        prob = sb("prob", [P, 2, LISTED], F32)
        fill = sb("fill", [P, LISTED], F32)
        top, bias = sb("top", [P, 2, 1], F32), sb("bias", [P, 2, 1], F32)
        sum_e, one_e = sb("sum_e", [P, 2, 1], F32), sb("one_e", [P, 2, 1], F32)
        den, rden, rest = sb("den", [P, 2, 1], F32), sb("rden", [P, 2, 1], F32), sb("rest", [P, 2, 1], F32)
        masked = sb("masked", [P, 1], F32)
        minus_half = sb("minus_half", [P, 1], F32)
        prob_t = sb("prob_t", [P, 2, CH, 2, P], F16)
        mix = sb("mix", [P, 2, D], F32)
        mix_t = sb("mix_t", [P, 2, KC, 2, P], F16)
        x_tok = sb("x_tok", [P, 2, D], F32)
        val = sb("val", [P, D], F32)
        x1 = sb("x1", [P, 2, D], F32)
        stats2, mv2 = sb("stats2", [P, 2, 6], F32), sb("mv2", [P, 2, 2], F32)
        var2, rstd2 = sb("var2", [P, 2, 2], F32), sb("rstd2", [P, 2, 2], F32)
        alpha = sb("alpha", [P, 2, 1], F32)
        rt_row = sb("rt_row", [P, D], F32)
        rt_sum = sb("rt_sum", [P, 1], F32)
        dot_junk = sb("dot_junk", [P, D], F32)
        dot, off = sb("dot", [P, 2, 1], F32), sb("off", [P, 2, 1], F32)
        y2 = sb("y2", [P, 2, D], F32)
        y2_t = sb("y2_t", [P, 2, KC, 2, P], F16)

        turn_bank = [pb(f"turn_bank{b}", [P, 2 * KC, P], F16) for b in range(2)]
        z_bank = [pb(f"z_bank{b}", [P, D], F32) for b in range(2)]
        pa_bank = [pb(f"pa_bank{b}", [P, KC, P], F32) for b in range(2)]
        u_bank = pb("u_bank", [P, D], F32)
        o_bank = pb("o_bank", [P, D], F32)

        def sems(*names):
            return [sem(n) for n in names]

        y_in, a_in = [sem(f"y_in{r}") for r in range(RING)], [sem(f"a_in{r}") for r in range(RING)]
        q_in, xt_in = [sem(f"q_in{r}") for r in range(2)], [sem(f"xt_in{r}") for r in range(2)]
        x1_out, y2_out = [sem(f"x1_out{r}") for r in range(2)], [sem(f"y2_out{r}") for r in range(2)]
        y2t_out = [sem(f"y2t_out{r}") for r in range(2)]
        index_ready, pow_done = sems("index_ready", "pow_done")
        passed, passed_dve = sems("passed2", "passed_dve2")
        setup, const_in, rt_ready = sems("setup", "const_in", "rt_ready")
        turn_full, turn_read = [sem(f"turn_full{b}") for b in range(2)], [sem(f"turn_read{b}") for b in range(2)]
        a_full, a_read, z_full, w_done = sems("a_full", "a_read", "z_full", "w_done")
        pt_full, pt_high, pt_low, pv_done = sems("pt_full", "pt_high", "pt_low", "pv_done")
        soft, top_ready, e_ready, prob_chain, prob_ready = sems("soft", "top_ready", "e_ready", "prob_chain", "prob_ready")
        mix_ready, mt_full, mt_high, mt_low, o_full = sems("mix_ready", "mt_full", "mt_high", "mt_low", "o_full")
        o_read, x1_ready, x1_chain, var_done, y2_ready = sems("o_read", "x1_ready", "x1_chain", "var_done", "y2_ready")
        route, norming, off_ready = sems("route", "norming", "off_ready")
        s_ready, y2_full, y2_high, y2_low = sems("s_ready", "y2_full", "y2_high", "y2_low")

        with nc.Block() as block:
            @block.sync
            def _(sp):
                sp.dma_start(rt_row[:, :], rtok.partition_broadcast(P)).then_inc(const_in, 16)

                def load_q(c):
                    wait(sp, z_full, 2 * (c.t - 1))
                    sp.dma_start(q_t[:, c.par].rearrange("p k e t -> p (k e t)"),
                                 qtab[bass.ds(c.t, 1)].rearrange("a p n -> p (a n)")).then_inc(q_in[c.par], 16)

                def load_x(c):
                    wait(sp, x1_ready, c.t - 1)
                    sp.dma_start(x_tok[:, c.par], x_tiles[bass.ds(c.t, 1)].rearrange("a p n -> p (a n)")
                                 ).then_inc(xt_in[c.par], 16)

                def store_y2t(c):
                    sp.wait_ge(y2_low, c.t + 1)
                    sp.dma_start(y2ttab[bass.ds(c.t, 1)].rearrange("a p n -> p (a n)"),
                                 y2_t[:, c.par].rearrange("p k e t -> p (k e t)")).then_inc(y2t_out[c.par], 16)

                def store_rows(c):
                    sp.wait_ge(x1_ready, c.t + 1)
                    sp.dma_start(x1_tiles[bass.ds(c.t, 1)].rearrange("a p n -> p (a n)"), x1[:, c.par]).then_inc(x1_out[c.par], 16)
                    sp.wait_ge(y2_ready, c.t + 1)
                    sp.dma_start(y2_tiles[bass.ds(c.t, 1)].rearrange("a p n -> p (a n)"), y2[:, c.par]).then_inc(y2_out[c.par], 16)

                pipeline(sp, [(load_q, 1), (load_x, 0), (store_rows, -3), (store_y2t, -3)])
                for b in range(2):
                    for s in (x1_out, y2_out, y2t_out):
                        sp.wait_ge(s[b], 16 * NT // 2)

            @block.gpsimd
            def _(pool):
                pool.memset(masked[:, :], MASKED).then_inc(setup, 1)
                pool.memset(minus_half[:, :], -0.5).then_inc(setup, 1)
                pool.wait_ge(setup, 2)

                def gather(c):
                    pool.wait_ge(index_ready, c.t + 1)
                    pool.sem_inc(passed, 1)
                    for n in range(CH):
                        pool.indirect_dma_start(out=y_src[:, c.ring, n, :], out_offset=None, in_=ytab,
                                                in_offset=bass.IndirectOffsetOnAxis(ap=index_now[:, c.ring, 0, n:n + 1], axis=0)
                                                ).then_inc(y_in[c.ring], 16)
                    for n in range(CH):
                        pool.indirect_dma_start(out=a_src[:, c.ring, n, :], out_offset=None, in_=adj_rows,
                                                in_offset=bass.IndirectOffsetOnAxis(ap=index_now[:, c.ring, 1, n:n + 1], axis=0)
                                                ).then_inc(a_in[c.ring], 16)

                def powers(c):
                    pool.wait_ge(var_done, c.t + 1)
                    pool.tensor_tensor(rstd2[:, c.par], var2[:, c.par], minus_half[:, :].broadcast_to([P, 2]),
                                       ALU.pow).then_inc(pow_done, 1)

                pipeline(pool, [(gather, 2), (powers, -2)])

            @block.tensor
            def _(pe):
                ident, ident16 = keep["ident"], keep["ident16"]

                def turn_sources(*chunks):
                    def stage(c):
                        if chunks[0] == 0:
                            pe.wait_ge(y_in[c.ring], (c.turn + 1) * (16 * CH))
                        for n in chunks:
                            b = n % 2
                            wait(pe, turn_read[b], c.t * (3 - b) + n // 2)
                            for m in range(2 * KC):
                                last = pe.transpose(turn_bank[b][:, m, :], y_src[:, c.ring, n, m * P:(m + 1) * P], ident16[:, :])
                            last.then_inc(turn_full[b], 1)
                    return stage

                def turn_adjacency(c):
                    pe.wait_ge(a_in[c.ring], (c.turn + 1) * (16 * CH))
                    wait(pe, pt_low, 2 * (c.t - 1))
                    for b, (lo, hi) in enumerate(BANKS):
                        for n in range(lo, hi):
                            last = pe.transpose(pa_bank[b][:, n - lo, :], a_src[:, c.ring, n, :], ident[:, :])
                        last.then_inc(a_full, 1)

                def scores(c):
                    pe.wait_ge(q_in[c.par], (c.pair + 1) * 16)
                    pe.wait_ge(turn_read[0], c.t * 3 + 3)
                    pe.wait_ge(turn_read[1], c.t * 2 + 2)
                    for b, (lo, hi) in enumerate(BANKS):
                        wait(pe, (y2_low, mt_low)[b], c.t - (3, 1)[b])
                        if isinstance(c.t, int) and 0 < c.t <= 3:
                            pe.wait_ge(w_done, 2 * c.t - 1 + b)
                        for k in range(KC):
                            for e, f in PASSES:
                                last = pe.matmul(z_bank[b][:, 0:(hi - lo) * P], q_t[:, c.par, k, e, :],
                                                 y_src_t[:, c.par, f * KC + k, lo * P:hi * P],
                                                 start=(k == 0 and e + f == 0), stop=(k == KC - 1 and e == 1))
                        last.then_inc(z_full, 1)

                def turn_probs(c):
                    pe.wait_ge(prob_ready, c.t + 1)
                    pe.wait_ge(a_read, min(2 * c.t + 4, 2 * NT) if isinstance(c.t, int) else c.t * 2 + 4)
                    for b, (lo, hi) in enumerate(BANKS):
                        for n in range(lo, hi):
                            last = pe.transpose(pa_bank[b][:, n - lo, :], prob[:, c.par, n * P:(n + 1) * P], ident[:, :])
                        last.then_inc(pt_full, 1)

                def mix_sources(*chunks):
                    def stage(c):
                        if chunks[0] == 0:
                            pe.wait_ge(pt_low, c.t * 2 + 2)
                            wait(pe, mix_ready, c.t)
                        for n in chunks:
                            for e, f in PASSES:
                                last = pe.matmul(u_bank[:, :], prob_t[:, c.par, n, e, :], y_src[:, c.ring, n, f * D:(f + 1) * D],
                                                 start=(n == 0 and e + f == 0), stop=(n == CH - 1 and e == 1))
                        if chunks[-1] == CH - 1:
                            last.then_inc(pv_done, 1)
                    return stage

                def turn_mix(c):
                    pe.wait_ge(mix_ready, c.t + 1)
                    pe.wait_ge(w_done, min(2 * c.t + 4, 2 * NT) if isinstance(c.t, int) else c.t * 2 + 4)
                    for k in range(KC):
                        last = pe.transpose(z_bank[1][:, k * P:(k + 1) * P], mix[:, c.par, k * P:(k + 1) * P], ident[:, :])
                    last.then_inc(mt_full, 1)

                def values(c):
                    pe.wait_ge(mt_low, c.t + 1)
                    wait(pe, o_read, c.t)
                    for k in range(KC):
                        for e, f in PASSES:
                            last = pe.matmul(o_bank[:, :], mix_t[:, c.par, k, e, :], keep["wv"][:, k, f, :],
                                             start=(k == 0 and e + f == 0), stop=(k == KC - 1 and e == 1))
                    last.then_inc(o_full, 1)

                def turn_y2(c):
                    pe.wait_ge(y2_ready, c.t + 1)
                    pe.wait_ge(w_done, min(2 * c.t + 7, 2 * NT) if isinstance(c.t, int) else c.t * 2 + 7)
                    for k in range(KC):
                        last = pe.transpose(z_bank[0][:, k * P:(k + 1) * P], y2[:, c.par, k * P:(k + 1) * P], ident[:, :])
                    last.then_inc(y2_full, 1)

                pipeline(pe, [(scores, 0), (turn_probs, -1), (turn_sources(0, 1), 1), (mix_sources(0), -1),
                              (turn_sources(2, 3), 1), (mix_sources(1), -1), (turn_sources(4), 1), (turn_adjacency, 1),
                              (mix_sources(*range(2, CH)), -1), (turn_y2, -3),
                              (values, -2), (turn_mix, -1)])

            def leave_turned(eng, c, n):
                b = n % 2
                eng.wait_ge(turn_full[b], c.t * (3 - b) + (n // 2 + 1))
                wait(eng, z_full, 2 * (c.t - 1))
                dst, src = y_src_t[:, c.par, :, n * P:(n + 1) * P], turn_bank[b][:, :, :]
                ins = eng.activation(dst, src, ACT.Copy) if eng is nc.scalar else eng.tensor_copy(dst, src)
                ins.then_inc(turn_read[b], 1)

            @block.scalar
            def _(act):
                act.wait_ge(setup, 2)

                def indices(c):
                    wait(act, pv_done, c.t - 3)
                    wait(act, a_full, 2 * (c.t - 3))
                    act.activation(index_now[:, c.ring], keep["index"][:, bass.ds(c.t, 1)].rearrange("p a b c -> p (a b) c"),
                                   ACT.Copy).then_inc(index_ready, 1)

                def high_probs(c):
                    wait(act, pv_done, c.t - 1)
                    for b, (lo, hi) in enumerate(BANKS):
                        act.wait_ge(pt_full, c.t * 2 + (b + 1))
                        act.activation(prob_t[:, c.par, lo:hi, 0, :], pa_bank[b][:, 0:hi - lo, :], ACT.Copy, scale=PS).then_inc(pt_high, 1)

                def turned(c):
                    for n in ACT_TURNS:
                        leave_turned(act, c, n)

                def adjacency(c):
                    wait(act, w_done, 2 * (c.t - 1))
                    for b, (lo, hi) in enumerate(BANKS):
                        act.wait_ge(a_full, c.t * 2 + (b + 1))
                        act.activation(a_tok[:, c.par, lo * P:hi * P], pa_bank[b][:, 0:hi - lo, :].rearrange("p c t -> p (c t)"),
                                       ACT.Copy).then_inc(a_read, 1)

                def high_y2(c):
                    act.wait_ge(y2_full, c.t + 1)
                    wait(act, y2t_out[c.par], c.pair * 16)
                    act.activation(y2_t[:, c.par, :, 0, :], z_bank[0][:, :].rearrange("p (k t) -> p k t", k=KC), ACT.Copy
                                   ).then_inc(y2_high, 1)

                def exps(c):
                    act.wait_ge(top_ready, c.t + 1)
                    act.activation(one_e[:, c.par], masked[:, :], ACT.Exp, bias=bias[:, c.par], scale=SCALE).then_inc(e_ready, 1)
                    act.activation(prob[:, c.par], prob[:, c.par], ACT.Exp, bias=bias[:, c.par], scale=SCALE,
                                   accum_out=sum_e[:, c.par]).then_inc(e_ready, 1)

                def high_mix(c):
                    act.wait_ge(mt_full, c.t + 1)
                    wait(act, o_full, c.t - 1)
                    act.activation(mix_t[:, c.par, :, 0, :], z_bank[1][:, :].rearrange("p (k t) -> p k t", k=KC), ACT.Copy,
                                   scale=1.0 / PS).then_inc(mt_high, 1)

                pipeline(act, [(high_probs, -1), (indices, 2), (turned, 1), (adjacency, 1), (exps, 0), (high_y2, -3), (high_mix, -1)])

            @block.vector
            def _(dve):
                dve.wait_ge(const_in, 16)
                dve.tensor_reduce(rt_sum[:, :], rt_row[:, :], AX_X, ALU.add).then_inc(rt_ready, 1)
                dve.wait_ge(rt_ready, 1)
                softs, probs, rows = StageChain(dve, soft, 2), StageChain(dve, prob_chain, 2), StageChain(dve, x1_chain, 3)
                routes, norm_chain = StageChain(dve, route, 1), StageChain(dve, norming, 1)

                def low_probs(c):
                    for b, (lo, hi) in enumerate(BANKS):
                        dve.wait_ge(pt_high, c.t * 2 + (b + 1))
                        dve.scalar_tensor_tensor(prob_t[:, c.par, lo:hi, 1, :], pa_bank[b][:, 0:hi - lo, :], PS,
                                                 prob_t[:, c.par, lo:hi, 0, :], ALU.mult, ALU.subtract).then_inc(pt_low, 1)

                def weigh(c):
                    wait(dve, pt_full, 2 * (c.t - 1))
                    for b, (lo, hi) in enumerate(BANKS):
                        dve.wait_ge(z_full, c.t * 2 + (b + 1))
                        dve.wait_ge(a_read, c.t * 2 + (b + 1))
                        dve.scalar_tensor_tensor(prob[:, c.par, lo * P:hi * P], z_bank[b][:, 0:(hi - lo) * P],
                                                 keep["cs"][:, bass.ds(c.t, 1)], a_tok[:, c.par, lo * P:hi * P],
                                                 ALU.add, ALU.mult).then_inc(w_done, 1)

                def turned(c):
                    for n in DVE_TURNS:
                        leave_turned(dve, c, n)

                def low_y2(c):
                    dve.wait_ge(y2_high, c.t + 1)
                    dve.tensor_tensor(y2_t[:, c.par, :, 1, :], z_bank[0][:, :].rearrange("p (k t) -> p k t", k=KC),
                                      y2_t[:, c.par, :, 0, :], ALU.subtract).then_inc(y2_low, 1)

                def maxima(c):
                    softs.begin(c)
                    dve.wait_ge(w_done, c.t * 2 + 2)
                    softs.step(dve.tensor_scalar(fill[:, :], prob[:, c.par], 0.0, MASKED, ALU.is_equal, ALU.mult))
                    dve.sem_inc(passed_dve, 1)
                    softs.step(dve.tensor_tensor_reduce(out=prob[:, c.par], in0=prob[:, c.par], in1=fill[:, :], scale=1.0,
                                                        scalar=MASKED, op0=ALU.add, op1=ALU.max, accum_out=top[:, c.par]))
                    dve.tensor_scalar(bias[:, c.par], top[:, c.par], -SCALE, float(np.log(PS)), ALU.mult, ALU.add).then_inc(top_ready, 1)
                    softs.end()

                def mixed(c):
                    dve.wait_ge(pv_done, c.t + 1)
                    wait(dve, mt_full, c.t - 1)
                    dve.scalar_tensor_tensor(mix[:, c.par], keep["ytot"][:, :], rest[:, c.par], u_bank[:, :],
                                             ALU.mult, ALU.add).then_inc(mix_ready, 1)

                def normalise(c):
                    probs.begin(c)
                    dve.wait_ge(e_ready, c.t * 2 + 2)
                    probs.step(dve.scalar_tensor_tensor(den[:, c.par], one_e[:, c.par], float(N - LISTED), sum_e[:, c.par],
                                                        ALU.mult, ALU.add))
                    probs.step(dve.reciprocal(rden[:, c.par], den[:, c.par]))
                    dve.tensor_scalar(rest[:, c.par], one_e[:, c.par], rden[:, c.par], PS, ALU.mult, ALU.mult)
                    dve.tensor_scalar(prob[:, c.par], prob[:, c.par], one_e[:, c.par], rden[:, c.par], ALU.subtract,
                                      ALU.mult).then_inc(prob_ready, 1)
                    probs.end()

                def residual(c):
                    dve.wait_ge(o_full, c.t + 1)
                    dve.scalar_tensor_tensor(val[:, :], o_bank[:, :], 1.0 / ZS, keep["bvb"][:, :], ALU.mult, ALU.add
                                             ).then_inc(o_read, 1)
                    dve.wait_ge(o_read, c.t + 1)
                    dve.wait_ge(xt_in[c.par], (c.pair + 1) * 16)
                    wait(dve, x1_out[c.par], c.pair * 16)
                    dve.scalar_tensor_tensor(x1[:, c.par], val[:, :], 0.0, x_tok[:, c.par], ALU.max, ALU.add).then_inc(x1_ready, 1)

                def variance(c):
                    rows.begin(c)
                    dve.wait_ge(x1_ready, c.t + 1)
                    rows.step(dve.bn_stats(stats2[:, c.par], x1[:, c.par]))
                    dve.sem_inc(passed_dve, 1)
                    rows.step(dve.bn_aggr(mv2[:, c.par], stats2[:, c.par]))
                    dve.tensor_scalar(var2[:, c.par, 0:1], mv2[:, c.par, 1:2], 1.0 / (YS * YS), None, ALU.mult)
                    rows.step(dve.tensor_scalar(var2[:, c.par, 1:2], mv2[:, c.par, 1:2], EPS_LN, 1.0 / (YS * YS), ALU.add, ALU.mult))
                    dve.sem_inc(var_done, 1)
                    rows.end()

                def low_mix(c):
                    dve.wait_ge(mt_high, c.t + 1)
                    dve.scalar_tensor_tensor(mix_t[:, c.par, :, 1, :], z_bank[1][:, :].rearrange("p (k t) -> p k t", k=KC),
                                             1.0 / PS, mix_t[:, c.par, :, 0, :], ALU.mult, ALU.subtract).then_inc(mt_low, 1)

                def dots(c):
                    routes.begin(c)
                    routes.step(dve.tensor_tensor_reduce(out=dot_junk[:, :], in0=x1[:, c.par], in1=rt_row[:, :], scale=1.0,
                                                         scalar=0.0, op0=ALU.mult, op1=ALU.add, accum_out=dot[:, c.par]))
                    dve.scalar_tensor_tensor(off[:, c.par], mv2[:, c.par, 0:1], rt_sum[:, 0:1], dot[:, c.par],
                                             ALU.mult, ALU.subtract).then_inc(off_ready, 1)
                    routes.end()

                def norms(c):
                    norm_chain.begin(c)
                    dve.wait_ge(pow_done, c.t + 1)
                    norm_chain.step(dve.scalar_tensor_tensor(alpha[:, c.par], rstd2[:, c.par, 1:2], float(np.sqrt(D)) * 1e12,
                                                             rstd2[:, c.par, 0:1], ALU.mult, ALU.min))
                    wait(dve, y2_out[c.par], c.pair * 16)
                    wait(dve, y2_full, c.t - 1)
                    dve.tensor_scalar(y2[:, c.par], x1[:, c.par], mv2[:, c.par, 0:1], alpha[:, c.par], ALU.subtract,
                                      ALU.mult).then_inc(y2_ready, 1)
                    dve.wait_ge(off_ready, c.t + 1)
                    dve.tensor_scalar(keep["s"][:, bass.ds(c.t, 1)], off[:, c.par], rstd2[:, c.par, 1:2], -1.0 / YS,
                                      ALU.mult, ALU.mult).then_inc(s_ready, 1)
                    norm_chain.end()

                pipeline(dve, [(low_probs, -1), (turned, 1), (weigh, 0), (norms, -3), (maxima, 0), (mixed, -1),
                               (normalise, 0), (low_y2, -3), (residual, -2), (low_mix, -1), (variance, -2),
                               (dots, -2)])


BANK = 512
PIECES = N // BANK


def attend_all(nc, keep, x, adj, rtok, ytab, qtab, x1tab, y2rows, y2ttab, sem):
    x_tiles = x.rearrange("(t p) d -> t p d", p=P)
    adj_tiles = adj.rearrange("(t p) j -> t p j", p=P)
    x1_tiles = x1tab.rearrange("(t p) d -> t p d", p=P)
    y2_tiles = y2rows.rearrange("(t p) d -> t p d", p=P)
    with ExitStack() as ctx:
        def sb(name, shape, dt):
            return ctx.enter_context(nc.sbuf_tensor(name, shape, dt))

        def pb(name, shape, dt):
            return ctx.enter_context(nc.psum_tensor(name, shape, dt))

        def sems(*names):
            return [sem(n) for n in names]

        ya = sb("all_y", [P, NT, 2 * D], F16)
        ya_t = sb("all_y_t", [P, 2 * KC, N], F16)
        adj_sb = sb("all_adj", [P, 2, BANK], F32)
        q_t = sb("all_q_t", [P, KC, 2, P], F16)
        prob = sb("all_prob", [P, N], F32)
        fill = sb("all_fill", [P, BANK], F32)
        tops, top, bias = sb("all_tops", [P, PIECES], F32), sb("all_top", [P, 1], F32), sb("all_bias", [P, 1], F32)
        sum_e, den, rden = sb("all_sum_e", [P, 1], F32), sb("all_den", [P, 1], F32), sb("all_rden", [P, 1], F32)
        minus_half = sb("all_minus_half", [P, 1], F32)
        prob_t = sb("all_prob_t", [P, 2, 4, 2, P], F16)
        mix, mix_t = sb("all_mix", [P, D], F32), sb("all_mix_t", [P, KC, 2, P], F16)
        x_tok, x1, y2 = sb("all_x_tok", [P, D], F32), sb("all_x1", [P, D], F32), sb("all_y2", [P, D], F32)
        stats, mv = sb("all_stats", [P, 6], F32), sb("all_mv", [P, 2], F32)
        var, rstd = sb("all_var", [P, 2], F32), sb("all_rstd", [P, 2], F32)
        alpha, dot, off = sb("all_alpha", [P, 1], F32), sb("all_dot", [P, 1], F32), sb("all_off", [P, 1], F32)
        rt_row, rt_sum = sb("all_rt_row", [P, D], F32), sb("all_rt_sum", [P, 1], F32)
        y2_t = sb("all_y2_t", [P, KC, 2, P], F16)
        z_bank = [pb(f"all_z_bank{b}", [P, BANK], F32) for b in range(2)]
        p_bank = [pb(f"all_p_bank{b}", [P, 4, P], F32) for b in range(2)]
        turn_bank = [pb(f"all_turn_bank{b}", [P, 2 * KC, P], F16) for b in range(2)]
        u_bank, o_bank = pb("all_u_bank", [P, D], F32), pb("all_o_bank", [P, D], F32)

        ya_in, rt_in, half_ready, rt_ready = sems("all_y_in", "all_rt_in", "all_half_ready", "all_rt_ready")
        turned, left = sems("all_turned", "all_left")
        adj_in = [sem("all_adj_in0"), sem("all_adj_in1")]
        q_in, x_in, x1_out, y2_out, y2t_out = sems("all_q_in", "all_x_in", "all_x1_out", "all_y2_out", "all_y2t_out")
        scored, weighed, adj_free, masking, top_ready = sems("all_scored", "all_weighed", "all_adj_free", "all_masking", "all_top_ready")
        e_ready, prob_ready, p_full, p_high, p_low, p_used = sems("all_e_ready", "all_prob_ready", "all_p_full",
                                                                   "all_p_high", "all_p_low", "all_p_used")
        mix_ready, mt_full, mt_high, mt_low, o_full = sems("all_mix_ready", "all_mt_full", "all_mt_high", "all_mt_low", "all_o_full")
        x1_ready, tail, var_done, pow_done, y2_ready = sems("all_x1_ready", "all_tail", "all_var_done", "all_pow_done", "all_y2_ready")
        y2_full, y2_high, y2_low, carried = sems("all_y2_full", "all_y2_high", "all_y2_low", "all_carried")

        with nc.Block() as block:
            @block.sync
            def _(sp):
                sp.dma_start(rt_row[:, :], rtok.partition_broadcast(P)).then_inc(rt_in, 16)
                sp.dma_start(ya[:, :, :], ytab.rearrange("(c p) d -> p c d", p=P)).then_inc(ya_in, 16)
                sp.sem_inc(adj_free, 2)
                with sp.Fori(0, NT) as t:
                    sp.dma_start(q_t[:, :, :, :].rearrange("p k e t -> p (k e t)"),
                                 qtab[bass.ds(t, 1)].rearrange("a p n -> p (a n)")).then_inc(q_in, 16)
                    sp.dma_start(x_tok[:, :], x_tiles[bass.ds(t, 1)].rearrange("a p n -> p (a n)")).then_inc(x_in, 16)
                    for b in range(PIECES):
                        sp.wait_ge(adj_free, t * PIECES + (b + 1))
                        sp.dma_start(adj_sb[:, b % 2], adj_tiles[bass.ds(t, 1), :, b * BANK:(b + 1) * BANK]
                                     .rearrange("a p n -> p (a n)")).then_inc(adj_in[b % 2], 16)
                    sp.wait_ge(x1_ready, t + 1)
                    sp.dma_start(x1_tiles[bass.ds(t, 1)].rearrange("a p n -> p (a n)"), x1[:, :]).then_inc(x1_out, 16)
                    sp.wait_ge(y2_ready, t + 1)
                    sp.dma_start(y2_tiles[bass.ds(t, 1)].rearrange("a p n -> p (a n)"), y2[:, :]).then_inc(y2_out, 16)
                    sp.wait_ge(y2_low, t + 1)
                    sp.dma_start(y2ttab[bass.ds(t, 1)].rearrange("a p n -> p (a n)"),
                                 y2_t[:, :, :, :].rearrange("p k e t -> p (k e t)")).then_inc(y2t_out, 16)
                for s in (x1_out, y2_out, y2t_out):
                    sp.wait_ge(s, 16 * (NT + 1))

            @block.gpsimd
            def _(pool):
                pool.memset(minus_half[:, :], -0.5).then_inc(half_ready, 1)
                pool.wait_ge(half_ready, 1)
                with pool.Fori(0, NT) as t:
                    pool.wait_ge(var_done, t + 1)
                    pool.tensor_tensor(rstd[:, :], var[:, :], minus_half[:, :].broadcast_to([P, 2]), ALU.pow).then_inc(pow_done, 1)

            @block.tensor
            def _(pe):
                ident, ident16 = keep["ident"], keep["ident16"]
                pe.wait_ge(ya_in, 16)
                pe.sem_inc(left, 2)
                with pe.Fori(0, NT // 2) as i:
                    for h in range(2):
                        pe.wait_ge(left, i * 2 + 2)
                        for m in range(2 * KC):
                            last = pe.transpose(turn_bank[h][:, m, :],
                                                ya[:, bass.ds(i * 2 + h, 1), m * P:(m + 1) * P].rearrange("p a n -> p (a n)"),
                                                ident16[:, :])
                        last.then_inc(turned, 1)
                pe.wait_ge(left, NT + 2)
                with pe.Fori(0, NT) as t:
                    pe.wait_ge(q_in, t * 16 + 16)
                    for b in range(PIECES):
                        if b >= 2:
                            pe.wait_ge(weighed, t * PIECES + (b - 1))
                        for k in range(KC):
                            for e, f in PASSES:
                                last = pe.matmul(z_bank[b % 2][:, :], q_t[:, k, e, :], ya_t[:, f * KC + k, b * BANK:(b + 1) * BANK],
                                                 start=(k == 0 and e + f == 0), stop=(k == KC - 1 and e == 1))
                        last.then_inc(scored, 1)
                    pe.wait_ge(prob_ready, t + 1)
                    for g in range(PIECES):
                        if g > 0:
                            pe.wait_ge(p_low, t * PIECES + g)
                        for n in range(4):
                            last = pe.transpose(p_bank[g % 2][:, n, :], prob[:, (4 * g + n) * P:(4 * g + n + 1) * P], ident[:, :])
                        last.then_inc(p_full, 1)
                        pe.wait_ge(p_low, t * PIECES + (g + 1))
                        for n in range(4):
                            for e, f in PASSES:
                                last = pe.matmul(u_bank[:, :], prob_t[:, g % 2, n, e, :], ya[:, 4 * g + n, f * D:(f + 1) * D],
                                                 start=(g + n + e + f == 0), stop=(g == PIECES - 1 and n == 3 and e == 1))
                        last.then_inc(p_used, 1)
                    pe.wait_ge(mix_ready, t + 1)
                    for k in range(KC):
                        last = pe.transpose(z_bank[1][:, k * P:(k + 1) * P], mix[:, k * P:(k + 1) * P], ident[:, :])
                    last.then_inc(mt_full, 1)
                    pe.wait_ge(mt_low, t + 1)
                    for k in range(KC):
                        for e, f in PASSES:
                            last = pe.matmul(o_bank[:, :], mix_t[:, k, e, :], keep["wv"][:, k, f, :],
                                             start=(k == 0 and e + f == 0), stop=(k == KC - 1 and e == 1))
                    last.then_inc(o_full, 1)
                    pe.wait_ge(y2_ready, t + 1)
                    for k in range(KC):
                        last = pe.transpose(z_bank[0][:, k * P:(k + 1) * P], y2[:, k * P:(k + 1) * P], ident[:, :])
                    last.then_inc(y2_full, 1)
                    pe.wait_ge(y2_low, t + 1)

            @block.scalar
            def _(act):
                act.sem_inc(y2t_out, 16)
                with act.Fori(0, NT) as t:
                    act.wait_ge(top_ready, t + 1)
                    act.activation(prob[:, :], prob[:, :], ACT.Exp, bias=bias[:, :], scale=SCALE, accum_out=sum_e[:, :]
                                   ).then_inc(e_ready, 1)
                    for g in range(PIECES):
                        act.wait_ge(p_full, t * PIECES + (g + 1))
                        if g >= 2:
                            act.wait_ge(p_used, t * PIECES + (g - 1))
                        act.activation(prob_t[:, g % 2, :, 0, :], p_bank[g % 2][:, :, :], ACT.Copy).then_inc(p_high, 1)
                    act.wait_ge(mt_full, t + 1)
                    act.activation(mix_t[:, :, 0, :], z_bank[1][:, :].rearrange("p (k t) -> p k t", k=KC), ACT.Copy,
                                   scale=1.0 / PS).then_inc(mt_high, 1)
                    act.wait_ge(y2_full, t + 1)
                    act.wait_ge(y2t_out, t * 16 + 16)
                    act.activation(y2_t[:, :, 0, :], z_bank[0][:, :].rearrange("p (k t) -> p k t", k=KC), ACT.Copy
                                   ).then_inc(y2_high, 1)

            @block.vector
            def _(dve):
                dve.wait_ge(rt_in, 16)
                dve.tensor_reduce(rt_sum[:, :], rt_row[:, :], AX_X, ALU.add).then_inc(rt_ready, 1)
                dve.wait_ge(rt_ready, 1)
                with dve.Fori(0, NT // 2) as i:
                    for h in range(2):
                        dve.wait_ge(turned, i * 2 + (h + 1))
                        dve.tensor_copy(ya_t[:, :, bass.ds(i * (2 * P) + h * P, P)], turn_bank[h][:, :, :]).then_inc(left, 1)
                dve.sem_inc(x1_out, 16)
                dve.sem_inc(y2_out, 16)
                with dve.Fori(0, NT) as t:
                    masks = Chain(dve, masking)
                    masks.base = t * (2 * PIECES + 1)
                    for b in range(PIECES):
                        piece = prob[:, b * BANK:(b + 1) * BANK]
                        dve.wait_ge(scored, t * PIECES + (b + 1))
                        dve.wait_ge(adj_in[b % 2], t * (8 * PIECES) + 16 * (b // 2 + 1))
                        dve.scalar_tensor_tensor(piece, z_bank[b % 2][:, :], keep["cs"][:, bass.ds(t, 1)], adj_sb[:, b % 2],
                                                 ALU.add, ALU.mult).then_inc(weighed, 1)
                        dve.wait_ge(weighed, t * PIECES + (b + 1))
                        dve.sem_inc(adj_free, 1)
                        masks.step(dve.tensor_scalar(fill[:, :], piece, 0.0, MASKED, ALU.is_equal, ALU.mult))
                        dve.sem_inc(carried, 1)
                        masks.step(dve.tensor_tensor_reduce(out=piece, in0=piece, in1=fill[:, :], scale=1.0, scalar=MASKED,
                                                            op0=ALU.add, op1=ALU.max, accum_out=tops[:, b:b + 1]))
                    masks.step(dve.tensor_reduce(top[:, :], tops[:, :], AX_X, ALU.max))
                    dve.tensor_scalar(bias[:, :], top[:, :], -SCALE, float(np.log(PS)), ALU.mult, ALU.add).then_inc(top_ready, 1)
                    ch = Chain(dve, tail)
                    ch.base = t * 10
                    dve.wait_ge(e_ready, t + 1)
                    ch.step(dve.tensor_scalar(den[:, :], sum_e[:, :], 1.0 / PS, None, ALU.mult))
                    ch.step(dve.reciprocal(rden[:, :], den[:, :]))
                    dve.tensor_scalar(prob[:, :], prob[:, :], rden[:, :], None, ALU.mult).then_inc(prob_ready, 1)
                    for g in range(PIECES):
                        dve.wait_ge(p_high, t * PIECES + (g + 1))
                        dve.tensor_tensor(prob_t[:, g % 2, :, 1, :], p_bank[g % 2][:, :, :], prob_t[:, g % 2, :, 0, :],
                                          ALU.subtract).then_inc(p_low, 1)
                    dve.wait_ge(p_used, t * PIECES + PIECES)
                    dve.tensor_copy(mix[:, :], u_bank[:, :]).then_inc(mix_ready, 1)
                    dve.wait_ge(mt_high, t + 1)
                    dve.scalar_tensor_tensor(mix_t[:, :, 1, :], z_bank[1][:, :].rearrange("p (k t) -> p k t", k=KC),
                                             1.0 / PS, mix_t[:, :, 0, :], ALU.mult, ALU.subtract).then_inc(mt_low, 1)
                    dve.wait_ge(o_full, t + 1)
                    dve.wait_ge(x1_out, t * 16 + 16)
                    ch.step(dve.scalar_tensor_tensor(x1[:, :], o_bank[:, :], 1.0 / ZS, keep["bvb"][:, :], ALU.mult, ALU.add))
                    dve.wait_ge(x_in, t * 16 + 16)
                    dve.scalar_tensor_tensor(x1[:, :], x1[:, :], 0.0, x_tok[:, :], ALU.max, ALU.add).then_inc(x1_ready, 1)
                    dve.wait_ge(x1_ready, t + 1)
                    ch.step(dve.bn_stats(stats[:, :], x1[:, :]))
                    dve.sem_inc(carried, 1)
                    ch.step(dve.bn_aggr(mv[:, :], stats[:, :]))
                    dve.tensor_scalar(var[:, 0:1], mv[:, 1:2], 1.0 / (YS * YS), None, ALU.mult)
                    ch.step(dve.tensor_scalar(var[:, 1:2], mv[:, 1:2], EPS_LN, 1.0 / (YS * YS), ALU.add, ALU.mult))
                    dve.sem_inc(var_done, 1)
                    dve.wait_ge(pow_done, t + 1)
                    ch.step(dve.scalar_tensor_tensor(alpha[:, :], rstd[:, 1:2], float(np.sqrt(D)) * 1e12, rstd[:, 0:1],
                                                     ALU.mult, ALU.min))
                    dve.wait_ge(y2_out, t * 16 + 16)
                    dve.tensor_scalar(y2[:, :], x1[:, :], mv[:, 0:1], alpha[:, :], ALU.subtract, ALU.mult).then_inc(y2_ready, 1)
                    ch.step(dve.tensor_tensor_reduce(out=fill[:, :], in0=x1[:, :], in1=rt_row[:, :], scale=1.0, scalar=0.0,
                                                     op0=ALU.mult, op1=ALU.add, accum_out=dot[:, :]))
                    ch.step(dve.scalar_tensor_tensor(off[:, :], mv[:, 0:1], rt_sum[:, 0:1], dot[:, :], ALU.mult, ALU.subtract))
                    ch.step(dve.tensor_scalar(keep["s"][:, bass.ds(t, 1)], off[:, :], rstd[:, 1:2], -1.0 / YS, ALU.mult, ALU.mult))
                    dve.wait_ge(y2_high, t + 1)
                    dve.tensor_tensor(y2_t[:, :, 1, :], z_bank[0][:, :].rearrange("p (k t) -> p k t", k=KC), y2_t[:, :, 0, :],
                                      ALU.subtract).then_inc(y2_low, 1)
                    dve.wait_ge(y2_low, t + 1)


K_ROUTE = 8.0
EPS_ROUTE = 0.1
RECENTRE = 12
CAP = 76.0
UNDERFLOW = -87.33654
LN_SHIFT = 50
WAYS = 8
ROUNDS, TOP_BIT = 10, 27
PER_STEP = 6
BEFORE_STEPS = 24
FIRST_RESULT = 6
HOT = 8
LATE_STEPS = 2


def feed_forward(nc, keep, ytab2t, x1tab, y2rows, w1h, w2h, out, sem):
    out_tiles = out.rearrange("(t p) d -> t p d", p=P)
    x1_tiles = x1tab.rearrange("(t p) d -> t p d", p=P)
    y2t_groups = ytab2t.rearrange("(g s) p n -> g p s n", s=GROUP)
    with ExitStack() as ctx:
        def sb(name, shape, dt):
            return ctx.enter_context(nc.sbuf_tensor(name, shape, dt))

        def sems(*names):
            return [sem(n) for n in names]

        w1l_sb, w2l_sb, b1l_sb, b1h_sb = keep["w1l"], keep["w2l"], keep["b1l"], keep["b1h"]
        b2l_row, b2h_row = keep["b2l"], keep["b2h"]
        w1h_sb = sb("w1h_sb", [P, KC, 2, HH], F16)
        w2h_sb = sb("w2h_sb", [P, HH // P // 4, 2, 4, D], F16)
        score = sb("score", [P, NT], F32)
        ones = sb("ones_c", [P, P], F32)
        threshold = sb("threshold", [P, 1], I32)

        with ExitStack() as c1:
            def tmp(name, shape, dt):
                return c1.enter_context(nc.sbuf_tensor(name, shape, dt))

            y_in_t = tmp("y_in_t", [P, 2, GROUP, KC, 2, P], F16)
            g32 = tmp("light_g32", [P, 2, HL // P, GROUP * P], F32)
            g64 = tmp("light_g64", [P, 2, HL // P, GROUP * P], F32)
            g_hl = tmp("light_g_hl", [P, 2, 2, HL // P, GROUP * P], F16)
            res = tmp("res", [P, 2, GROUP, D], F32)
            eighths = tmp("eighths", [P, P], F32)
            logits = tmp("logits", [P, NT + 1], F32)
            args, weights = tmp("args", [P, NT + 1], F32), tmp("weights", [P, NT + 1], F32)
            part, centre, s_top, s_part = (tmp(n, [P, 1], F32) for n in ("part_sum", "centre", "s_top", "s_part"))
            junk, log_a, low = tmp("junk", [P, NT], F32), tmp("log_a", [P, 1], F32), tmp("low", [P, NT], F32)
            steps_i, steps = tmp("steps_i", [P, WAYS], I32), tmp("steps", [P, WAYS], I32)
            cand = tmp("cand", [P, WAYS], I32)
            reached, count = tmp("reached", [P, WAYS, NT], F32), tmp("count", [P, WAYS], F32)
            met = tmp("met", [P, WAYS], F32)
            raw = tmp("heavy_raw", [P, 2, HH], F32)
            scaled = tmp("heavy_scaled", [P, 2, HH], F32)
            ps_h = [c1.enter_context(nc.psum_tensor(f"ps_h{i}", [P, GROUP * P], F32)) for i in range(4)]
            ps_o = [c1.enter_context(nc.psum_tensor(f"ps_o{i}", [P, D], F32)) for i in range(2)]
            ps_a = c1.enter_context(nc.psum_tensor("ps_a", [P, 1], F32))
            ps_n = c1.enter_context(nc.psum_tensor("ps_n", [P, WAYS], F32))
            g_in, x1_in, res_out = [[sem(f"{n}{h}") for h in range(2)] for n in ("g_in", "x1_in", "res_out")]
            c1_const, top_in, top_out, h_full = sems("c1_const", "top_in", "top_out", "h_full")
            gelu_ready, halves_ready, low_ready, with_bias, o_full, res_ready = sems(
                "gelu_ready", "halves_ready", "low_ready", "with_bias", "light_o_full", "res_ready")
            dve3, args_ready, exp_ready, part_ready, sum_ready, log_ready = sems(
                "dve3", "args_ready", "exp_ready", "part_ready", "sum_ready", "log_ready")
            final_ready, search, counted, totalled, carried_by = sems("final_ready", "search", "counted", "totalled", "carried_by")
            heavy_raw_in = [sem("heavy_raw_in0"), sem("heavy_raw_in1")]
            heavy_scaled, heavy_high, heavy_low = sems("heavy_scaled", "heavy_high", "heavy_low")
            TURNS = NG // 2
            assert TURNS == KC == HH // P // 4

            def heavy_half(weights_hl, u, half):
                v = weights_hl[:, bass.ds(u, 1), half]
                return v.rearrange("p a n -> p (a n)") if len(v.shape) == 3 else v.rearrange("p a c n -> p (a c n)")

            with nc.Block() as block:
                @block.sync
                def _(sp):
                    w1h_quarters = w1h.rearrange("(u p) n -> u p n", p=P)
                    w2h_quarters = w2h.rearrange("(u c p) n -> u p c n", c=4, p=P)
                    x1_groups = x1tab.rearrange("(g s p) d -> g p s d", s=GROUP, p=P)
                    out_groups = out.rearrange("(g s p) d -> g p s d", s=GROUP, p=P)

                    def load_y(g, h):
                        sp.dma_start(y_in_t[:, h].rearrange("p s k e t -> p s (k e t)"),
                                     y2t_groups[bass.ds(g, 1)].rearrange("a p s n -> p (a s) n")).then_inc(g_in[h], 16)

                    def load_x1(g, h):
                        sp.dma_start(res[:, h], x1_groups[bass.ds(g, 1)].rearrange("a p s d -> p (a s) d")).then_inc(x1_in[h], 16)

                    def store(g, h):
                        sp.wait_ge(res_ready, g * GROUP + GROUP)
                        sp.dma_start(out_groups[bass.ds(g, 1)].rearrange("a p s d -> p (a s) d"), res[:, h]).then_inc(res_out[h], 16)

                    def load_heavy(u):
                        sp.dma_start(raw[:, 0], w1h_quarters[bass.ds(u, 1)].rearrange("a p n -> p (a n)")).then_inc(heavy_raw_in[0], 16)
                        sp.dma_start(raw[:, 1].rearrange("p (c n) -> p c n", c=4),
                                     w2h_quarters[bass.ds(u, 1)].rearrange("a p c n -> p (a c) n")).then_inc(heavy_raw_in[1], 16)

                    load_y(0, 0)
                    load_y(1, 1)
                    load_x1(0, 0)
                    load_x1(1, 1)
                    load_heavy(0)
                    with sp.Fori(0, TURNS - 1) as i:
                        for h in range(2):
                            sp.wait_ge(h_full, i * 4 + 2 * (h + 1))
                            load_y(i * 2 + (2 + h), h)
                        for h in range(2):
                            store(i * 2 + h, h)
                        for h in range(2):
                            sp.wait_ge(res_out[h], i * 16 + 16)
                            load_x1(i * 2 + (2 + h), h)
                        sp.wait_ge(heavy_scaled, i * 2 + 2)
                        load_heavy(i + 1)
                    for h in range(2):
                        store(2 * TURNS - 2 + h, h)
                    for h in range(2):
                        sp.wait_ge(res_out[h], 16 * TURNS)

                @block.gpsimd
                def _(pool):
                    pool.memset(eighths[:, :], 1.0 / K_ROUTE).then_inc(c1_const, 1)
                    pool.memset(ones[:, :], 1.0).then_inc(c1_const, 1)
                    pool.iota(steps_i[:, :], pattern=[[1, WAYS]], base=0, channel_multiplier=0).then_inc(c1_const, 1)
                    pool.wait_ge(top_in, 1)
                    pool.partition_all_reduce(s_top[:, :], s_part[:, :], P, bass.bass_isa.ReduceOp.max).then_inc(top_out, 1)
                    with pool.Fori(0, TURNS) as i:
                        for h in range(2):
                            pool.wait_ge(halves_ready, i * 4 + 2 * (h + 1))
                            pool.tensor_tensor(g_hl[:, h, 1], g64[:, h], g_hl[:, h, 0], ALU.subtract).then_inc(low_ready, 1)
                            pool.wait_ge(x1_in[h], i * 16 + 16)
                            pool.sem_inc(carried_by, 1)
                            pool.tensor_tensor(res[:, h], res[:, h], b2l_row[:, :].unsqueeze(1).broadcast_to([P, GROUP, D]),
                                               ALU.add).then_inc(with_bias, 1)
                        for m, dst in enumerate((w1h_sb, w2h_sb)):
                            pool.wait_ge(heavy_high, i * 2 + (m + 1))
                            pool.tensor_tensor(heavy_half(dst, i, 1), scaled[:, m], heavy_half(dst, i, 0), ALU.subtract
                                               ).then_inc(heavy_low, 1)

                @block.vector
                def _(dve):
                    ch = Chain(dve, dve3)
                    ch.step(dve.tensor_copy(logits[:, 0:NT], keep["s"][:, :]))
                    dve.memset(logits[:, NT:NT + 1], 0.0)
                    dve.tensor_reduce(s_part[:, :], keep["s"][:, :], AX_X, ALU.max).then_inc(top_in, 1)
                    dve.wait_ge(top_out, 1)
                    ch.step(dve.tensor_copy(low[:, 0:1], s_part[:, :]))

                    def recentre(turn):
                        ch.step(dve.tensor_tensor(centre[:, :], logits[:, NT:NT + 1], s_top[:, :], ALU.min))
                        ch.step(dve.tensor_scalar(args[:, :], logits[:, :], centre[:, :], 1.0 / EPS_ROUTE, ALU.subtract, ALU.mult))
                        dve.tensor_scalar(args[:, :], args[:, :], CAP, None, ALU.min).then_inc(args_ready, 1)
                        dve.wait_ge(exp_ready, turn + 1)

                    def descend(done, n):
                        if n > 0:
                            dve.wait_ge(sum_ready, done + n)
                        a = weights[:, NT:NT + 1] if n == 0 else ps_a[:, :]
                        dve.tensor_scalar(junk[:, :], weights[:, 0:NT], a, None, ALU.min, ALU.add,
                                          accum_out=part[:, :]).then_inc(part_ready, 1)

                    def take_log(turn):
                        dve.wait_ge(log_ready, turn + 1)
                        ch.step(dve.tensor_scalar(log_a[:, :], log_a[:, :], LN_SHIFT * float(np.log(2.0)), EPS_ROUTE, ALU.add, ALU.mult))
                        ch.step(dve.tensor_tensor(logits[:, NT:NT + 1], log_a[:, :], centre[:, :], ALU.add))

                    def result(i, k):
                        h, s = k // GROUP, k % GROUP
                        if s == 0:
                            dve.wait_ge(with_bias, i * 2 + (h + 1))
                        dve.wait_ge(o_full, i * (2 * GROUP) + (k + 1))
                        dve.scalar_tensor_tensor(res[:, h, s], ps_o[k % 2][:, :], 1.0 / ZS, res[:, h, s], ALU.mult, ALU.add
                                                 ).then_inc(res_ready, 1)

                    base = ch.n
                    with dve.Fori(0, TURNS) as i:
                        ch.base, ch.n = i * 4 + base, 0
                        recentre(i)
                        for n in range(RECENTRE):
                            descend(i * RECENTRE, n)
                            if n >= FIRST_RESULT:
                                result(i, n - FIRST_RESULT)
                        for k in range(RECENTRE - FIRST_RESULT, 2 * GROUP):
                            result(i, k)
                        dve.wait_ge(res_ready, i * (2 * GROUP) + 2 * GROUP)
                        take_log(i)
                    ch.base, ch.n = 0, base + 4 * TURNS
                    recentre(TURNS)
                    for n in range(LATE_STEPS):
                        descend(TURNS * RECENTRE, n)
                    take_log(TURNS)
                    ch.step(dve.tensor_scalar(args[:, 0:NT], keep["s"][:, :], logits[:, NT:NT + 1], None, ALU.subtract))
                    ch.step(dve.tensor_scalar(low[:, :], args[:, 0:NT], 0.0, None, ALU.max))
                    ch.step(dve.tensor_tensor(args[:, 0:NT], args[:, 0:NT], low[:, :], ALU.subtract))
                    ch.step(dve.tensor_scalar(args[:, 0:NT], args[:, 0:NT], 1.0 / EPS_ROUTE, None, ALU.mult))
                    ch.step(dve.tensor_scalar(low[:, :], args[:, 0:NT], UNDERFLOW, None, ALU.is_ge))
                    dve.sem_inc(final_ready, 1)
                    dve.wait_ge(exp_ready, TURNS + 2)
                    ch.step(dve.tensor_tensor(score[:, :], weights[:, 0:NT], low[:, :], ALU.mult))

                    find = Chain(dve, search)
                    dve.wait_ge(c1_const, 3)
                    find.step(dve.tensor_single_scalar(steps[:, :], steps_i[:, :], TOP_BIT, ALU.logical_shift_left))
                    find.step(dve.memset(threshold[:, :], 0))
                    with dve.Fori(0, 2) as half:
                        find.base, find.n = half * (ROUNDS // 2 * 4) + 2, 0
                        for n in range(ROUNDS // 2):
                            find.step(dve.tensor_tensor(cand[:, :], steps[:, :], threshold[:, :].broadcast_to([P, WAYS]), ALU.bitwise_or))
                            find.step(dve.tensor_tensor(reached[:, :, :], score[:, :].unsqueeze(1).broadcast_to([P, WAYS, NT]),
                                                        cand[:, :].bitcast(F32).unsqueeze(2).broadcast_to([P, WAYS, NT]), ALU.is_ge))
                            dve.tensor_reduce(count[:, :], reached[:, :, :], AX_X, ALU.add).then_inc(counted, 1)
                            dve.tensor_single_scalar(steps[:, :], steps[:, :], 3, ALU.logical_shift_right)
                            dve.wait_ge(totalled, half * (ROUNDS // 2) + (n + 1))
                            find.step(dve.scalar_tensor_tensor(met[:, :], ps_n[:, :], float(ROUTED), cand[:, :].bitcast(F32),
                                                               ALU.is_ge, ALU.mult))
                            find.step(dve.tensor_reduce(threshold[:, :].bitcast(F32), met[:, :], AX_X, ALU.max))

                @block.scalar
                def _(act):
                    def split_heavy(i):
                        act.wait_ge(heavy_low, i * 2 + 2)
                        act.wait_ge(heavy_raw_in[0], i * 16 + 16)
                        act.activation(scaled[:, 0], raw[:, 0], ACT.Copy, scale=keep["gain_h"][:, bass.ds(i, 1)]).then_inc(heavy_scaled, 1)
                        act.wait_ge(heavy_raw_in[1], i * 16 + 16)
                        act.activation(scaled[:, 1], raw[:, 1], ACT.Copy, scale=YS).then_inc(heavy_scaled, 1)
                        for m, dst in enumerate((w1h_sb, w2h_sb)):
                            act.wait_ge(heavy_scaled, i * 2 + (m + 1))
                            act.activation(heavy_half(dst, i, 0), scaled[:, m], ACT.Copy).then_inc(heavy_high, 1)

                    def activate(i, h):
                        for c in range(HL // P):
                            act.wait_ge(h_full, i * 4 + (2 * h + c + 1))
                            act.activation(g32[:, h, c], ps_h[2 * h + c][:, :], ACT.Gelu, bias=b1l_sb[:, c:c + 1],
                                           scale=1.0 / ZS).then_inc(gelu_ready, 1)
                        act.wait_ge(gelu_ready, i * 4 + 2 * (h + 1))
                        act.activation(g_hl[:, h, 0], g32[:, h], ACT.Copy, scale=YS).then_inc(halves_ready, 1)
                        act.activation(g64[:, h], g32[:, h], ACT.Copy, scale=YS).then_inc(halves_ready, 1)

                    def exps(turn):
                        act.wait_ge(args_ready, turn + 1)
                        act.activation(weights[:, :], args[:, :], ACT.Exp).then_inc(exp_ready, 1)

                    def logs(turn, done):
                        act.wait_ge(sum_ready, done)
                        act.activation(log_a[:, :], ps_a[:, :], ACT.Ln, scale=2.0 ** -LN_SHIFT).then_inc(log_ready, 1)

                    act.sem_inc(heavy_low, 2)
                    with act.Fori(0, TURNS) as i:
                        exps(i)
                        for h in range(2):
                            activate(i, h)
                        split_heavy(i)
                        logs(i, i * RECENTRE + RECENTRE)
                    exps(TURNS)
                    logs(TURNS, TURNS * RECENTRE + LATE_STEPS)
                    act.wait_ge(final_ready, 1)
                    act.activation(weights[:, 0:NT], args[:, 0:NT], ACT.Exp).then_inc(exp_ready, 1)

                @block.tensor
                def _(pe):
                    pe.wait_ge(c1_const, 3)

                    def total(done):
                        pe.wait_ge(part_ready, done + 1)
                        pe.matmul(ps_a[:, :], eighths[:, :], part[:, :], start=True, stop=True).then_inc(sum_ready, 1)

                    with pe.Fori(0, TURNS) as i:
                        products = 0

                        def routing_steps():
                            n = (products - BEFORE_STEPS) // PER_STEP
                            if products >= BEFORE_STEPS and (products - BEFORE_STEPS) % PER_STEP == 0 and n < RECENTRE:
                                total(i * RECENTRE + n)

                        for h in range(2):
                            pe.wait_ge(g_in[h], i * 16 + 16)
                            for c in range(HL // P):
                                for k in range(KC):
                                    for e, f in PASSES:
                                        last = pe.matmul(ps_h[2 * h + c][:, :], w1l_sb[:, e, k, c * P:(c + 1) * P],
                                                         y_in_t[:, h, :, k, f, :], start=(k == 0 and e + f == 0),
                                                         stop=(k == KC - 1 and e == 1))
                                        products += 1
                                        if k == KC - 1 and e == 1:
                                            last.then_inc(h_full, 1)
                                        routing_steps()
                        for k in range(2 * GROUP):
                            h, s = k // GROUP, k % GROUP
                            if s == 0:
                                pe.wait_ge(low_ready, i * 2 + (h + 1))
                            if k >= 2:
                                pe.wait_ge(res_ready, i * (2 * GROUP) + (k - 1))
                            for c in range(HL // P):
                                for e, f in PASSES:
                                    last = pe.matmul(ps_o[k % 2][:, :], g_hl[:, h, e, c, s * P:(s + 1) * P], w2l_sb[:, f, c, :],
                                                     start=(c == 0 and e + f == 0), stop=(c == 1 and e == 1))
                                    products += 1
                                    if c == 1 and e == 1:
                                        last.then_inc(o_full, 1)
                                    routing_steps()
                    for n in range(LATE_STEPS):
                        total(TURNS * RECENTRE + n)
                    with pe.Fori(0, ROUNDS) as r:
                        pe.wait_ge(counted, r + 1)
                        pe.matmul(ps_n[:, :], ones[:, :], count[:, :], start=True, stop=True).then_inc(totalled, 1)

        route_and_heavy(nc, keep, score, threshold, ones, y2rows, w1h_sb, w2h_sb, b1h_sb, b2h_row, out, sem)


def route_and_heavy(nc, keep, score, threshold, ones, y2rows, w1h_sb, w2h_sb, b1h_sb, b2h_row, out, sem):
    B = ROUTED // P
    HC = HH // P
    with ExitStack() as ctx:
        def sb(name, shape, dt):
            return ctx.enter_context(nc.sbuf_tensor(name, shape, dt))

        def sems(*names):
            return [sem(n) for n in names]

        before = sb("before", [P, P], F32)
        above, level = sb("above", [P, NT], F32), sb("level", [P, NT], F32)
        run = sb("run", [P, NT], F32)
        need, n_above = sb("need", [P, 1], F32), sb("n_above", [P, 1], F32)
        place, taken = sb("place", [P, NT], F32), sb("taken", [P, NT], F32)
        slots_i, slots = sb("slots_i", [P, ROUTED], I32), sb("slots", [P, ROUTED], F16)
        slots_f = sb("slots_f", [P, ROUTED], F32)
        gain = sb("gain", [P, NT], F32)
        facts = sb("facts", [P, NT, 4], F16)
        p_i, t_i = sb("p_i", [P, 1], I32), sb("t_i", [P, NT], I32)
        hot = sb("hot", [P, HOT, ROUTED], F16)
        found = sb("found", [P, B, 4], F32)
        token_f, token, gains = sb("token_f", [P, B], F32), sb("token", [P, B], I32), sb("gains_r", [P, B], F32)
        y_rt = sb("y_rt", [P, B, D], F32)
        y_rt_t = sb("y_rt_t", [P, KC, 2, ROUTED], F16)
        base = sb("base", [P, B, D], F32)
        g32 = sb("g32", [P, 2, ROUTED], F32)
        g_hl = sb("g_hl", [P, HC, 2, ROUTED], F16)
        fin = sb("fin", [P, B, D], F32)
        ps_w = ctx.enter_context(nc.psum_tensor("ps_w", [P, 3, NT], F32))
        ps_f = ctx.enter_context(nc.psum_tensor("ps_f", [P, B, 4], F32))
        ps_r = [ctx.enter_context(nc.psum_tensor(f"ps_r{i}", [P, KC, P], F32)) for i in range(2)]
        ps_u = [ctx.enter_context(nc.psum_tensor(f"ps_u{i}", [P, D], F32)) for i in range(4)]

        tri_ready, iota2, dve4, sel_ready, prefix_ready = sems("tri_ready", "iota2", "dve4", "sel_ready", "prefix_ready")
        hot_ready, facts_ready, found_ready, token_ready = sems("hot_ready", "facts_ready", "found_ready", "token_ready")
        hot_used = sem("hot_used")
        rows_in = [sem(f"rows_in{b}") for b in range(B)]
        base_in, r_full, r_high, r_low, u_full, u_act, u_high, u_low = sems(
            "base_in", "r_full", "r_high", "r_low", "u_full", "u_act", "u_high", "u_low")
        d_full, d_read, fin_ready, fin_out = sems("d_full", "d_read", "fin_ready", "fin_out")

        with nc.Block() as block:
            @block.gpsimd
            def _(pool):
                pool.memset(before[:, :], 1.0).then_inc(tri_ready, 1)
                pool.wait_ge(tri_ready, 1)
                pool.affine_select(out=before[:, :], in_=before[:, :], compare_op=ALU.is_gt, fill=0.0, base=0,
                                   pattern=[[1, P]], channel_multiplier=-1).then_inc(tri_ready, 1)
                pool.iota(slots_i[:, :], pattern=[[1, ROUTED]], base=0, channel_multiplier=0).then_inc(iota2, 1)
                pool.iota(p_i[:, :], pattern=[[0, 1]], base=0, channel_multiplier=1).then_inc(iota2, 1)
                pool.iota(t_i[:, :], pattern=[[1, NT]], base=0, channel_multiplier=0).then_inc(iota2, 1)
                pool.wait_ge(token_ready, 1)
                for b in range(B):
                    pool.indirect_dma_start(out=y_rt[:, b, :], out_offset=None, in_=y2rows,
                                            in_offset=bass.IndirectOffsetOnAxis(ap=token[:, b:b + 1], axis=0)).then_inc(rows_in[b], 16)
                for b in range(B):
                    pool.indirect_dma_start(out=base[:, b, :], out_offset=None, in_=out,
                                            in_offset=bass.IndirectOffsetOnAxis(ap=token[:, b:b + 1], axis=0)).then_inc(base_in, 16)
                for b in range(B):
                    pool.wait_ge(fin_ready, b + 1)
                    pool.indirect_dma_start(out=out, out_offset=bass.IndirectOffsetOnAxis(ap=token[:, b:b + 1], axis=0),
                                            in_=fin[:, b, :], in_offset=None).then_inc(fin_out, 16)
                pool.wait_ge(fin_out, 16 * B)

            @block.vector
            def _(dve):
                ch = Chain(dve, dve4)
                level_f = threshold[:, :].bitcast(F32)
                dve.wait_ge(iota2, 3)
                dve.tensor_copy(slots[:, :], slots_i[:, :])
                dve.tensor_copy(facts[:, :, 0], p_i[:, :].broadcast_to([P, NT]))
                dve.tensor_copy(facts[:, :, 1], t_i[:, :])
                dve.tensor_scalar(above[:, :], score[:, :], level_f, None, ALU.is_gt)
                ch.step(dve.tensor_scalar(gain[:, :], score[:, :], -1.0, 1.0, ALU.mult, ALU.add))
                ch.step(dve.tensor_tensor(gain[:, :], gain[:, :], score[:, :], ALU.add))
                ch.step(dve.tensor_copy(facts[:, :, 2], gain[:, :]))
                ch.step(dve.tensor_tensor(facts[:, :, 3], gain[:, :], facts[:, :, 2], ALU.subtract))
                ch.step(dve.tensor_scalar(level[:, :], score[:, :], level_f, None, ALU.is_equal))
                dve.sem_inc(sel_ready, 1)

                def running(n):
                    dve.wait_ge(prefix_ready, n)
                    ch.step(dve.tensor_tensor_scan(run[:, 1:NT], ones[:, 0:NT - 1], ps_w[:, 1, 0:NT - 1], 0.0, ALU.mult, ALU.add))
                    ch.step(dve.tensor_tensor(place[:, :], run[:, :], ps_w[:, 0, :], ALU.add))

                dve.memset(run[:, 0:1], 0.0)
                running(1)
                ch.step(dve.tensor_reduce(n_above[:, :], ps_w[:, 2, :], AX_X, ALU.add))
                ch.step(dve.tensor_scalar(need[:, :], n_above[:, :], -1.0, float(ROUTED), ALU.mult, ALU.add))
                ch.step(dve.tensor_scalar(place[:, :], place[:, :], need[:, :], None, ALU.is_lt))
                ch.step(dve.tensor_tensor(place[:, :], place[:, :], level[:, :], ALU.mult))
                ch.step(dve.tensor_tensor(taken[:, :], place[:, :], above[:, :], ALU.add))
                dve.sem_inc(sel_ready, 1)
                running(2)
                ch.step(dve.tensor_scalar(place[:, :], place[:, :], 1.0, None, ALU.add))
                ch.step(dve.tensor_tensor(place[:, :], place[:, :], taken[:, :], ALU.mult))
                ch.step(dve.tensor_scalar(place[:, :], place[:, :], 1.0, None, ALU.subtract))
                dve.sem_inc(facts_ready, 1)
                dve.sem_inc(hot_used, HOT)
                with dve.Fori(0, NT // HOT) as i:
                    for h in range(HOT):
                        dve.wait_ge(hot_used, i * HOT + (h + 1))
                        dve.tensor_scalar(hot[:, h], slots[:, :], place[:, bass.ds(i * HOT + h, 1)], None, ALU.is_equal
                                          ).then_inc(hot_ready, 1)
                dve.wait_ge(found_ready, 1)
                ch.step(dve.tensor_copy(found[:, :, :], ps_f[:, :, :]))
                ch.step(dve.scalar_tensor_tensor(token_f[:, :], found[:, :, 1], float(P), found[:, :, 0], ALU.mult, ALU.add))
                dve.tensor_tensor(gains[:, :], found[:, :, 2], found[:, :, 3], ALU.add)
                dve.tensor_copy(token[:, :], token_f[:, :]).then_inc(token_ready, 1)
                for b in range(B):
                    dve.wait_ge(r_high, b + 1)
                    dve.tensor_tensor(y_rt_t[:, :, 1, b * P:(b + 1) * P], ps_r[b % 2][:, :, :],
                                      y_rt_t[:, :, 0, b * P:(b + 1) * P], ALU.subtract).then_inc(r_low, 1)
                for c in range(HC):
                    dve.wait_ge(u_act, c + 1)
                    dve.tensor_scalar(g_hl[:, c, 0, :], g32[:, c % 2], YS, None, ALU.mult).then_inc(u_high, 1)
                    dve.wait_ge(u_high, c + 1)
                    dve.scalar_tensor_tensor(g_hl[:, c, 1, :], g32[:, c % 2], YS, g_hl[:, c, 0, :], ALU.mult,
                                             ALU.subtract).then_inc(u_low, 1)
                dve.wait_ge(base_in, 16 * B)
                for b in range(B):
                    dve.wait_ge(d_full, b + 1)
                    dve.scalar_tensor_tensor(fin[:, b], ps_u[b][:, :], 1.0 / ZS, b2h_row[:, :], ALU.mult, ALU.add
                                             ).then_inc(d_read, 1)
                    dve.wait_ge(d_read, b + 1)
                    dve.scalar_tensor_tensor(fin[:, b], fin[:, b], gains[:, b:b + 1], base[:, b], ALU.mult, ALU.add
                                             ).then_inc(fin_ready, 1)

            @block.scalar
            def _(act):
                for b in range(B):
                    act.wait_ge(r_full, b + 1)
                    act.activation(y_rt_t[:, :, 0, b * P:(b + 1) * P], ps_r[b % 2][:, :, :], ACT.Copy).then_inc(r_high, 1)
                for c in range(HC):
                    act.wait_ge(u_full, c + 1)
                    if c >= 2:
                        act.wait_ge(u_low, c - 1)
                    act.activation(g32[:, c % 2], ps_u[c % 4][:, :], ACT.Gelu, bias=b1h_sb[:, c:c + 1], scale=1.0 / ZS
                                   ).then_inc(u_act, 1)

            @block.tensor
            def _(pe):
                pe.wait_ge(tri_ready, 2)
                for n, m in ((1, level), (2, taken)):
                    pe.wait_ge(sel_ready, n)
                    pe.matmul(ps_w[:, 0, :], before[:, :], m[:, :], start=True, stop=True)
                    pe.matmul(ps_w[:, 1, :], ones[:, :], m[:, :], start=True, stop=True)
                    pe.matmul(ps_w[:, 2, :], ones[:, :], above[:, :], start=True, stop=True).then_inc(prefix_ready, 1)
                pe.wait_ge(facts_ready, 1)
                pe.matmul(ps_f[:, :, :].rearrange("p b n -> p (b n)"), keep["ones16"][:, :], keep["zeros"][:, 0:4 * B],
                          start=True, stop=False, skip_group_check=True)
                with pe.Fori(0, NT // HOT) as i:
                    for h in range(HOT):
                        pe.wait_ge(hot_ready, i * HOT + (h + 1))
                        for b in range(B):
                            last = pe.matmul(ps_f[:, b, :], hot[:, h, b * P:(b + 1) * P],
                                             facts[:, bass.ds(i * HOT + h, 1), :].rearrange("p a n -> p (a n)"),
                                             start=False, stop=False, skip_group_check=True)
                        last.then_inc(hot_used, 1)
                pe.matmul(ps_f[:, 0, 0:1], keep["ones16"][:, :], keep["zeros"][:, 0:1], start=False, stop=True,
                          skip_group_check=True).then_inc(found_ready, 1)
                for b in range(B):
                    pe.wait_ge(rows_in[b], 16)
                    if b >= 2:
                        pe.wait_ge(r_low, b - 1)
                    for k in range(KC):
                        last = pe.transpose(ps_r[b % 2][:, k, :], y_rt[:, b, k * P:(k + 1) * P], keep["ident"][:, :])
                    last.then_inc(r_full, 1)
                pe.wait_ge(r_low, B)
                for c in range(HC):
                    if c >= 4:
                        pe.wait_ge(u_act, c - 3)
                    for k in range(KC):
                        for e, f in PASSES:
                            last = pe.matmul(ps_u[c % 4][:, :], w1h_sb[:, k, e, c * P:(c + 1) * P], y_rt_t[:, k, f, :],
                                             start=(k == 0 and e + f == 0), stop=(k == KC - 1 and e == 1))
                    last.then_inc(u_full, 1)
                pe.wait_ge(u_low, HC)
                pe.wait_ge(u_act, HC)
                for b in range(B):
                    for c in range(HC):
                        for e, f in PASSES:
                            last = pe.matmul(ps_u[b][:, :], g_hl[:, c, e, b * P:(b + 1) * P], w2h_sb[:, c // 4, f, c % 4, :],
                                             start=(c == 0 and e + f == 0), stop=(c == HC - 1 and e == 1))
                    last.then_inc(d_full, 1)


_INS = ["x", "adj", "adj_t", "L0_gnn_W_q", "L0_gnn_b_q", "L0_gnn_W_k", "L0_gnn_b_k", "L0_gnn_W_v_t", "L0_gnn_b_v",
        "L0_ffn_routing_token", "L0_ffn_gamma_light", "L0_ffn_w1_light", "L0_ffn_b1_light", "L0_ffn_w2_light",
        "L0_ffn_b2_light", "L0_ffn_gamma_heavy", "L0_ffn_w1_heavy", "L0_ffn_b1_heavy", "L0_ffn_w2_heavy",
        "L0_ffn_b2_heavy"]


def build(nc, shapes):
    args = [nc.dram_tensor(f"in_{n}", tuple(shapes[n]), F32, kind="ExternalInput").ap() for n in _INS]
    args.append(nc.dram_tensor("out_0", (N, D), F32, kind="ExternalOutput").ap())
    gnn_ffn_kernel(nc, *args)


def kernel(**inputs):
    import concourse.bacc as _bacc
    from concourse.bass_utils import run_bass_kernel_spmd as _run

    inputs = {k: np.asarray(v) for k, v in inputs.items()}
    inputs["adj_t"] = inputs["adj"].T
    inputs["L0_gnn_W_v_t"] = inputs["L0_gnn_W_v"].T
    arrays = {f"in_{n}": np.ascontiguousarray(inputs[n]) for n in _INS}
    nc = _bacc.Bacc("TRN2", target_bir_lowering=False, num_devices=1)
    build(nc, {n: inputs[n].shape for n in _INS})
    r = _run(nc, [arrays], core_ids=[0])
    return r.results[0]["out_0"]
```

```python
from contextlib import ExitStack

import numpy as np

import concourse.bass as bass
from concourse import mybir

ALU = mybir.AluOpType
ACT = mybir.ActivationFunctionType
AX_X = mybir.AxisListType.X
F32 = mybir.dt.float32
F16 = mybir.dt.float16
I32 = mybir.dt.int32
U32 = mybir.dt.uint32

P = 128
N = 4096
D = 512
HL = 256
HH = 2048
ROUTED = 512
NT = N // P
KC = D // P
GROUP = 4
NG = NT // GROUP
YS = 64.0
MS = 1024.0
ZS = YS * YS
SCALE = 1.0 / (ZS * float(np.sqrt(D)))
MASKED = -10000.0 / SCALE
PS = 4096.0
EPS_LN = 1e-5


class Chain:

    def __init__(self, eng, sem):
        self.eng, self.sem, self.n, self.base = eng, sem, 0, 0

    def step(self, ins):
        self.n += 1
        ins.then_inc(self.sem, 1)
        self.eng.wait_ge(self.sem, self.base + self.n)


class Semaphores:

    def __init__(self, nc):
        self.nc, self.held = nc, []

    def __call__(self, name):
        self.held.append(self.nc.alloc_semaphore(name=name))
        return self.held[-1]

    def done(self):
        self.nc.all_engine_barrier()
        self.nc.clear_and_free_semaphores([h for h in self.held])
        self.nc.all_engine_barrier()
        self.held = []


def gnn_ffn_kernel(nc, x, adj, adj_t, wq, bq, wk, bk, wv_t, bv, rtok, gl, w1l, b1l, w2l, b2l,
                   gh, w1h, b1h, w2h, b2h, out):
    ytab = nc.dram_tensor("ytab", (N, 2 * D), F16).ap()
    qtab = nc.dram_tensor("qtab", (NT, P, KC * 2 * P), F16).ap()
    x1tab = nc.dram_tensor("x1tab", (N, D), F32).ap()
    y2ttab = nc.dram_tensor("y2ttab", (NT, P, KC * 2 * P), F16).ap()
    with ExitStack() as ctx:
        def sb(name, shape, dt, c=ctx):
            return c.enter_context(nc.sbuf_tensor(name, shape, dt))

        keep = {
            "cs": sb("cs", [P, NT], F32), "bvb": sb("bvb", [P, D], F32),
            "wv": sb("wv", [P, KC, 2, D], F16), "ident": sb("ident", [P, P], F32),
            "zeros": sb("zeros", [P, D], F16), "ident16": sb("ident16", [P, P], F16), "s": sb("s", [P, NT], F32),
            "index": sb("index", [P, NT, 2, CH], I32),
            "overflow": sb("overflow", [P, 1], I32), "nz": sb("nz", [P, NT, NT], F32), "ytot": sb("ytot", [P, D], F32), "ones16": sb("ones16", [P, P], F16),
            "ramp": sb("ramp", [P, SEG // P], I32), "part": sb("part", [P, 1], I32), "tile_no": sb("tile_no", [P, NT], I32),
            "place_i": sb("place_i", [P, SEG], I32), "ones": sb("ones_f", [P, P], F32),
            "w1l": sb("w1l_hl", [P, 2, KC, HL], F16), "w2l": sb("w2l_hl", [P, 2, HL // P, D], F16),
            "b1l": sb("b1l_sb", [P, HL // P], F32), "b1h": sb("b1h_sb", [P, HH // P], F32),
            "b2l": sb("b2l_row", [P, D], F32), "b2h": sb("b2h_row", [P, D], F32), "gain_h": sb("gain_h", [P, KC], F32),
        }
        sem = Semaphores(nc)
        split_weights(nc, keep, wk=wk, wq=wq, bq=bq, bk=bk, wv_t=wv_t, bv=bv, gl=gl, w1l=w1l, w2l=w2l,
                      gh=gh, b1l=b1l, b2l=b2l, b1h=b1h, b2h=b2h, sem=sem, x=x, ytab=ytab, qtab=qtab, adj_t=adj_t)
        sem.done()
        overflow = nc.values_load(keep["overflow"][0:1, 0:1], min_val=0, max_val=P)
        with nc.If(overflow == 0):
            attend_listed(nc, keep, x, adj_t, rtok, ytab, qtab, x1tab, y2ttab, sem)
        sem.done()
        with nc.If(overflow > 0):
            attend_all(nc, keep, x, adj, rtok, ytab, qtab, x1tab, y2ttab, sem)
        sem.done()
        feed_forward(nc, keep, y2ttab, x1tab, w1h, w2h, out, sem)


def split_weights(nc, keep, wk, wq, bq, bk, wv_t, bv, gl, w1l, w2l, gh, b1l, b2l, b1h, b2h, sem, x, ytab, qtab, adj_t):
    with ExitStack() as ctx:
        def sb(name, shape, dt):
            return ctx.enter_context(nc.sbuf_tensor(name, shape, dt))

        def pb(name, shape, dt):
            return ctx.enter_context(nc.psum_tensor(name, shape, dt))

        xg = sb("xg", [P, 2, GROUP, D], F32)
        adj_sb = sb("adj_sb", [P, GROUP, N], F32)
        x_in, adj_in = [sem("x_in0"), sem("x_in1")], [sem(f"adj_in{s}") for s in range(GROUP)]
        m_hl = sb("m_hl", [P, KC, 2, D], F16)
        u_hl = sb("u_hl", [P, KC, 2], F16)
        w64 = sb("w64", [P, KC], F32)
        c0 = sb("c0", [P, 1], F32)
        zeros = keep["zeros"]

        loaded_v, loaded_b = sem("loaded_v"), sem("loaded_b")
        loaded_qk, consts = sem("loaded_qk"), sem("consts")
        light_in, light_scaled, light_high = sem("light_in"), sem("light_scaled"), sem("light_high")
        bq_ready, m_ready, m_copied, vec_ready, dve0 = sem("bq_ready"), sem("m_ready"), sem("m_copied"), sem("vec_ready"), sem("dve0")
        m_done = sem("m_done")
        pool0, wv_scaled, wv_high = sem("pool0"), sem("wv_scaled"), sem("wv_high")

        with ExitStack() as pctx:
            def tmp(name, shape, dt):
                return pctx.enter_context(nc.sbuf_tensor(name, shape, dt))

            wq_sb, wk_sb = tmp("wq_sb", [P, KC, D], F32), tmp("wk_sb", [P, KC, D], F32)
            wv_sb = tmp("wv_sb", [P, KC, D], F32)
            bq_sb, bk_sb = tmp("bq_sb", [P, KC], F32), tmp("bk_sb", [P, KC], F32)
            bq_wide = tmp("bq_wide", [P, KC, P], F32)
            gl_sb, gh_sb = tmp("gl_sb", [P, KC], F32), tmp("gh_sb", [P, KC], F32)
            gain_l = tmp("gain_l", [P, KC], F32)
            w1l_raw, w2l_raw = tmp("w1l_raw", [P, KC, HL], F32), tmp("w2l_raw", [P, HL // P, D], F32)
            m32 = tmp("m32", [P, 2, D], F32)
            u32 = tmp("u32", [P, KC], F32)
            ps_m = [pctx.enter_context(nc.psum_tensor(f"ps_m{i}", [P, D], F32)) for i in range(2)]
            ps_v = pctx.enter_context(nc.psum_tensor("ps_v", [P, 16], F32))
            with nc.Block() as block:
                @block.sync
                def _(sp):
                    sp.dma_start(wq_sb[:, :, :], wq.rearrange("(c p) k -> p c k", p=P)).then_inc(loaded_qk, 16)
                    sp.dma_start(wk_sb[:, :, :], wk.rearrange("(c p) k -> p c k", p=P)).then_inc(loaded_qk, 16)
                    for t, s in ((bq_sb, bq), (bk_sb, bk), (gl_sb, gl), (gh_sb, gh)):
                        sp.dma_start(t[:, :], s.rearrange("(c p) -> p c", p=P),
                                     allow_slow_non_contiguous=True).then_inc(loaded_b, 16)
                    sp.dma_start(wv_sb[:, :, :], wv_t.rearrange("(c p) k -> p c k", p=P)).then_inc(loaded_v, 16)
                    sp.dma_start(keep["bvb"][:, :], bv.partition_broadcast(P)).then_inc(loaded_v, 16)
                    for t, s in ((keep["b1l"], b1l), (keep["b1h"], b1h)):
                        sp.dma_start(t[:, :], s.rearrange("(c p) -> p c", p=P),
                                     allow_slow_non_contiguous=True).then_inc(loaded_v, 16)
                    for t, s in ((keep["b2l"], b2l), (keep["b2h"], b2h)):
                        sp.dma_start(t[:, :], s.partition_broadcast(P)).then_inc(loaded_v, 16)
                    sp.dma_start(w1l_raw[:, :, :], w1l.rearrange("(c p) n -> p c n", p=P)).then_inc(light_in, 16)
                    sp.dma_start(w2l_raw[:, :, :], w2l.rearrange("(c p) n -> p c n", p=P)).then_inc(light_in, 16)
                    for g in range(2):
                        sp.dma_start(xg[:, g], x[g * GROUP * P:(g + 1) * GROUP * P, :].rearrange("(s p) d -> p s d", p=P)
                                     ).then_inc(x_in[g], 16)
                    for s in range(GROUP):
                        sp.dma_start(adj_sb[:, s], adj_t[s * P:(s + 1) * P, :]).then_inc(adj_in[s], 16)

                @block.gpsimd
                def _(pool):
                    ch = Chain(pool, pool0)
                    ch.step(pool.memset(keep["ident"][:, :], 0.0))
                    pool.affine_select(out=keep["ident"][:, :], in_=keep["ident"][:, :], compare_op=ALU.not_equal,
                                       fill=1.0, base=0, pattern=[[-1, P]], channel_multiplier=1).then_inc(consts, 1)
                    pool.wait_ge(consts, 1)
                    pool.tensor_copy(keep["ident16"][:, :], keep["ident"][:, :])
                    pool.memset(keep["ones16"][:, :], 1.0).then_inc(consts, 1)
                    pool.memset(zeros[:, :], 0.0).then_inc(consts, 1)
                    pool.iota(keep["ramp"][:, :], pattern=[[P, SEG // P]], base=0, channel_multiplier=0).then_inc(consts, 1)
                    pool.iota(keep["part"][:, :], pattern=[[0, 1]], base=0, channel_multiplier=1).then_inc(consts, 1)
                    pool.iota(keep["tile_no"][:, :], pattern=[[1, NT]], base=0, channel_multiplier=0).then_inc(consts, 1)
                    pool.iota(keep["place_i"][:, :], pattern=[[-1, SEG]], base=SEG, channel_multiplier=0).then_inc(consts, 1)
                    pool.memset(keep["ones"][:, :], 1.0).then_inc(consts, 1)

                @block.vector
                def _(dve):
                    ch = Chain(dve, dve0)
                    dve.wait_ge(loaded_b, 64)
                    dve.tensor_copy(bq_wide[:, :, :], bq_sb[:, :].unsqueeze(2).broadcast_to([P, KC, P])).then_inc(bq_ready, 1)
                    dve.tensor_scalar(keep["gain_h"][:, :], gh_sb[:, :], YS, None, ALU.mult)
                    ch.step(dve.tensor_scalar(gain_l[:, :], gl_sb[:, :], YS, None, ALU.mult))
                    dve.wait_ge(loaded_v, 96)
                    dve.tensor_scalar(wv_sb[:, :, :], wv_sb[:, :, :], YS, None, ALU.mult).then_inc(wv_scaled, 1)
                    dve.wait_ge(light_in, 32)
                    for kc in range(KC):
                        dve.tensor_scalar(w1l_raw[:, kc, :], w1l_raw[:, kc, :], gain_l[:, kc:kc + 1], None, ALU.mult)
                    dve.tensor_scalar(w2l_raw[:, :, :], w2l_raw[:, :, :], YS, None, ALU.mult).then_inc(light_scaled, 1)
                    dve.wait_ge(wv_high, 1)
                    dve.tensor_tensor(keep["wv"][:, :, 1, :], wv_sb[:, :, :], keep["wv"][:, :, 0, :], ALU.subtract)
                    dve.wait_ge(light_high, 2)
                    dve.tensor_tensor(keep["w1l"][:, 1], w1l_raw[:, :, :], keep["w1l"][:, 0], ALU.subtract)
                    dve.tensor_tensor(keep["w2l"][:, 1], w2l_raw[:, :, :], keep["w2l"][:, 0], ALU.subtract)
                    for kc in range(KC):
                        dve.wait_ge(m_copied, 2 * kc + 2)
                        dve.tensor_tensor(m_hl[:, kc, 1, :], m32[:, kc % 2, :], m_hl[:, kc, 0, :],
                                          ALU.subtract).then_inc(m_ready, 1)
                    dve.wait_ge(vec_ready, 1)
                    dve.tensor_scalar(w64[:, :], ps_v[:, 4:8], YS, None, ALU.mult)
                    dve.tensor_scalar(c0[:, :], ps_v[:, 8:9], ZS, None, ALU.mult)
                    ch.step(dve.tensor_scalar(u32[:, :], ps_v[:, 0:4], MS, None, ALU.mult))
                    ch.step(dve.tensor_copy(u_hl[:, :, 0], u32[:, :]))
                    ch.step(dve.tensor_tensor(u_hl[:, :, 1], u32[:, :], u_hl[:, :, 0], ALU.subtract))

                @block.scalar
                def _(act):
                    def leave_m(kc):
                        act.wait_ge(m_done, kc + 1)
                        if kc >= 2:
                            act.wait_ge(m_ready, kc - 1)
                        act.activation(m32[:, kc % 2, :], ps_m[kc % 2][:, :], ACT.Copy, scale=MS).then_inc(m_copied, 1)
                        act.wait_ge(m_copied, 2 * kc + 1)
                        act.activation(m_hl[:, kc, 0, :], m32[:, kc % 2, :], ACT.Copy).then_inc(m_copied, 1)

                    leave_m(0)
                    leave_m(1)
                    act.wait_ge(wv_scaled, 1)
                    act.activation(keep["wv"][:, :, 0, :], wv_sb[:, :, :], ACT.Copy).then_inc(wv_high, 1)
                    act.wait_ge(light_scaled, 1)
                    act.activation(keep["w1l"][:, 0], w1l_raw[:, :, :], ACT.Copy).then_inc(light_high, 1)
                    act.activation(keep["w2l"][:, 0], w2l_raw[:, :, :], ACT.Copy).then_inc(light_high, 1)
                    leave_m(2)
                    leave_m(3)

                @block.tensor
                def _(pe):
                    pe.wait_ge(loaded_qk, 32)
                    for kc in range(KC):
                        if kc >= 2:
                            pe.wait_ge(m_copied, 2 * (kc - 1))
                        for d in range(KC):
                            last = pe.matmul(ps_m[kc % 2][:, :], wq_sb[:, d, kc * P:(kc + 1) * P], wk_sb[:, d, :],
                                             start=(d == 0), stop=(d == KC - 1))
                        last.then_inc(m_done, 1)
                    pe.wait_ge(loaded_b, 64)
                    pe.wait_ge(bq_ready, 1)
                    for kc in range(KC):
                        for d in range(KC):
                            pe.matmul(ps_v[:, kc:kc + 1], wq_sb[:, d, kc * P:(kc + 1) * P], bk_sb[:, d:d + 1],
                                      start=(d == 0), stop=(d == KC - 1))
                        for d in range(KC):
                            pe.matmul(ps_v[:, 4 + kc:5 + kc], wk_sb[:, d, kc * P:(kc + 1) * P], bq_sb[:, d:d + 1],
                                      start=(d == 0), stop=(d == KC - 1))
                    for d in range(KC):
                        last = pe.matmul(ps_v[:, 8:9], bq_wide[:, d, :], bk_sb[:, d:d + 1], start=(d == 0), stop=(d == KC - 1))
                    last.then_inc(vec_ready, 1)
        project_queries(nc, keep, m_hl, u_hl, w64, c0, zeros, x, xg, x_in, ytab, qtab, adj_t, adj_sb, adj_in, sem)


def project_queries(nc, keep, m_hl, u_hl, w64, c0, zeros, x, xg, x_in, ytab, qtab, adj_t, adj_sb, adj_in, sem):
    x_groups = x.rearrange("(g s p) d -> g p s d", s=GROUP, p=P)
    ytab_g = ytab.rearrange("(g s p) d -> g p s d", s=GROUP, p=P)
    qtab_g = qtab.rearrange("(g s) p n -> g p s n", s=GROUP)
    with ExitStack() as ctx:
        def sb(name, shape, dt):
            return ctx.enter_context(nc.sbuf_tensor(name, shape, dt))

        stats = sb("stats", [P, 2, GROUP, 6], F32)
        mv = sb("mv", [P, 2, GROUP, 2], F32)
        half_pow = sb("half_pow", [P, 1], F32)
        var_eps = sb("var_eps", [P, 2, GROUP], F32)
        rstd = sb("rstd", [P, 2, GROUP], F32)
        y32 = sb("y32", [P, 2, GROUP, D], F32)
        y_rows = sb("y_rows", [P, 2, GROUP, 2, D], F16)
        y_t = sb("y_t", [P, 2, KC, 2, GROUP * P], F16)
        q32 = sb("q32", [P, 2, D], F32)
        q_hl = sb("q_hl", [P, 2, GROUP, KC, 2, P], F16)
        ps_t = [ctx.enter_context(nc.psum_tensor(f"ps_t{i}", [P, KC, P], F32)) for i in range(2)]
        ps_q = [ctx.enter_context(nc.psum_tensor(f"ps_q{i}", [P, GROUP * P], F32)) for i in range(2)]
        ps_c = [ctx.enter_context(nc.psum_tensor(f"ps_c{i}", [P, GROUP, 2], F32)) for i in range(2)]
        ps_y = ctx.enter_context(nc.psum_tensor("ps_y", [P, D], F32))

        c_part = sb("c_part", [P, 2, GROUP], F32)
        adj_t_tiles = adj_t.rearrange("(c p) i -> c p i", p=P)

        passed_dve, passed_act = sem("passed_dve"), sem("passed_act")
        xg_used, scanned, rows_free, y32_free = sem("xg_used"), sem("scanned"), sem("rows_free"), sem("y32_free")
        rows_high, q_high = sem("rows_high"), sem("q_high")
        pow_ready = sem("pow_ready")
        dve1 = sem("dve1")
        var_ready, rstd_ready, y_ready, rows_ready = sem("var_ready"), sem("rstd_ready"), sem("y_ready"), sem("rows_ready")
        rows_out, q_out = [sem("rows_out0"), sem("rows_out1")], [sem("q_out0"), sem("q_out1")]
        t_ready, t_high, t_low = sem("t_ready"), sem("t_high"), sem("t_low")
        q_ready, q_biased, q_split = sem("q_ready"), sem("q_biased"), sem("q_split")
        c_ready, c_read = sem("c_ready"), sem("c_read")
        summed = sem("summed")
        HALVES = NG // 2
        lists = NeighbourLists(nc, keep, sb, sem, adj_sb[:, 0], ps_t, ps_c[0][:, 0, 0:1])

        with nc.Block() as block:
            @block.sync
            def _(sp):
                def load_x(g):
                    sp.wait_ge(xg_used, g - 1)
                    sp.dma_start(xg[:, h], x_groups[bass.ds(g, 1)].rearrange("a p s d -> p (a s) d")).then_inc(x_in[h], 16)

                def load_adjacency(g):
                    for s in range(GROUP):
                        sp.wait_ge(scanned, g * GROUP - GROUP + (s + 1))
                        sp.dma_start(adj_sb[:, s], adj_t_tiles[bass.ds(g * GROUP + s, 1)].rearrange("a p i -> p (a i)")
                                     ).then_inc(adj_in[s], 16)

                with sp.Fori(0, HALVES - 1) as i:
                    for h in range(2):
                        load_x(i * 2 + (2 + h))
                        load_adjacency(i * 2 + (1 + h))
                load_adjacency(NG - 1)
                sp.sem_inc(x_in[0], 16)
                for h in range(2):
                    sp.wait_ge(rows_out[h], 16 * (HALVES + 1))
                    sp.wait_ge(q_out[h], 16 * (HALVES + 1))

            @block.gpsimd
            def _(pool):
                pool.memset(half_pow[:, :], -0.5).then_inc(pow_ready, 1)
                pool.wait_ge(pow_ready, 1)
                def power(g, h):
                    pool.wait_ge(var_ready, g + 1)
                    pool.tensor_tensor(rstd[:, h], var_eps[:, h], half_pow[:, :].broadcast_to([P, GROUP]),
                                       ALU.pow).then_inc(rstd_ready, 1)

                power(0, 0)
                with pool.Fori(0, HALVES) as i:
                    for h in range(2):
                        g = i * 2 + h
                        pool.wait_ge(rows_high, g + 1)
                        pool.tensor_tensor(y_rows[:, h, :, 1, :], y32[:, h], y_rows[:, h, :, 0, :],
                                           ALU.subtract).then_inc(rows_ready, 1)
                        pool.wait_ge(rows_ready, g + 1)
                        pool.sem_inc(y32_free, 1)
                        power(g + 1, 1 - h)
                        for k in range(KC):
                            pool.wait_ge(q_high, g * KC + (k + 1))
                            pool.tensor_tensor(q_hl[:, h, :, k, 1, :], q32[:, k % 2].rearrange("p (s t) -> p s t", s=GROUP),
                                               q_hl[:, h, :, k, 0, :], ALU.subtract).then_inc(q_split, 1)

            @block.vector
            def _(dve):
                ch = Chain(dve, dve1)
                dve.sem_inc(y32_free, 2)
                def scan(g, s):
                    dve.wait_ge(adj_in[s], g * 16 + 16)
                    dve.tensor_reduce(keep["nz"][:, bass.ds(g * GROUP + s, 1), :].rearrange("p a t -> p (a t)"),
                                      adj_sb[:, s].rearrange("p (t i) -> p t i", i=P), AX_X, ALU.max,
                                      apply_absolute_value=True).then_inc(scanned, 1)

                def statistics(g, h):
                    dve.wait_ge(x_in[h], g // 2 * 16 + 16 if isinstance(g, int) else g * 8 + (16 - 8 * h))
                    for s in range(GROUP):
                        last = dve.bn_stats(stats[:, h, s], xg[:, h, s])
                    ch.step(last)
                    dve.sem_inc(passed_dve, 1)
                    for s in range(GROUP):
                        last = dve.bn_aggr(mv[:, h, s], stats[:, h, s])
                    ch.step(last)
                    dve.tensor_scalar(var_eps[:, h], mv[:, h, :, 1], EPS_LN, 1.0 / (YS * YS), ALU.add,
                                      ALU.mult).then_inc(var_ready, 1)

                statistics(0, 0)
                with dve.Fori(0, HALVES) as i:
                    for h in range(2):
                        g = i * 2 + h
                        ch.base, ch.n = i * (2 * 3) + 2, 3 * h
                        dve.wait_ge(rstd_ready, g + 1)
                        dve.wait_ge(y32_free, g + 1)
                        for s in range(GROUP):
                            last = dve.tensor_scalar(y32[:, h, s], xg[:, h, s], mv[:, h, s, 0:1], rstd[:, h, s:s + 1],
                                                     ALU.subtract, ALU.mult)
                            last.then_inc(y_ready, 1)
                        dve.wait_ge(y_ready, g * GROUP + GROUP)
                        dve.sem_inc(xg_used, 1)
                        scan(g, 0)
                        statistics(g + 1, 1 - h)
                        for s in range(GROUP):
                            if s % 2 == 0:
                                scan(g, 1 + s // 2)
                            dve.wait_ge(t_high, g * GROUP + (s + 1))
                            dve.tensor_tensor(y_t[:, h, :, 1, s * P:(s + 1) * P], ps_t[s % 2][:, :, :],
                                              y_t[:, h, :, 0, s * P:(s + 1) * P], ALU.subtract).then_inc(t_low, 1)
                        scan(g, 3)
                        dve.wait_ge(c_ready, g + 1)
                        ch.step(dve.tensor_scalar(c_part[:, h], ps_c[h][:, :, 0], ZS / (YS * MS), c0[:, 0:1], ALU.mult, ALU.add))
                        dve.scalar_tensor_tensor(keep["cs"][:, bass.ds(g * GROUP, GROUP)], ps_c[h][:, :, 1], ZS / (YS * MS),
                                                 c_part[:, h], ALU.mult, ALU.add).then_inc(c_read, 1)
                lists.on_vector(dve)
                dve.wait_ge(summed, 1)
                dve.tensor_copy(keep["ytot"][:, :], ps_y[:, :])

            @block.scalar
            def _(act):
                act.sem_inc(rows_free, 2)
                for h in range(2):
                    act.sem_inc(q_out[h], 16)
                    act.sem_inc(rows_out[h], 16)
                with act.Fori(0, HALVES) as i:
                    for h in range(2):
                        g = i * 2 + h
                        act.wait_ge(rows_free, g + 1)
                        act.wait_ge(rows_out[h], i * 16 + 16)
                        act.wait_ge(y_ready, g * GROUP + GROUP)
                        act.activation(y_rows[:, h, :, 0, :], y32[:, h], ACT.Copy).then_inc(rows_high, 1)
                        for s in range(GROUP):
                            act.wait_ge(t_ready, g * GROUP + (s + 1))
                            act.activation(y_t[:, h, :, 0, s * P:(s + 1) * P], ps_t[s % 2][:, :, :], ACT.Copy).then_inc(t_high, 1)
                        act.wait_ge(rows_ready, g + 1)
                        act.sem_inc(passed_act, 1)
                        act.dma_start(ytab_g[bass.ds(g, 1)].rearrange("a p s d -> p (a s) d"),
                                      y_rows[:, h].rearrange("p s e d -> p s (e d)")).then_inc(rows_out[h], 16)
                        act.wait_ge(q_out[h], i * 16 + 16)
                        for k in range(KC):
                            act.wait_ge(q_ready, g * KC + (k + 1))
                            if k >= 2:
                                act.wait_ge(q_split, g * KC + (k - 1))
                            act.activation(q32[:, k % 2], ps_q[k % 2][:, :], ACT.Identity, bias=w64[:, k:k + 1],
                                           scale=1.0 / MS).then_inc(q_biased, 1)
                            act.wait_ge(q_biased, g * KC + (k + 1))
                            act.activation(q_hl[:, h, :, k, 0, :], q32[:, k % 2].rearrange("p (s t) -> p s t", s=GROUP),
                                           ACT.Copy).then_inc(q_high, 1)
                        act.wait_ge(q_split, g * KC + KC)
                        act.sem_inc(passed_act, 1)
                        act.dma_start(qtab_g[bass.ds(g, 1)].rearrange("a p s n -> p (a s) n"),
                                      q_hl[:, h].rearrange("p s k e t -> p s (k e t)")).then_inc(q_out[h], 16)

            @block.tensor
            def _(pe):
                pe.matmul(ps_y[:, :], keep["ones16"][:, :], zeros[:, :], start=True, stop=False, skip_group_check=True)
                def group(g, h, last_one=False):
                    for s in range(GROUP):
                        pe.wait_ge(y_ready, g * GROUP + (s + 1))
                        if s >= 2:
                            pe.wait_ge(t_low, g * GROUP + (s - 1))
                        for k in range(KC):
                            last = pe.transpose(ps_t[s % 2][:, k, :], y32[:, h, s, k * P:(k + 1) * P], keep["ident"][:, :])
                        last.then_inc(t_ready, 1)
                    pe.wait_ge(t_low, g * GROUP + GROUP)
                    for s in range(GROUP):
                        for k in range(KC):
                            pe.matmul(ps_c[h][:, s, :], y_t[:, h, k, 0, s * P:(s + 1) * P], u_hl[:, k, :],
                                      start=(k == 0), stop=False, skip_group_check=True)
                            last = pe.matmul(ps_c[h][:, s, 0:1], y_t[:, h, k, 1, s * P:(s + 1) * P], u_hl[:, k, 0:1],
                                             start=False, stop=(k == KC - 1), skip_group_check=True)
                    last.then_inc(c_ready, 1)
                    pe.wait_ge(rows_ready, g + 1)
                    for s in range(GROUP):
                        for e in range(2):
                            last = pe.matmul(ps_y[:, :], keep["ones16"][:, :], y_rows[:, h, s, e, :], start=False,
                                             stop=False, skip_group_check=True)
                    last.then_inc(rows_free, 1)
                    if last_one:
                        pe.matmul(ps_y[0:P, 0:1], keep["ones16"][:, :], zeros[:, 0:1], start=False, stop=True,
                                  skip_group_check=True).then_inc(summed, 1)
                        lists.keys_on_tensor(pe)
                    for k in range(KC):
                        if k >= 2:
                            pe.wait_ge(q_biased, g * KC + (k - 1))
                        for c in range(KC):
                            for a, b in ((0, 0), (0, 1), (1, 0)):
                                last = pe.matmul(ps_q[k % 2][:, :], m_hl[:, c, a, k * P:(k + 1) * P], y_t[:, h, c, b, :],
                                                 start=(c == 0 and a == 0 and b == 0), stop=(c == KC - 1 and a == 1))
                        last.then_inc(q_ready, 1)
                    pe.wait_ge(q_biased, g * KC + KC)
                    pe.wait_ge(c_read, g + 1)

                with pe.Fori(0, HALVES - 1) as i:
                    for h in range(2):
                        group(i * 2 + h, h)
                group(NG - 2, 0)
                group(NG - 1, 1, last_one=True)
                lists.overflow_on_tensor(pe)


SEGS = 4
SEG = N // SEGS
SLOTS = 160
CH = SEGS * SLOTS // P
LISTED = CH * P
RING = 4


EVEN = 1024


def window(rank):
    p = 1.0 - (1.0 - 1.0 / EVEN) ** P
    spread = 5.0 * np.sqrt(1.0 - p) / p
    lo, hi = rank / p - spread * np.sqrt(rank), (rank + 8) / p + spread * np.sqrt(rank + 8)
    return max(0, int(lo)), min(SEG, int(hi) + 1)


class NeighbourLists:

    def __init__(self, nc, keep, sb, sem, spare, ps_keys, ps_over):
        self.keep, self.ps_keys, self.ps_over = keep, ps_keys, ps_over
        self.has = spare[:, 0:SEG].rearrange("p (r s t) -> p r s t", r=SEG // P, s=SEGS)
        self.keys, self.unlisted, self.place_f = (spare[:, n * SEG:(n + 1) * SEG] for n in (1, 2, 3))
        self.ramp_f, self.part_f = sb("ramp_f", [P, SEG // P], F32), sb("part_f", [P, 1], F32)
        self.local, self.free = sb("local", [P, SEG // P], F32), sb("free", [P, 8], F32)
        self.pad, self.listed, self.turned = (sb(n, [P, SLOTS], F32) for n in ("pad", "listed", "turned"))
        self.left, self.seg_base = sb("left", [P, 8], F32), sb("seg_base", [P, 1], F32)
        self.tile_f, self.seg_i = sb("tile_f", [P, NT], F32), sb("seg_i", [P, 1], I32)
        self.source, self.row = sb("source", [P, CH, NT], F32), sb("row", [P, CH, NT], F32)
        self.over = sb("over", [P, 1], F32)
        self.dve2, self.key_ready, self.key_turned = sem("dve2"), sem("key_ready"), sem("key_turned")
        self.over_ready, self.over_sum = sem("over_ready"), sem("over_sum")

    def on_vector(self, dve):
        keep, part, tile_no, ramp, place_i = self.keep, self.keep["part"], self.keep["tile_no"], self.keep["ramp"], self.keep["place_i"]
        ramp_f, part_f, local, free, pad, listed, turned = (
            self.ramp_f, self.part_f, self.local, self.free, self.pad, self.listed, self.turned)
        left, seg_base, tile_f, seg_i, source, row, over = (
            self.left, self.seg_base, self.tile_f, self.seg_i, self.source, self.row, self.over)
        has, keys, unlisted, place_f, ps, ps_over = self.has, self.keys, self.unlisted, self.place_f, self.ps_keys, self.ps_over
        key_ready, key_turned, over_ready, over_sum = self.key_ready, self.key_turned, self.over_ready, self.over_sum
        ch = Chain(dve, self.dve2)
        dve.tensor_copy(part_f[:, :], part[:, :])
        dve.tensor_copy(tile_f[:, :], tile_no[:, :])
        dve.tensor_scalar(seg_i[:, :], part[:, :], 5, None, ALU.logical_shift_right)
        ch.step(dve.tensor_copy(ramp_f[:, :], ramp[:, :]))
        ch.step(dve.tensor_scalar(local[:, :], ramp_f[:, :], part_f[:, 0:1], -1.0, ALU.add, ALU.mult))
        ch.step(dve.tensor_copy(seg_base[:, :], seg_i[:, :]))
        ch.step(dve.tensor_scalar(seg_base[:, :], seg_base[:, :], 1.0, float(SEG), ALU.add, ALU.mult))
        ch.step(dve.tensor_scalar(local[:, :], local[:, :], float(SEG), None, ALU.add))
        for r in range(SEG // P):
            last = dve.tensor_scalar(has[:, r], keep["nz"][:, r::SEG // P, :], 0.0, local[:, r:r + 1], ALU.not_equal, ALU.mult)
        last.then_inc(key_ready, 1)
        dve.tensor_copy(place_f, place_i[:, :])
        for b in range(2):
            dve.wait_ge(key_turned, b + 1)
            last = dve.tensor_copy(keys[:, b * 512:(b + 1) * 512], ps[b][:, :, :].rearrange("p a j -> p (a j)"))
        ch.step(last)
        ch.step(dve.scalar_tensor_tensor(unlisted, keys, 0.0, place_f, ALU.is_equal, ALU.mult))
        ch.step(dve.max(free[:, :], unlisted))
        for n in range(SLOTS // 8):
            lo, hi = window(8 * n)
            ch.step(dve.max(listed[:, 8 * n:8 * n + 8], keys[:, lo:hi]))
            ch.step(dve.match_replace(keys[:, lo:hi], listed[:, 8 * n:8 * n + 8], keys[:, lo:hi], 0.0))
        ch.step(dve.max(left[:, :], keys))
        dve.tensor_scalar(over[:, :], left[:, 0:1], 0.0, None, ALU.is_gt).then_inc(over_ready, 1)
        ch.step(dve.tensor_scalar(pad[:, :], listed[:, :], 0.0, free[:, 0:1], ALU.is_equal, ALU.mult))
        ch.step(dve.tensor_tensor(listed[:, :], listed[:, :], pad[:, :], ALU.add))
        ch.step(dve.transpose(turned[:, :], listed[:, :]))
        tv = turned[:, :].rearrange("p (c t) -> p c t", c=CH)
        ch.step(dve.tensor_scalar(source[:, :, :], tv, seg_base[:, 0:1], -1.0, ALU.subtract, ALU.mult))
        dve.tensor_copy(keep["index"][:, :, 0, :].rearrange("p t c -> p c t"), source[:, :, :])
        ch.step(dve.tensor_scalar(row[:, :, :], source[:, :, :], float(NT), None, ALU.mult))
        ch.step(dve.tensor_tensor(row[:, :, :], row[:, :, :], tile_f[:, :].unsqueeze(1).broadcast_to([P, CH, NT]), ALU.add))
        dve.tensor_copy(keep["index"][:, :, 1, :].rearrange("p t c -> p c t"), row[:, :, :])
        dve.wait_ge(over_sum, 1)
        ch.step(dve.tensor_copy(keep["overflow"][:, :], ps_over))

    def keys_on_tensor(self, pe):
        pe.wait_ge(self.key_ready, 1)
        for r in range(SEG // P):
            last = pe.transpose(self.ps_keys[r // 4][:, r % 4, :], self.has[:, r].rearrange("p s t -> p (s t)"),
                                self.keep["ident"][:, :])
            if r % 4 == 3:
                last.then_inc(self.key_turned, 1)

    def overflow_on_tensor(self, pe):
        pe.wait_ge(self.over_ready, 1)
        pe.matmul(self.ps_over, self.keep["ones"][:, :], self.over[:, :], start=True, stop=True).then_inc(self.over_sum, 1)


class Tile:

    def __init__(self, turn, k):
        self.t = turn * RING + k
        self.ring, self.par = k % RING, k % 2
        self.turn, self.pair = turn + k // RING, turn * (RING // 2) + k // 2


def wait(eng, sem, value):
    if not isinstance(value, int) or value > 0:
        eng.wait_ge(sem, value)


def pipeline(eng, stages):
    def step(turn, n):
        for stage, lag in stages:
            k = n + lag
            if turn is None and not 0 <= k < NT:
                continue
            stage(Tile(0 if turn is None else turn, k))

    first, turns = 5, (NT - 8) // RING
    for n in range(-2, first):
        step(None, n)
    with eng.Fori(0, turns) as turn:
        for u in range(RING):
            step(turn, first + u)
    for n in range(first + turns * RING, NT + 3):
        step(None, n)


class StageChain:

    def __init__(self, eng, sem, count):
        self.eng, self.sem, self.count = eng, sem, count

    def begin(self, tile):
        self.base, self.n = tile.t * self.count, 0

    def step(self, ins):
        self.n += 1
        ins.then_inc(self.sem, 1)
        self.eng.wait_ge(self.sem, self.base + self.n)

    def end(self):
        assert self.n == self.count, (self.n, self.count)


PASSES = ((0, 0), (0, 1), (1, 0))
A0 = 3
ACT_TURNS, DVE_TURNS = (0, 2, 4), (1, 3)
BANKS = ((0, A0), (A0, CH))


def attend_listed(nc, keep, x, adj_t, rtok, ytab, qtab, x1tab, y2ttab, sem):
    adj_rows = adj_t.rearrange("j (t i) -> (j t) i", i=P)
    x_tiles = x.rearrange("(t p) d -> t p d", p=P)
    x1_tiles = x1tab.rearrange("(t p) d -> t p d", p=P)
    with ExitStack() as ctx:
        def sb(name, shape, dt):
            return ctx.enter_context(nc.sbuf_tensor(name, shape, dt))

        def pb(name, shape, dt):
            return ctx.enter_context(nc.psum_tensor(name, shape, dt))

        index_now = sb("index_now", [P, RING, 2, CH], I32)
        y_src = sb("y_src", [P, RING, CH, 2 * D], F16)
        a_src = sb("a_src", [P, RING, CH, P], F32)
        y_src_t = sb("y_src_t", [P, 2, 2 * KC, LISTED], F16)
        a_tok = sb("a_tok", [P, 2, LISTED], F32)
        q_t = sb("q_t", [P, 2, KC, 2, P], F16)
        prob = sb("prob", [P, 2, LISTED], F32)
        fill = sb("fill", [P, LISTED], F32)
        top, bias = sb("top", [P, 2, 1], F32), sb("bias", [P, 2, 1], F32)
        sum_e, one_e = sb("sum_e", [P, 2, 1], F32), sb("one_e", [P, 2, 1], F32)
        den, rden, rest = sb("den", [P, 2, 1], F32), sb("rden", [P, 2, 1], F32), sb("rest", [P, 2, 1], F32)
        masked = sb("masked", [P, 1], F32)
        minus_half = sb("minus_half", [P, 1], F32)
        prob_t = sb("prob_t", [P, 2, CH, 2, P], F16)
        mix = sb("mix", [P, 2, D], F32)
        mix_t = sb("mix_t", [P, 2, KC, 2, P], F16)
        x_tok = sb("x_tok", [P, 2, D], F32)
        val = sb("val", [P, D], F32)
        x1 = sb("x1", [P, 2, D], F32)
        stats2, mv2 = sb("stats2", [P, 2, 6], F32), sb("mv2", [P, 2, 2], F32)
        var2, rstd2 = sb("var2", [P, 2, 2], F32), sb("rstd2", [P, 2, 2], F32)
        alpha = sb("alpha", [P, 2, 1], F32)
        rt_row = sb("rt_row", [P, D], F32)
        rt_sum = sb("rt_sum", [P, 1], F32)
        dot_junk = sb("dot_junk", [P, D], F32)
        dot, off = sb("dot", [P, 2, 1], F32), sb("off", [P, 2, 1], F32)
        y2 = sb("y2", [P, 2, D], F32)
        y2_t = sb("y2_t", [P, 2, KC, 2, P], F16)

        turn_bank = [pb(f"turn_bank{b}", [P, 2 * KC, P], F16) for b in range(2)]
        z_bank = [pb(f"z_bank{b}", [P, D], F32) for b in range(2)]
        pa_bank = [pb(f"pa_bank{b}", [P, KC, P], F32) for b in range(2)]
        u_bank = pb("u_bank", [P, D], F32)
        o_bank = pb("o_bank", [P, D], F32)

        def sems(*names):
            return [sem(n) for n in names]

        y_in, a_in = [sem(f"y_in{r}") for r in range(RING)], [sem(f"a_in{r}") for r in range(RING)]
        q_in, xt_in = [sem(f"q_in{r}") for r in range(2)], [sem(f"xt_in{r}") for r in range(2)]
        x1_out = [sem(f"x1_out{r}") for r in range(2)]
        y2t_out = [sem(f"y2t_out{r}") for r in range(2)]
        index_ready, pow_done = sems("index_ready", "pow_done")
        passed, passed_dve = sems("passed2", "passed_dve2")
        setup, const_in, rt_ready = sems("setup", "const_in", "rt_ready")
        turn_full, turn_read = [sem(f"turn_full{b}") for b in range(2)], [sem(f"turn_read{b}") for b in range(2)]
        a_full, a_read, z_full, w_done = sems("a_full", "a_read", "z_full", "w_done")
        pt_full, pt_high, pt_low, pv_done = sems("pt_full", "pt_high", "pt_low", "pv_done")
        soft, top_ready, e_ready, prob_chain, prob_ready = sems("soft", "top_ready", "e_ready", "prob_chain", "prob_ready")
        mix_ready, mt_full, mt_high, mt_low, o_full = sems("mix_ready", "mt_full", "mt_high", "mt_low", "o_full")
        o_read, x1_ready, x1_chain, var_done, y2_ready = sems("o_read", "x1_ready", "x1_chain", "var_done", "y2_ready")
        route, norming, off_ready = sems("route", "norming", "off_ready")
        s_ready, y2_full, y2_high, y2_low = sems("s_ready", "y2_full", "y2_high", "y2_low")

        with nc.Block() as block:
            @block.sync
            def _(sp):
                sp.dma_start(rt_row[:, :], rtok.partition_broadcast(P)).then_inc(const_in, 16)

                def load_q(c):
                    wait(sp, z_full, 2 * (c.t - 1))
                    sp.dma_start(q_t[:, c.par].rearrange("p k e t -> p (k e t)"),
                                 qtab[bass.ds(c.t, 1)].rearrange("a p n -> p (a n)")).then_inc(q_in[c.par], 16)

                def load_x(c):
                    wait(sp, x1_ready, c.t - 1)
                    sp.dma_start(x_tok[:, c.par], x_tiles[bass.ds(c.t, 1)].rearrange("a p n -> p (a n)")
                                 ).then_inc(xt_in[c.par], 16)

                def store_y2t(c):
                    sp.wait_ge(y2_low, c.t + 1)
                    sp.dma_start(y2ttab[bass.ds(c.t, 1)].rearrange("a p n -> p (a n)"),
                                 y2_t[:, c.par].rearrange("p k e t -> p (k e t)")).then_inc(y2t_out[c.par], 16)

                def store_rows(c):
                    sp.wait_ge(x1_ready, c.t + 1)
                    sp.dma_start(x1_tiles[bass.ds(c.t, 1)].rearrange("a p n -> p (a n)"), x1[:, c.par]).then_inc(x1_out[c.par], 16)

                pipeline(sp, [(load_q, 1), (load_x, 0), (store_rows, -3), (store_y2t, -3)])
                for b in range(2):
                    for s in (x1_out, y2t_out):
                        sp.wait_ge(s[b], 16 * NT // 2)

            @block.gpsimd
            def _(pool):
                pool.memset(masked[:, :], MASKED).then_inc(setup, 1)
                pool.memset(minus_half[:, :], -0.5).then_inc(setup, 1)
                pool.wait_ge(setup, 2)

                def gather(c):
                    pool.wait_ge(index_ready, c.t + 1)
                    pool.sem_inc(passed, 1)
                    for n in range(CH):
                        pool.indirect_dma_start(out=y_src[:, c.ring, n, :], out_offset=None, in_=ytab,
                                                in_offset=bass.IndirectOffsetOnAxis(ap=index_now[:, c.ring, 0, n:n + 1], axis=0)
                                                ).then_inc(y_in[c.ring], 16)
                    for n in range(CH):
                        pool.indirect_dma_start(out=a_src[:, c.ring, n, :], out_offset=None, in_=adj_rows,
                                                in_offset=bass.IndirectOffsetOnAxis(ap=index_now[:, c.ring, 1, n:n + 1], axis=0)
                                                ).then_inc(a_in[c.ring], 16)

                def powers(c):
                    pool.wait_ge(var_done, c.t + 1)
                    pool.tensor_tensor(rstd2[:, c.par], var2[:, c.par], minus_half[:, :].broadcast_to([P, 2]),
                                       ALU.pow).then_inc(pow_done, 1)

                pipeline(pool, [(gather, 2), (powers, -2)])

            @block.tensor
            def _(pe):
                ident, ident16 = keep["ident"], keep["ident16"]

                def turn_sources(*chunks):
                    def stage(c):
                        if chunks[0] == 0:
                            pe.wait_ge(y_in[c.ring], (c.turn + 1) * (16 * CH))
                        for n in chunks:
                            b = n % 2
                            wait(pe, turn_read[b], c.t * (3 - b) + n // 2)
                            for m in range(2 * KC):
                                last = pe.transpose(turn_bank[b][:, m, :], y_src[:, c.ring, n, m * P:(m + 1) * P], ident16[:, :])
                            last.then_inc(turn_full[b], 1)
                    return stage

                def turn_adjacency(c):
                    pe.wait_ge(a_in[c.ring], (c.turn + 1) * (16 * CH))
                    wait(pe, pt_low, 2 * (c.t - 1))
                    for b, (lo, hi) in enumerate(BANKS):
                        for n in range(lo, hi):
                            last = pe.transpose(pa_bank[b][:, n - lo, :], a_src[:, c.ring, n, :], ident[:, :])
                        last.then_inc(a_full, 1)

                def scores(c):
                    pe.wait_ge(q_in[c.par], (c.pair + 1) * 16)
                    pe.wait_ge(turn_read[0], c.t * 3 + 3)
                    pe.wait_ge(turn_read[1], c.t * 2 + 2)
                    for b, (lo, hi) in enumerate(BANKS):
                        wait(pe, (y2_low, mt_low)[b], c.t - (3, 1)[b])
                        if isinstance(c.t, int) and 0 < c.t <= 3:
                            pe.wait_ge(w_done, 2 * c.t - 1 + b)
                        for k in range(KC):
                            for e, f in PASSES:
                                last = pe.matmul(z_bank[b][:, 0:(hi - lo) * P], q_t[:, c.par, k, e, :],
                                                 y_src_t[:, c.par, f * KC + k, lo * P:hi * P],
                                                 start=(k == 0 and e + f == 0), stop=(k == KC - 1 and e == 1))
                        last.then_inc(z_full, 1)

                def turn_probs(c):
                    pe.wait_ge(prob_ready, c.t + 1)
                    pe.wait_ge(a_read, min(2 * c.t + 4, 2 * NT) if isinstance(c.t, int) else c.t * 2 + 4)
                    for b, (lo, hi) in enumerate(BANKS):
                        for n in range(lo, hi):
                            last = pe.transpose(pa_bank[b][:, n - lo, :], prob[:, c.par, n * P:(n + 1) * P], ident[:, :])
                        last.then_inc(pt_full, 1)

                def mix_sources(*chunks):
                    def stage(c):
                        if chunks[0] == 0:
                            pe.wait_ge(pt_low, c.t * 2 + 2)
                            wait(pe, mix_ready, c.t)
                        for n in chunks:
                            for e, f in PASSES:
                                last = pe.matmul(u_bank[:, :], prob_t[:, c.par, n, e, :], y_src[:, c.ring, n, f * D:(f + 1) * D],
                                                 start=(n == 0 and e + f == 0), stop=(n == CH - 1 and e == 1))
                        if chunks[-1] == CH - 1:
                            last.then_inc(pv_done, 1)
                    return stage

                def turn_mix(c):
                    pe.wait_ge(mix_ready, c.t + 1)
                    pe.wait_ge(w_done, min(2 * c.t + 4, 2 * NT) if isinstance(c.t, int) else c.t * 2 + 4)
                    for k in range(KC):
                        last = pe.transpose(z_bank[1][:, k * P:(k + 1) * P], mix[:, c.par, k * P:(k + 1) * P], ident[:, :])
                    last.then_inc(mt_full, 1)

                def values(c):
                    pe.wait_ge(mt_low, c.t + 1)
                    wait(pe, o_read, c.t)
                    for k in range(KC):
                        for e, f in PASSES:
                            last = pe.matmul(o_bank[:, :], mix_t[:, c.par, k, e, :], keep["wv"][:, k, f, :],
                                             start=(k == 0 and e + f == 0), stop=(k == KC - 1 and e == 1))
                    last.then_inc(o_full, 1)

                def turn_y2(c):
                    pe.wait_ge(y2_ready, c.t + 1)
                    pe.wait_ge(w_done, min(2 * c.t + 7, 2 * NT) if isinstance(c.t, int) else c.t * 2 + 7)
                    for k in range(KC):
                        last = pe.transpose(z_bank[0][:, k * P:(k + 1) * P], y2[:, c.par, k * P:(k + 1) * P], ident[:, :])
                    last.then_inc(y2_full, 1)

                pipeline(pe, [(scores, 0), (turn_probs, -1), (turn_sources(0, 1), 1), (mix_sources(0), -1),
                              (turn_sources(2, 3), 1), (mix_sources(1), -1), (turn_sources(4), 1), (turn_adjacency, 1),
                              (mix_sources(*range(2, CH)), -1), (turn_y2, -3),
                              (values, -2), (turn_mix, -1)])

            def leave_turned(eng, c, n):
                b = n % 2
                eng.wait_ge(turn_full[b], c.t * (3 - b) + (n // 2 + 1))
                wait(eng, z_full, 2 * (c.t - 1))
                dst, src = y_src_t[:, c.par, :, n * P:(n + 1) * P], turn_bank[b][:, :, :]
                ins = eng.activation(dst, src, ACT.Copy) if eng is nc.scalar else eng.tensor_copy(dst, src)
                ins.then_inc(turn_read[b], 1)

            @block.scalar
            def _(act):
                act.wait_ge(setup, 2)

                def indices(c):
                    wait(act, pv_done, c.t - 3)
                    wait(act, a_full, 2 * (c.t - 3))
                    act.activation(index_now[:, c.ring], keep["index"][:, bass.ds(c.t, 1)].rearrange("p a b c -> p (a b) c"),
                                   ACT.Copy).then_inc(index_ready, 1)

                def high_probs(c):
                    wait(act, pv_done, c.t - 1)
                    for b, (lo, hi) in enumerate(BANKS):
                        act.wait_ge(pt_full, c.t * 2 + (b + 1))
                        act.activation(prob_t[:, c.par, lo:hi, 0, :], pa_bank[b][:, 0:hi - lo, :], ACT.Copy, scale=PS).then_inc(pt_high, 1)

                def turned(c):
                    for n in ACT_TURNS:
                        leave_turned(act, c, n)

                def adjacency(c):
                    wait(act, w_done, 2 * (c.t - 1))
                    for b, (lo, hi) in enumerate(BANKS):
                        act.wait_ge(a_full, c.t * 2 + (b + 1))
                        act.activation(a_tok[:, c.par, lo * P:hi * P], pa_bank[b][:, 0:hi - lo, :].rearrange("p c t -> p (c t)"),
                                       ACT.Copy).then_inc(a_read, 1)

                def high_y2(c):
                    act.wait_ge(y2_full, c.t + 1)
                    wait(act, y2t_out[c.par], c.pair * 16)
                    act.activation(y2_t[:, c.par, :, 0, :], z_bank[0][:, :].rearrange("p (k t) -> p k t", k=KC), ACT.Copy
                                   ).then_inc(y2_high, 1)

                def exps(c):
                    act.wait_ge(top_ready, c.t + 1)
                    act.activation(one_e[:, c.par], masked[:, :], ACT.Exp, bias=bias[:, c.par], scale=SCALE).then_inc(e_ready, 1)
                    act.activation(prob[:, c.par], prob[:, c.par], ACT.Exp, bias=bias[:, c.par], scale=SCALE,
                                   accum_out=sum_e[:, c.par]).then_inc(e_ready, 1)

                def high_mix(c):
                    act.wait_ge(mt_full, c.t + 1)
                    wait(act, o_full, c.t - 1)
                    act.activation(mix_t[:, c.par, :, 0, :], z_bank[1][:, :].rearrange("p (k t) -> p k t", k=KC), ACT.Copy,
                                   scale=1.0 / PS).then_inc(mt_high, 1)

                pipeline(act, [(high_probs, -1), (indices, 2), (turned, 1), (adjacency, 1), (exps, 0), (high_y2, -3), (high_mix, -1)])

            @block.vector
            def _(dve):
                dve.wait_ge(const_in, 16)
                dve.tensor_reduce(rt_sum[:, :], rt_row[:, :], AX_X, ALU.add).then_inc(rt_ready, 1)
                dve.wait_ge(rt_ready, 1)
                softs, probs, rows = StageChain(dve, soft, 2), StageChain(dve, prob_chain, 2), StageChain(dve, x1_chain, 3)
                routes, norm_chain = StageChain(dve, route, 1), StageChain(dve, norming, 1)

                def low_probs(c):
                    for b, (lo, hi) in enumerate(BANKS):
                        dve.wait_ge(pt_high, c.t * 2 + (b + 1))
                        dve.scalar_tensor_tensor(prob_t[:, c.par, lo:hi, 1, :], pa_bank[b][:, 0:hi - lo, :], PS,
                                                 prob_t[:, c.par, lo:hi, 0, :], ALU.mult, ALU.subtract).then_inc(pt_low, 1)

                def weigh(c):
                    wait(dve, pt_full, 2 * (c.t - 1))
                    for b, (lo, hi) in enumerate(BANKS):
                        dve.wait_ge(z_full, c.t * 2 + (b + 1))
                        dve.wait_ge(a_read, c.t * 2 + (b + 1))
                        dve.scalar_tensor_tensor(prob[:, c.par, lo * P:hi * P], z_bank[b][:, 0:(hi - lo) * P],
                                                 keep["cs"][:, bass.ds(c.t, 1)], a_tok[:, c.par, lo * P:hi * P],
                                                 ALU.add, ALU.mult).then_inc(w_done, 1)

                def turned(c):
                    for n in DVE_TURNS:
                        leave_turned(dve, c, n)

                def low_y2(c):
                    dve.wait_ge(y2_high, c.t + 1)
                    dve.tensor_tensor(y2_t[:, c.par, :, 1, :], z_bank[0][:, :].rearrange("p (k t) -> p k t", k=KC),
                                      y2_t[:, c.par, :, 0, :], ALU.subtract).then_inc(y2_low, 1)

                def maxima(c):
                    softs.begin(c)
                    dve.wait_ge(w_done, c.t * 2 + 2)
                    softs.step(dve.tensor_scalar(fill[:, :], prob[:, c.par], 0.0, MASKED, ALU.is_equal, ALU.mult))
                    dve.sem_inc(passed_dve, 1)
                    softs.step(dve.tensor_tensor_reduce(out=prob[:, c.par], in0=prob[:, c.par], in1=fill[:, :], scale=1.0,
                                                        scalar=MASKED, op0=ALU.add, op1=ALU.max, accum_out=top[:, c.par]))
                    dve.tensor_scalar(bias[:, c.par], top[:, c.par], -SCALE, float(np.log(PS)), ALU.mult, ALU.add).then_inc(top_ready, 1)
                    softs.end()

                def mixed(c):
                    dve.wait_ge(pv_done, c.t + 1)
                    wait(dve, mt_full, c.t - 1)
                    dve.scalar_tensor_tensor(mix[:, c.par], keep["ytot"][:, :], rest[:, c.par], u_bank[:, :],
                                             ALU.mult, ALU.add).then_inc(mix_ready, 1)

                def normalise(c):
                    probs.begin(c)
                    dve.wait_ge(e_ready, c.t * 2 + 2)
                    probs.step(dve.scalar_tensor_tensor(den[:, c.par], one_e[:, c.par], float(N - LISTED), sum_e[:, c.par],
                                                        ALU.mult, ALU.add))
                    probs.step(dve.reciprocal(rden[:, c.par], den[:, c.par]))
                    dve.tensor_scalar(rest[:, c.par], one_e[:, c.par], rden[:, c.par], PS, ALU.mult, ALU.mult)
                    dve.tensor_scalar(prob[:, c.par], prob[:, c.par], one_e[:, c.par], rden[:, c.par], ALU.subtract,
                                      ALU.mult).then_inc(prob_ready, 1)
                    probs.end()

                def residual(c):
                    dve.wait_ge(o_full, c.t + 1)
                    dve.scalar_tensor_tensor(val[:, :], o_bank[:, :], 1.0 / ZS, keep["bvb"][:, :], ALU.mult, ALU.add
                                             ).then_inc(o_read, 1)
                    dve.wait_ge(o_read, c.t + 1)
                    dve.wait_ge(xt_in[c.par], (c.pair + 1) * 16)
                    wait(dve, x1_out[c.par], c.pair * 16)
                    dve.scalar_tensor_tensor(x1[:, c.par], val[:, :], 0.0, x_tok[:, c.par], ALU.max, ALU.add).then_inc(x1_ready, 1)

                def variance(c):
                    rows.begin(c)
                    dve.wait_ge(x1_ready, c.t + 1)
                    rows.step(dve.bn_stats(stats2[:, c.par], x1[:, c.par]))
                    dve.sem_inc(passed_dve, 1)
                    rows.step(dve.bn_aggr(mv2[:, c.par], stats2[:, c.par]))
                    dve.tensor_scalar(var2[:, c.par, 0:1], mv2[:, c.par, 1:2], 1.0 / (YS * YS), None, ALU.mult)
                    rows.step(dve.tensor_scalar(var2[:, c.par, 1:2], mv2[:, c.par, 1:2], EPS_LN, 1.0 / (YS * YS), ALU.add, ALU.mult))
                    dve.sem_inc(var_done, 1)
                    rows.end()

                def low_mix(c):
                    dve.wait_ge(mt_high, c.t + 1)
                    dve.scalar_tensor_tensor(mix_t[:, c.par, :, 1, :], z_bank[1][:, :].rearrange("p (k t) -> p k t", k=KC),
                                             1.0 / PS, mix_t[:, c.par, :, 0, :], ALU.mult, ALU.subtract).then_inc(mt_low, 1)

                def dots(c):
                    routes.begin(c)
                    routes.step(dve.tensor_tensor_reduce(out=dot_junk[:, :], in0=x1[:, c.par], in1=rt_row[:, :], scale=1.0,
                                                         scalar=0.0, op0=ALU.mult, op1=ALU.add, accum_out=dot[:, c.par]))
                    dve.scalar_tensor_tensor(off[:, c.par], mv2[:, c.par, 0:1], rt_sum[:, 0:1], dot[:, c.par],
                                             ALU.mult, ALU.subtract).then_inc(off_ready, 1)
                    routes.end()

                def norms(c):
                    norm_chain.begin(c)
                    dve.wait_ge(pow_done, c.t + 1)
                    norm_chain.step(dve.scalar_tensor_tensor(alpha[:, c.par], rstd2[:, c.par, 1:2], float(np.sqrt(D)) * 1e12,
                                                             rstd2[:, c.par, 0:1], ALU.mult, ALU.min))
                    wait(dve, y2_full, c.t - 1)
                    dve.tensor_scalar(y2[:, c.par], x1[:, c.par], mv2[:, c.par, 0:1], alpha[:, c.par], ALU.subtract,
                                      ALU.mult).then_inc(y2_ready, 1)
                    dve.wait_ge(off_ready, c.t + 1)
                    dve.tensor_scalar(keep["s"][:, bass.ds(c.t, 1)], off[:, c.par], rstd2[:, c.par, 1:2], -1.0 / YS,
                                      ALU.mult, ALU.mult).then_inc(s_ready, 1)
                    norm_chain.end()

                pipeline(dve, [(low_probs, -1), (turned, 1), (weigh, 0), (norms, -3), (maxima, 0), (mixed, -1),
                               (normalise, 0), (low_y2, -3), (residual, -2), (low_mix, -1), (variance, -2),
                               (dots, -2)])


BANK = 512
PIECES = N // BANK


def attend_all(nc, keep, x, adj, rtok, ytab, qtab, x1tab, y2ttab, sem):
    x_tiles = x.rearrange("(t p) d -> t p d", p=P)
    adj_tiles = adj.rearrange("(t p) j -> t p j", p=P)
    x1_tiles = x1tab.rearrange("(t p) d -> t p d", p=P)
    with ExitStack() as ctx:
        def sb(name, shape, dt):
            return ctx.enter_context(nc.sbuf_tensor(name, shape, dt))

        def pb(name, shape, dt):
            return ctx.enter_context(nc.psum_tensor(name, shape, dt))

        def sems(*names):
            return [sem(n) for n in names]

        ya = sb("all_y", [P, NT, 2 * D], F16)
        ya_t = sb("all_y_t", [P, 2 * KC, N], F16)
        adj_sb = sb("all_adj", [P, 2, BANK], F32)
        q_t = sb("all_q_t", [P, KC, 2, P], F16)
        prob = sb("all_prob", [P, N], F32)
        fill = sb("all_fill", [P, BANK], F32)
        tops, top, bias = sb("all_tops", [P, PIECES], F32), sb("all_top", [P, 1], F32), sb("all_bias", [P, 1], F32)
        sum_e, den, rden = sb("all_sum_e", [P, 1], F32), sb("all_den", [P, 1], F32), sb("all_rden", [P, 1], F32)
        minus_half = sb("all_minus_half", [P, 1], F32)
        prob_t = sb("all_prob_t", [P, 2, 4, 2, P], F16)
        mix, mix_t = sb("all_mix", [P, D], F32), sb("all_mix_t", [P, KC, 2, P], F16)
        x_tok, x1, y2 = sb("all_x_tok", [P, D], F32), sb("all_x1", [P, D], F32), sb("all_y2", [P, D], F32)
        stats, mv = sb("all_stats", [P, 6], F32), sb("all_mv", [P, 2], F32)
        var, rstd = sb("all_var", [P, 2], F32), sb("all_rstd", [P, 2], F32)
        alpha, dot, off = sb("all_alpha", [P, 1], F32), sb("all_dot", [P, 1], F32), sb("all_off", [P, 1], F32)
        rt_row, rt_sum = sb("all_rt_row", [P, D], F32), sb("all_rt_sum", [P, 1], F32)
        y2_t = sb("all_y2_t", [P, KC, 2, P], F16)
        z_bank = [pb(f"all_z_bank{b}", [P, BANK], F32) for b in range(2)]
        p_bank = [pb(f"all_p_bank{b}", [P, 4, P], F32) for b in range(2)]
        turn_bank = [pb(f"all_turn_bank{b}", [P, 2 * KC, P], F16) for b in range(2)]
        u_bank, o_bank = pb("all_u_bank", [P, D], F32), pb("all_o_bank", [P, D], F32)

        ya_in, rt_in, half_ready, rt_ready = sems("all_y_in", "all_rt_in", "all_half_ready", "all_rt_ready")
        turned, left = sems("all_turned", "all_left")
        adj_in = [sem("all_adj_in0"), sem("all_adj_in1")]
        q_in, x_in, x1_out, y2t_out = sems("all_q_in", "all_x_in", "all_x1_out", "all_y2t_out")
        scored, weighed, adj_free, masking, top_ready = sems("all_scored", "all_weighed", "all_adj_free", "all_masking", "all_top_ready")
        e_ready, prob_ready, p_full, p_high, p_low, p_used = sems("all_e_ready", "all_prob_ready", "all_p_full",
                                                                   "all_p_high", "all_p_low", "all_p_used")
        mix_ready, mt_full, mt_high, mt_low, o_full = sems("all_mix_ready", "all_mt_full", "all_mt_high", "all_mt_low", "all_o_full")
        x1_ready, tail, var_done, pow_done, y2_ready = sems("all_x1_ready", "all_tail", "all_var_done", "all_pow_done", "all_y2_ready")
        y2_full, y2_high, y2_low, carried = sems("all_y2_full", "all_y2_high", "all_y2_low", "all_carried")

        with nc.Block() as block:
            @block.sync
            def _(sp):
                sp.dma_start(rt_row[:, :], rtok.partition_broadcast(P)).then_inc(rt_in, 16)
                sp.dma_start(ya[:, :, :], ytab.rearrange("(c p) d -> p c d", p=P)).then_inc(ya_in, 16)
                sp.sem_inc(adj_free, 2)
                with sp.Fori(0, NT) as t:
                    sp.dma_start(q_t[:, :, :, :].rearrange("p k e t -> p (k e t)"),
                                 qtab[bass.ds(t, 1)].rearrange("a p n -> p (a n)")).then_inc(q_in, 16)
                    sp.dma_start(x_tok[:, :], x_tiles[bass.ds(t, 1)].rearrange("a p n -> p (a n)")).then_inc(x_in, 16)
                    for b in range(PIECES):
                        sp.wait_ge(adj_free, t * PIECES + (b + 1))
                        sp.dma_start(adj_sb[:, b % 2], adj_tiles[bass.ds(t, 1), :, b * BANK:(b + 1) * BANK]
                                     .rearrange("a p n -> p (a n)")).then_inc(adj_in[b % 2], 16)
                    sp.wait_ge(x1_ready, t + 1)
                    sp.dma_start(x1_tiles[bass.ds(t, 1)].rearrange("a p n -> p (a n)"), x1[:, :]).then_inc(x1_out, 16)
                    sp.wait_ge(y2_low, t + 1)
                    sp.dma_start(y2ttab[bass.ds(t, 1)].rearrange("a p n -> p (a n)"),
                                 y2_t[:, :, :, :].rearrange("p k e t -> p (k e t)")).then_inc(y2t_out, 16)
                for s in (x1_out, y2t_out):
                    sp.wait_ge(s, 16 * (NT + 1))

            @block.gpsimd
            def _(pool):
                pool.memset(minus_half[:, :], -0.5).then_inc(half_ready, 1)
                pool.wait_ge(half_ready, 1)
                with pool.Fori(0, NT) as t:
                    pool.wait_ge(var_done, t + 1)
                    pool.tensor_tensor(rstd[:, :], var[:, :], minus_half[:, :].broadcast_to([P, 2]), ALU.pow).then_inc(pow_done, 1)

            @block.tensor
            def _(pe):
                ident, ident16 = keep["ident"], keep["ident16"]
                pe.wait_ge(ya_in, 16)
                pe.sem_inc(left, 2)
                with pe.Fori(0, NT // 2) as i:
                    for h in range(2):
                        pe.wait_ge(left, i * 2 + 2)
                        for m in range(2 * KC):
                            last = pe.transpose(turn_bank[h][:, m, :],
                                                ya[:, bass.ds(i * 2 + h, 1), m * P:(m + 1) * P].rearrange("p a n -> p (a n)"),
                                                ident16[:, :])
                        last.then_inc(turned, 1)
                pe.wait_ge(left, NT + 2)
                with pe.Fori(0, NT) as t:
                    pe.wait_ge(q_in, t * 16 + 16)
                    for b in range(PIECES):
                        if b >= 2:
                            pe.wait_ge(weighed, t * PIECES + (b - 1))
                        for k in range(KC):
                            for e, f in PASSES:
                                last = pe.matmul(z_bank[b % 2][:, :], q_t[:, k, e, :], ya_t[:, f * KC + k, b * BANK:(b + 1) * BANK],
                                                 start=(k == 0 and e + f == 0), stop=(k == KC - 1 and e == 1))
                        last.then_inc(scored, 1)
                    pe.wait_ge(prob_ready, t + 1)
                    for g in range(PIECES):
                        if g > 0:
                            pe.wait_ge(p_low, t * PIECES + g)
                        for n in range(4):
                            last = pe.transpose(p_bank[g % 2][:, n, :], prob[:, (4 * g + n) * P:(4 * g + n + 1) * P], ident[:, :])
                        last.then_inc(p_full, 1)
                        pe.wait_ge(p_low, t * PIECES + (g + 1))
                        for n in range(4):
                            for e, f in PASSES:
                                last = pe.matmul(u_bank[:, :], prob_t[:, g % 2, n, e, :], ya[:, 4 * g + n, f * D:(f + 1) * D],
                                                 start=(g + n + e + f == 0), stop=(g == PIECES - 1 and n == 3 and e == 1))
                        last.then_inc(p_used, 1)
                    pe.wait_ge(mix_ready, t + 1)
                    for k in range(KC):
                        last = pe.transpose(z_bank[1][:, k * P:(k + 1) * P], mix[:, k * P:(k + 1) * P], ident[:, :])
                    last.then_inc(mt_full, 1)
                    pe.wait_ge(mt_low, t + 1)
                    for k in range(KC):
                        for e, f in PASSES:
                            last = pe.matmul(o_bank[:, :], mix_t[:, k, e, :], keep["wv"][:, k, f, :],
                                             start=(k == 0 and e + f == 0), stop=(k == KC - 1 and e == 1))
                    last.then_inc(o_full, 1)
                    pe.wait_ge(y2_ready, t + 1)
                    for k in range(KC):
                        last = pe.transpose(z_bank[0][:, k * P:(k + 1) * P], y2[:, k * P:(k + 1) * P], ident[:, :])
                    last.then_inc(y2_full, 1)
                    pe.wait_ge(y2_low, t + 1)

            @block.scalar
            def _(act):
                act.sem_inc(y2t_out, 16)
                with act.Fori(0, NT) as t:
                    act.wait_ge(top_ready, t + 1)
                    act.activation(prob[:, :], prob[:, :], ACT.Exp, bias=bias[:, :], scale=SCALE, accum_out=sum_e[:, :]
                                   ).then_inc(e_ready, 1)
                    for g in range(PIECES):
                        act.wait_ge(p_full, t * PIECES + (g + 1))
                        if g >= 2:
                            act.wait_ge(p_used, t * PIECES + (g - 1))
                        act.activation(prob_t[:, g % 2, :, 0, :], p_bank[g % 2][:, :, :], ACT.Copy).then_inc(p_high, 1)
                    act.wait_ge(mt_full, t + 1)
                    act.activation(mix_t[:, :, 0, :], z_bank[1][:, :].rearrange("p (k t) -> p k t", k=KC), ACT.Copy,
                                   scale=1.0 / PS).then_inc(mt_high, 1)
                    act.wait_ge(y2_full, t + 1)
                    act.wait_ge(y2t_out, t * 16 + 16)
                    act.activation(y2_t[:, :, 0, :], z_bank[0][:, :].rearrange("p (k t) -> p k t", k=KC), ACT.Copy
                                   ).then_inc(y2_high, 1)

            @block.vector
            def _(dve):
                dve.wait_ge(rt_in, 16)
                dve.tensor_reduce(rt_sum[:, :], rt_row[:, :], AX_X, ALU.add).then_inc(rt_ready, 1)
                dve.wait_ge(rt_ready, 1)
                with dve.Fori(0, NT // 2) as i:
                    for h in range(2):
                        dve.wait_ge(turned, i * 2 + (h + 1))
                        dve.tensor_copy(ya_t[:, :, bass.ds(i * (2 * P) + h * P, P)], turn_bank[h][:, :, :]).then_inc(left, 1)
                dve.sem_inc(x1_out, 16)
                with dve.Fori(0, NT) as t:
                    masks = Chain(dve, masking)
                    masks.base = t * (2 * PIECES + 1)
                    for b in range(PIECES):
                        piece = prob[:, b * BANK:(b + 1) * BANK]
                        dve.wait_ge(scored, t * PIECES + (b + 1))
                        dve.wait_ge(adj_in[b % 2], t * (8 * PIECES) + 16 * (b // 2 + 1))
                        dve.scalar_tensor_tensor(piece, z_bank[b % 2][:, :], keep["cs"][:, bass.ds(t, 1)], adj_sb[:, b % 2],
                                                 ALU.add, ALU.mult).then_inc(weighed, 1)
                        dve.wait_ge(weighed, t * PIECES + (b + 1))
                        dve.sem_inc(adj_free, 1)
                        masks.step(dve.tensor_scalar(fill[:, :], piece, 0.0, MASKED, ALU.is_equal, ALU.mult))
                        dve.sem_inc(carried, 1)
                        masks.step(dve.tensor_tensor_reduce(out=piece, in0=piece, in1=fill[:, :], scale=1.0, scalar=MASKED,
                                                            op0=ALU.add, op1=ALU.max, accum_out=tops[:, b:b + 1]))
                    masks.step(dve.tensor_reduce(top[:, :], tops[:, :], AX_X, ALU.max))
                    dve.tensor_scalar(bias[:, :], top[:, :], -SCALE, float(np.log(PS)), ALU.mult, ALU.add).then_inc(top_ready, 1)
                    ch = Chain(dve, tail)
                    ch.base = t * 10
                    dve.wait_ge(e_ready, t + 1)
                    ch.step(dve.tensor_scalar(den[:, :], sum_e[:, :], 1.0 / PS, None, ALU.mult))
                    ch.step(dve.reciprocal(rden[:, :], den[:, :]))
                    dve.tensor_scalar(prob[:, :], prob[:, :], rden[:, :], None, ALU.mult).then_inc(prob_ready, 1)
                    for g in range(PIECES):
                        dve.wait_ge(p_high, t * PIECES + (g + 1))
                        dve.tensor_tensor(prob_t[:, g % 2, :, 1, :], p_bank[g % 2][:, :, :], prob_t[:, g % 2, :, 0, :],
                                          ALU.subtract).then_inc(p_low, 1)
                    dve.wait_ge(p_used, t * PIECES + PIECES)
                    dve.tensor_copy(mix[:, :], u_bank[:, :]).then_inc(mix_ready, 1)
                    dve.wait_ge(mt_high, t + 1)
                    dve.scalar_tensor_tensor(mix_t[:, :, 1, :], z_bank[1][:, :].rearrange("p (k t) -> p k t", k=KC),
                                             1.0 / PS, mix_t[:, :, 0, :], ALU.mult, ALU.subtract).then_inc(mt_low, 1)
                    dve.wait_ge(o_full, t + 1)
                    dve.wait_ge(x1_out, t * 16 + 16)
                    ch.step(dve.scalar_tensor_tensor(x1[:, :], o_bank[:, :], 1.0 / ZS, keep["bvb"][:, :], ALU.mult, ALU.add))
                    dve.wait_ge(x_in, t * 16 + 16)
                    dve.scalar_tensor_tensor(x1[:, :], x1[:, :], 0.0, x_tok[:, :], ALU.max, ALU.add).then_inc(x1_ready, 1)
                    dve.wait_ge(x1_ready, t + 1)
                    ch.step(dve.bn_stats(stats[:, :], x1[:, :]))
                    dve.sem_inc(carried, 1)
                    ch.step(dve.bn_aggr(mv[:, :], stats[:, :]))
                    dve.tensor_scalar(var[:, 0:1], mv[:, 1:2], 1.0 / (YS * YS), None, ALU.mult)
                    ch.step(dve.tensor_scalar(var[:, 1:2], mv[:, 1:2], EPS_LN, 1.0 / (YS * YS), ALU.add, ALU.mult))
                    dve.sem_inc(var_done, 1)
                    dve.wait_ge(pow_done, t + 1)
                    ch.step(dve.scalar_tensor_tensor(alpha[:, :], rstd[:, 1:2], float(np.sqrt(D)) * 1e12, rstd[:, 0:1],
                                                     ALU.mult, ALU.min))
                    dve.tensor_scalar(y2[:, :], x1[:, :], mv[:, 0:1], alpha[:, :], ALU.subtract, ALU.mult).then_inc(y2_ready, 1)
                    ch.step(dve.tensor_tensor_reduce(out=fill[:, :], in0=x1[:, :], in1=rt_row[:, :], scale=1.0, scalar=0.0,
                                                     op0=ALU.mult, op1=ALU.add, accum_out=dot[:, :]))
                    ch.step(dve.scalar_tensor_tensor(off[:, :], mv[:, 0:1], rt_sum[:, 0:1], dot[:, :], ALU.mult, ALU.subtract))
                    ch.step(dve.tensor_scalar(keep["s"][:, bass.ds(t, 1)], off[:, :], rstd[:, 1:2], -1.0 / YS, ALU.mult, ALU.mult))
                    dve.wait_ge(y2_high, t + 1)
                    dve.tensor_tensor(y2_t[:, :, 1, :], z_bank[0][:, :].rearrange("p (k t) -> p k t", k=KC), y2_t[:, :, 0, :],
                                      ALU.subtract).then_inc(y2_low, 1)
                    dve.wait_ge(y2_low, t + 1)


K_ROUTE = 8.0
EPS_ROUTE = 0.1
RECENTRE = 12
LAST_STEPS = 50 - (NG // 2 - 1) * RECENTRE
CAP = 87.0
UNDERFLOW = -87.33654
LN_SHIFT = 64
WAYS = 8
ROUNDS, TOP_BIT = 10, 27
PER_STEP = 6
BEFORE_STEPS = 24
FIRST_BIAS = 3
FIRST_RESULT = 6
BEFORE_ROUNDS, PER_ROUND = 12, 8
PRODUCTS = 3 * (2 * (HL // P) * KC + 2 * GROUP * (HL // P))
HOT = 8


def feed_forward(nc, keep, ytab2t, x1tab, w1h, w2h, out, sem):
    y2t_groups = ytab2t.rearrange("(g s) p n -> g p s n", s=GROUP)
    with ExitStack() as ctx:
        def sb(name, shape, dt):
            return ctx.enter_context(nc.sbuf_tensor(name, shape, dt))

        def sems(*names):
            return [sem(n) for n in names]

        w1l_sb, w2l_sb, b1l_sb, b1h_sb = keep["w1l"], keep["w2l"], keep["b1l"], keep["b1h"]
        b2l_row, b2h_row = keep["b2l"], keep["b2h"]
        w1h_sb = sb("w1h_sb", [P, KC, 2, HH], F16)
        w2h_sb = sb("w2h_sb", [P, HH // P // 4, 2, 4, D], F16)
        score = sb("score", [P, NT], F32)
        ones = sb("ones_c", [P, P], F32)
        threshold = sb("threshold", [P, 1], I32)
        res = sb("res", [P, 2, GROUP, D], F32)
        res_out = [sem("res_out0"), sem("res_out1")]
        before = sb("before", [P, P], F32)
        slots = sb("slots", [P, ROUTED], F16)
        facts = sb("facts", [P, NT, 4], F16)
        minus_half = sb("minus_half_r", [P, 1], F32)

        with ExitStack() as c1:
            def tmp(name, shape, dt):
                return c1.enter_context(nc.sbuf_tensor(name, shape, dt))

            y_in_t = tmp("y_in_t", [P, 2, GROUP, KC, 2, P], F16)
            g32 = tmp("light_g32", [P, 2, HL // P, GROUP * P], F32)
            g64 = tmp("light_g64", [P, 2, HL // P, GROUP * P], F32)
            g_hl = tmp("light_g_hl", [P, 2, 2, HL // P, GROUP * P], F16)
            eighths = tmp("eighths", [P, P], F32)
            logits = tmp("logits", [P, NT + 1], F32)
            args, weights = tmp("args", [P, NT + 1], F32), tmp("weights", [P, NT + 1], F32)
            part, centre, s_top, s_part = (tmp(n, [P, 1], F32) for n in ("part_sum", "centre", "s_top", "s_part"))
            junk, log_a, low = tmp("junk", [P, NT], F32), tmp("log_a", [P, 1], F32), tmp("low", [P, NT], F32)
            steps_i, steps = tmp("steps_i", [P, WAYS], I32), tmp("steps", [P, WAYS], I32)
            slots_i, p_i, t_i = tmp("slots_i", [P, ROUTED], I32), tmp("p_i", [P, 1], I32), tmp("t_i", [P, NT], I32)
            cand = tmp("cand", [P, WAYS], I32)
            reached, count = tmp("reached", [P, WAYS, NT], F32), tmp("count", [P, WAYS], F32)
            met = tmp("met", [P, WAYS], F32)
            raw = tmp("heavy_raw", [P, 2, HH], F32)
            scaled = tmp("heavy_scaled", [P, 2, HH], F32)
            ps_h = [c1.enter_context(nc.psum_tensor(f"ps_h{i}", [P, GROUP * P], F32)) for i in range(4)]
            ps_o = [c1.enter_context(nc.psum_tensor(f"ps_o{i}", [P, D], F32)) for i in range(2)]
            ps_a = c1.enter_context(nc.psum_tensor("ps_a", [P, 1], F32))
            ps_n = c1.enter_context(nc.psum_tensor("ps_n", [P, WAYS], F32))
            g_in, x1_in = [[sem(f"{n}{h}") for h in range(2)] for n in ("g_in", "x1_in")]
            c1_const, top_in, top_out, h_full = sems("c1_const", "top_in", "top_out", "h_full")
            gelu_ready, halves_ready, low_ready, with_bias, o_full, res_ready = sems(
                "gelu_ready", "halves_ready", "low_ready", "with_bias", "light_o_full", "res_ready")
            dve3, args_ready, exp_ready, part_ready, sum_ready, log_ready = sems(
                "dve3", "args_ready", "exp_ready", "part_ready", "sum_ready", "log_ready")
            final_ready, search, counted, totalled = sems("final_ready", "search", "counted", "totalled")
            heavy_raw_in = [sem("heavy_raw_in0"), sem("heavy_raw_in1")]
            heavy_scaled, heavy_high, heavy_low = sems("heavy_scaled", "heavy_high", "heavy_low")
            TURNS = NG // 2
            LAST = TURNS - 1
            o_tok = tmp("o_tok", [P, 2, D], F32)
            late_bias, late_copied, late_ready, late_ready_dve = sems("late_bias", "late_copied", "late_ready", "late_ready_dve")
            LATE_BY_POOL = 2 * GROUP - 2
            iota2, tri_ready = sems("iota2", "tri_ready")
            assert TURNS == KC == HH // P // 4

            def heavy_half(weights_hl, u, half):
                v = weights_hl[:, bass.ds(u, 1), half]
                return v.rearrange("p a n -> p (a n)") if len(v.shape) == 3 else v.rearrange("p a c n -> p (a c n)")

            with nc.Block() as block:
                @block.sync
                def _(sp):
                    w1h_quarters = w1h.rearrange("(u p) n -> u p n", p=P)
                    w2h_quarters = w2h.rearrange("(u c p) n -> u p c n", c=4, p=P)
                    x1_groups = x1tab.rearrange("(g s p) d -> g p s d", s=GROUP, p=P)
                    out_groups = out.rearrange("(g s p) d -> g p s d", s=GROUP, p=P)

                    def load_y(g, h):
                        sp.dma_start(y_in_t[:, h].rearrange("p s k e t -> p s (k e t)"),
                                     y2t_groups[bass.ds(g, 1)].rearrange("a p s n -> p (a s) n")).then_inc(g_in[h], 16)

                    def load_x1(g, h):
                        sp.dma_start(res[:, h], x1_groups[bass.ds(g, 1)].rearrange("a p s d -> p (a s) d")).then_inc(x1_in[h], 16)

                    def store(g, h, late=False):
                        if late:
                            sp.wait_ge(late_ready, min((h + 1) * GROUP, LATE_BY_POOL))
                            if (h + 1) * GROUP > LATE_BY_POOL:
                                sp.wait_ge(late_ready_dve, 2 * GROUP - LATE_BY_POOL)
                        else:
                            sp.wait_ge(res_ready, g * GROUP + GROUP)
                        sp.dma_start(out_groups[bass.ds(g, 1)].rearrange("a p s d -> p (a s) d"), res[:, h]).then_inc(res_out[h], 16)

                    def load_heavy(u):
                        sp.dma_start(raw[:, 0], w1h_quarters[bass.ds(u, 1)].rearrange("a p n -> p (a n)")).then_inc(heavy_raw_in[0], 16)
                        sp.dma_start(raw[:, 1].rearrange("p (c n) -> p c n", c=4),
                                     w2h_quarters[bass.ds(u, 1)].rearrange("a p c n -> p (a c) n")).then_inc(heavy_raw_in[1], 16)

                    load_y(0, 0)
                    load_y(1, 1)
                    load_x1(0, 0)
                    load_x1(1, 1)
                    load_heavy(0)
                    with sp.Fori(0, TURNS - 1) as i:
                        for h in range(2):
                            sp.wait_ge(h_full, i * 4 + 2 * (h + 1))
                            load_y(i * 2 + (2 + h), h)
                        sp.wait_ge(heavy_scaled, i * 2 + 2)
                        load_heavy(i + 1)
                        for h in range(2):
                            store(i * 2 + h, h)
                        for h in range(2):
                            sp.wait_ge(res_out[h], i * 16 + 16)
                            load_x1(i * 2 + (2 + h), h)
                    for h in range(2):
                        store(2 * LAST + h, h, late=True)

                @block.gpsimd
                def _(pool):
                    pool.memset(eighths[:, :], 1.0 / K_ROUTE).then_inc(c1_const, 1)
                    pool.memset(ones[:, :], 1.0).then_inc(c1_const, 1)
                    pool.iota(steps_i[:, :], pattern=[[1, WAYS]], base=0, channel_multiplier=0).then_inc(c1_const, 1)
                    pool.wait_ge(top_in, 1)
                    pool.partition_all_reduce(s_top[:, :], s_part[:, :], P, bass.bass_isa.ReduceOp.max).then_inc(top_out, 1)

                    pool.iota(slots_i[:, :], pattern=[[1, ROUTED]], base=0, channel_multiplier=0).then_inc(iota2, 1)
                    pool.iota(p_i[:, :], pattern=[[0, 1]], base=0, channel_multiplier=1).then_inc(iota2, 1)
                    pool.iota(t_i[:, :], pattern=[[1, NT]], base=0, channel_multiplier=0).then_inc(iota2, 1)
                    pool.memset(minus_half[:, :], -0.5)
                    pool.memset(before[:, :], 1.0).then_inc(tri_ready, 1)
                    pool.wait_ge(tri_ready, 1)
                    pool.affine_select(out=before[:, :], in_=before[:, :], compare_op=ALU.is_gt, fill=0.0, base=0,
                                       pattern=[[1, P]], channel_multiplier=-1)

                    def low_half(i, h):
                        pool.wait_ge(halves_ready, i * 4 + 2 * (h + 1))
                        pool.tensor_tensor(g_hl[:, h, 1], g64[:, h], g_hl[:, h, 0], ALU.subtract).then_inc(low_ready, 1)

                    def heavy_low_halves(i):
                        for m, dst in enumerate((w1h_sb, w2h_sb)):
                            pool.wait_ge(heavy_high, i * 2 + (m + 1))
                            pool.tensor_tensor(heavy_half(dst, i, 1), scaled[:, m], heavy_half(dst, i, 0), ALU.subtract
                                               ).then_inc(heavy_low, 1)

                    with pool.Fori(0, LAST) as i:
                        for h in range(2):
                            low_half(i, h)
                        heavy_low_halves(i)
                    heavy_low_halves(LAST)
                    for h in range(2):
                        pool.wait_ge(x1_in[h], LAST * 16 + 16)
                        pool.tensor_tensor(res[:, h], res[:, h], b2l_row[:, :].unsqueeze(1).broadcast_to([P, GROUP, D]),
                                           ALU.add).then_inc(late_bias, 1)
                    for h in range(2):
                        low_half(LAST, h)
                    pool.wait_ge(late_bias, 2)
                    for k in range(LATE_BY_POOL):
                        pool.wait_ge(late_copied, k + 1)
                        pool.tensor_tensor(res[:, k // GROUP, k % GROUP], res[:, k // GROUP, k % GROUP], o_tok[:, k % 2],
                                           ALU.add).then_inc(late_ready, 1)

                @block.vector
                def _(dve):
                    ch = Chain(dve, dve3)
                    ch.step(dve.tensor_copy(logits[:, 0:NT], keep["s"][:, :]))
                    dve.memset(logits[:, NT:NT + 1], 0.0)
                    dve.tensor_reduce(s_part[:, :], keep["s"][:, :], AX_X, ALU.max).then_inc(top_in, 1)
                    dve.wait_ge(top_out, 1)
                    ch.step(dve.tensor_copy(low[:, 0:1], s_part[:, :]))

                    def recentre(turn):
                        ch.step(dve.tensor_tensor(centre[:, :], logits[:, NT:NT + 1], s_top[:, :], ALU.min))
                        ch.step(dve.tensor_scalar(args[:, :], logits[:, :], centre[:, :], 1.0 / EPS_ROUTE, ALU.subtract, ALU.mult))
                        dve.tensor_scalar(args[:, :], args[:, :], CAP, None, ALU.min).then_inc(args_ready, 1)
                        dve.wait_ge(exp_ready, turn + 1)

                    def descend(done, n):
                        if n > 0:
                            dve.wait_ge(sum_ready, done + n)
                        a = weights[:, NT:NT + 1] if n == 0 else ps_a[:, :]
                        dve.tensor_scalar(junk[:, :], weights[:, 0:NT], a, None, ALU.min, ALU.add,
                                          accum_out=part[:, :]).then_inc(part_ready, 1)

                    def take_log(turn):
                        dve.wait_ge(log_ready, turn + 1)
                        ch.step(dve.tensor_scalar(log_a[:, :], log_a[:, :], LN_SHIFT * float(np.log(2.0)), EPS_ROUTE, ALU.add, ALU.mult))
                        ch.step(dve.tensor_tensor(logits[:, NT:NT + 1], log_a[:, :], centre[:, :], ALU.add))

                    def result(i, k):
                        h, s = k // GROUP, k % GROUP
                        dve.wait_ge(with_bias, i * (2 * GROUP) + (k + 1))
                        dve.wait_ge(o_full, i * (2 * GROUP) + (k + 1))
                        dve.scalar_tensor_tensor(res[:, h, s], ps_o[k % 2][:, :], 1.0 / ZS, res[:, h, s], ALU.mult, ALU.add
                                                 ).then_inc(res_ready, 1)

                    def bias(i, k):
                        h, s = k // GROUP, k % GROUP
                        if s == 0:
                            dve.wait_ge(x1_in[h], i * 16 + 16)
                        dve.tensor_tensor(res[:, h, s], res[:, h, s], b2l_row[:, :], ALU.add).then_inc(with_bias, 1)

                    base = ch.n
                    with dve.Fori(0, LAST) as i:
                        ch.base, ch.n = i * 4 + base, 0
                        recentre(i)
                        for n in range(RECENTRE):
                            descend(i * RECENTRE, n)
                            if FIRST_BIAS <= n < FIRST_BIAS + 2 * GROUP:
                                bias(i, n - FIRST_BIAS)
                            if n >= FIRST_RESULT:
                                result(i, n - FIRST_RESULT)
                        for k in range(RECENTRE - FIRST_RESULT, 2 * GROUP):
                            result(i, k)
                        dve.wait_ge(res_ready, i * (2 * GROUP) + 2 * GROUP)
                        take_log(i)
                    ch.base, ch.n = 0, base + 4 * LAST
                    recentre(LAST)
                    for n in range(LAST_STEPS):
                        descend(LAST * RECENTRE, n)
                    take_log(LAST)
                    ch.step(dve.tensor_scalar(args[:, 0:NT], keep["s"][:, :], logits[:, NT:NT + 1], None, ALU.subtract))
                    ch.step(dve.tensor_scalar(low[:, :], args[:, 0:NT], 0.0, None, ALU.max))
                    ch.step(dve.tensor_tensor(args[:, 0:NT], args[:, 0:NT], low[:, :], ALU.subtract))
                    ch.step(dve.tensor_scalar(args[:, 0:NT], args[:, 0:NT], 1.0 / EPS_ROUTE, None, ALU.mult))
                    ch.step(dve.tensor_scalar(low[:, :], args[:, 0:NT], UNDERFLOW, None, ALU.is_ge))
                    dve.sem_inc(final_ready, 1)
                    dve.wait_ge(iota2, 3)
                    dve.tensor_copy(slots[:, :], slots_i[:, :])
                    dve.tensor_copy(facts[:, :, 0], p_i[:, :].broadcast_to([P, NT]))
                    dve.tensor_copy(facts[:, :, 1], t_i[:, :])
                    dve.wait_ge(exp_ready, TURNS + 1)
                    ch.step(dve.tensor_tensor(score[:, :], weights[:, 0:NT], low[:, :], ALU.mult))

                    find = Chain(dve, search)
                    dve.wait_ge(c1_const, 3)
                    find.step(dve.tensor_single_scalar(steps[:, :], steps_i[:, :], TOP_BIT, ALU.logical_shift_left))
                    find.step(dve.memset(threshold[:, :], 0))
                    with dve.Fori(0, 2) as half:
                        find.base, find.n = half * (ROUNDS // 2 * 4) + 2, 0
                        for n in range(ROUNDS // 2):
                            find.step(dve.tensor_tensor(cand[:, :], steps[:, :], threshold[:, :].broadcast_to([P, WAYS]), ALU.bitwise_or))
                            find.step(dve.tensor_tensor(reached[:, :, :], score[:, :].unsqueeze(1).broadcast_to([P, WAYS, NT]),
                                                        cand[:, :].bitcast(F32).unsqueeze(2).broadcast_to([P, WAYS, NT]), ALU.is_ge))
                            dve.tensor_reduce(count[:, :], reached[:, :, :], AX_X, ALU.add).then_inc(counted, 1)
                            dve.tensor_single_scalar(steps[:, :], steps[:, :], 3, ALU.logical_shift_right)
                            dve.wait_ge(totalled, half * (ROUNDS // 2) + (n + 1))
                            find.step(dve.scalar_tensor_tensor(met[:, :], ps_n[:, :], float(ROUTED), cand[:, :].bitcast(F32),
                                                               ALU.is_ge, ALU.mult))
                            find.step(dve.tensor_reduce(threshold[:, :].bitcast(F32), met[:, :], AX_X, ALU.max))
                    dve.wait_ge(late_bias, 2)
                    for k in range(LATE_BY_POOL, 2 * GROUP):
                        h, s = k // GROUP, k % GROUP
                        dve.wait_ge(o_full, LAST * (2 * GROUP) + (k + 1))
                        dve.scalar_tensor_tensor(res[:, h, s], ps_o[k % 2][:, :], 1.0 / ZS, res[:, h, s], ALU.mult, ALU.add
                                                 ).then_inc(late_ready_dve, 1)

                @block.scalar
                def _(act):
                    def split_heavy(i):
                        act.wait_ge(heavy_low, i * 2 + 2)
                        act.wait_ge(heavy_raw_in[0], i * 16 + 16)
                        act.activation(scaled[:, 0], raw[:, 0], ACT.Copy, scale=keep["gain_h"][:, bass.ds(i, 1)]).then_inc(heavy_scaled, 1)
                        act.wait_ge(heavy_raw_in[1], i * 16 + 16)
                        act.activation(scaled[:, 1], raw[:, 1], ACT.Copy, scale=YS).then_inc(heavy_scaled, 1)
                        for m, dst in enumerate((w1h_sb, w2h_sb)):
                            act.wait_ge(heavy_scaled, i * 2 + (m + 1))
                            act.activation(heavy_half(dst, i, 0), scaled[:, m], ACT.Copy).then_inc(heavy_high, 1)

                    def activate(i, h):
                        for c in range(HL // P):
                            act.wait_ge(h_full, i * 4 + (2 * h + c + 1))
                            act.activation(g32[:, h, c], ps_h[2 * h + c][:, :], ACT.Gelu, bias=b1l_sb[:, c:c + 1],
                                           scale=1.0 / ZS).then_inc(gelu_ready, 1)
                        act.wait_ge(gelu_ready, i * 4 + 2 * (h + 1))
                        act.activation(g_hl[:, h, 0], g32[:, h], ACT.Copy, scale=YS).then_inc(halves_ready, 1)
                        act.activation(g64[:, h], g32[:, h], ACT.Copy, scale=YS).then_inc(halves_ready, 1)

                    def exps(turn):
                        act.wait_ge(args_ready, turn + 1)
                        act.activation(weights[:, :], args[:, :], ACT.Exp).then_inc(exp_ready, 1)

                    def logs(turn, done):
                        act.wait_ge(sum_ready, done)
                        act.activation(log_a[:, :], ps_a[:, :], ACT.Ln, scale=2.0 ** -LN_SHIFT).then_inc(log_ready, 1)

                    act.sem_inc(heavy_low, 2)
                    with act.Fori(0, LAST) as i:
                        exps(i)
                        for h in range(2):
                            activate(i, h)
                        split_heavy(i)
                        logs(i, i * RECENTRE + RECENTRE)
                    exps(LAST)
                    split_heavy(LAST)
                    logs(LAST, LAST * RECENTRE + LAST_STEPS)
                    act.wait_ge(final_ready, 1)
                    act.activation(weights[:, 0:NT], args[:, 0:NT], ACT.Exp).then_inc(exp_ready, 1)
                    for h in range(2):
                        activate(LAST, h)
                    for k in range(LATE_BY_POOL):
                        act.wait_ge(o_full, LAST * (2 * GROUP) + (k + 1))
                        if k >= 2:
                            act.wait_ge(late_ready, k - 1)
                        act.activation(o_tok[:, k % 2], ps_o[k % 2][:, :], ACT.Copy, scale=1.0 / ZS).then_inc(late_copied, 1)

                @block.tensor
                def _(pe):
                    pe.wait_ge(c1_const, 3)

                    def total(done):
                        pe.wait_ge(part_ready, done + 1)
                        pe.matmul(ps_a[:, :], eighths[:, :], part[:, :], start=True, stop=True).then_inc(sum_ready, 1)

                    def light_turn(i, between, free):
                        products = 0
                        for h in range(2):
                            pe.wait_ge(g_in[h], i * 16 + 16)
                            for c in range(HL // P):
                                for k in range(KC):
                                    for e, f in PASSES:
                                        last = pe.matmul(ps_h[2 * h + c][:, :], w1l_sb[:, e, k, c * P:(c + 1) * P],
                                                         y_in_t[:, h, :, k, f, :], start=(k == 0 and e + f == 0),
                                                         stop=(k == KC - 1 and e == 1))
                                        products += 1
                                        if k == KC - 1 and e == 1:
                                            last.then_inc(h_full, 1)
                                        between(products)
                        for k in range(2 * GROUP):
                            h, s = k // GROUP, k % GROUP
                            if s == 0:
                                pe.wait_ge(low_ready, i * 2 + (h + 1))
                            if k >= 2:
                                free(k)
                            for c in range(HL // P):
                                for e, f in PASSES:
                                    last = pe.matmul(ps_o[k % 2][:, :], g_hl[:, h, e, c, s * P:(s + 1) * P], w2l_sb[:, f, c, :],
                                                     start=(c == 0 and e + f == 0), stop=(c == 1 and e == 1))
                                    products += 1
                                    if c == 1 and e == 1:
                                        last.then_inc(o_full, 1)
                                    between(products)

                    with pe.Fori(0, LAST) as i:
                        def routing_step(products):
                            n = (products - BEFORE_STEPS) // PER_STEP
                            if products >= BEFORE_STEPS and (products - BEFORE_STEPS) % PER_STEP == 0 and n < RECENTRE:
                                total(i * RECENTRE + n)

                        light_turn(i, routing_step, lambda k: pe.wait_ge(res_ready, i * (2 * GROUP) + (k - 1)))
                    for n in range(LAST_STEPS):
                        total(LAST * RECENTRE + n)

                    def count_total(r):
                        pe.wait_ge(counted, r + 1)
                        pe.matmul(ps_n[:, :], ones[:, :], count[:, :], start=True, stop=True).then_inc(totalled, 1)

                    def search_round(products):
                        r = (products - BEFORE_ROUNDS) // PER_ROUND
                        if products >= BEFORE_ROUNDS and (products - BEFORE_ROUNDS) % PER_ROUND == 0 and r < ROUNDS:
                            count_total(r)

                    light_turn(LAST, search_round, lambda k: pe.wait_ge(late_copied, k - 1))
                    for r in range((PRODUCTS - BEFORE_ROUNDS) // PER_ROUND + 1, ROUNDS):
                        count_total(r)

        route_and_heavy(nc, keep, score, threshold, ones, before, slots, facts, minus_half, x1tab, w1h_sb,
                        w2h_sb, b1h_sb, b2h_row, res_out, out, sem)


def route_and_heavy(nc, keep, score, threshold, ones, before, slots, facts, minus_half, x1tab, w1h_sb,
                    w2h_sb, b1h_sb, b2h_row, res_out, out, sem):
    B = ROUTED // P
    HC = HH // P
    with ExitStack() as ctx:
        def sb(name, shape, dt):
            return ctx.enter_context(nc.sbuf_tensor(name, shape, dt))

        def sems(*names):
            return [sem(n) for n in names]

        chosen = sb("chosen", [P, 2 * NT], F32)
        run, order, held = sb("run", [P, 2 * NT], F32), sb("order", [P, 2 * NT], F32), sb("held", [P, 2 * NT], F32)
        place = sb("place", [P, NT], F32)
        gain = sb("gain", [P, NT], F32)
        hot = sb("hot", [P, HOT, ROUTED], F16)
        found = sb("found", [P, B, 4], F32)
        token_f, token, gains = sb("token_f", [P, B], F32), sb("token", [P, B], I32), sb("gains_r", [P, B], F32)
        y_rt = sb("y_rt", [P, B, D], F32)
        stats_r, mv_r = sb("stats_r", [P, B, 6], F32), sb("mv_r", [P, B, 2], F32)
        var_r, rstd_r, alpha_r = sb("var_r", [P, B, 2], F32), sb("rstd_r", [P, B, 2], F32), sb("alpha_r", [P, B], F32)
        y_rt_t = sb("y_rt_t", [P, KC, 2, ROUTED], F16)
        base = sb("base", [P, B, D], F32)
        g32 = sb("g32", [P, 2, ROUTED], F32)
        g_hl = sb("g_hl", [P, HC, 2, ROUTED], F16)
        fin = sb("fin", [P, B, D], F32)
        ps_w = ctx.enter_context(nc.psum_tensor("ps_w", [P, 2, 2 * NT], F32))
        ps_f = ctx.enter_context(nc.psum_tensor("ps_f", [P, B, 4], F32))
        ps_r = [ctx.enter_context(nc.psum_tensor(f"ps_r{i}", [P, KC, P], F32)) for i in range(2)]
        ps_u = [ctx.enter_context(nc.psum_tensor(f"ps_u{i}", [P, D], F32)) for i in range(4)]

        dve4, sel_ready, prefix_ready = sems("dve4", "sel_ready", "prefix_ready")
        hot_ready, facts_ready, found_ready, token_ready = sems("hot_ready", "facts_ready", "found_ready", "token_ready")
        hot_used, var_rt_ready, pow_rt_done, y_rt_ready = sems("hot_used", "var_rt_ready", "pow_rt_done", "y_rt_ready")
        rows_in = [sem(f"rows_in{b}") for b in range(B)]
        base_in, r_full, r_high, r_low, u_full, u_act, u_high, u_low = sems(
            "base_in", "r_full", "r_high", "r_low", "u_full", "u_act", "u_high", "u_low")
        d_full, d_read, fin_ready, fin_out = sems("d_full", "d_read", "fin_ready", "fin_out")

        with nc.Block() as block:
            @block.gpsimd
            def _(pool):
                pool.wait_ge(token_ready, 1)
                for b in range(B):
                    pool.indirect_dma_start(out=y_rt[:, b, :], out_offset=None, in_=x1tab,
                                            in_offset=bass.IndirectOffsetOnAxis(ap=token[:, b:b + 1], axis=0)).then_inc(rows_in[b], 16)
                for b in range(B):
                    pool.wait_ge(var_rt_ready, b + 1)
                    pool.tensor_tensor(rstd_r[:, b], var_r[:, b], minus_half[:, :].broadcast_to([P, 2]), ALU.pow).then_inc(pow_rt_done, 1)
                for h in range(2):
                    pool.wait_ge(res_out[h], 16 * (NG // 2))
                for b in range(B):
                    pool.indirect_dma_start(out=base[:, b, :], out_offset=None, in_=out,
                                            in_offset=bass.IndirectOffsetOnAxis(ap=token[:, b:b + 1], axis=0)).then_inc(base_in, 16)
                for b in range(B):
                    pool.wait_ge(fin_ready, b + 1)
                    pool.indirect_dma_start(out=out, out_offset=bass.IndirectOffsetOnAxis(ap=token[:, b:b + 1], axis=0),
                                            in_=fin[:, b, :], in_offset=None).then_inc(fin_out, 16)
                pool.wait_ge(fin_out, 16 * B)

            @block.vector
            def _(dve):
                ch = Chain(dve, dve4)
                level_f = threshold[:, :].bitcast(F32)
                dve.tensor_scalar(chosen[:, 0:NT], score[:, :], level_f, None, ALU.is_gt)
                ch.step(dve.tensor_scalar(chosen[:, NT:2 * NT], score[:, :], level_f, None, ALU.is_equal))
                dve.sem_inc(sel_ready, 1)
                dve.memset(run[:, 0:1], 0.0)
                ch.step(dve.tensor_scalar(gain[:, :], score[:, :], -1.0, 1.0, ALU.mult, ALU.add))
                ch.step(dve.tensor_tensor(gain[:, :], gain[:, :], score[:, :], ALU.add))
                ch.step(dve.tensor_copy(facts[:, :, 2], gain[:, :]))
                dve.tensor_tensor(facts[:, :, 3], gain[:, :], facts[:, :, 2], ALU.subtract)
                dve.wait_ge(prefix_ready, 1)
                ch.step(dve.tensor_tensor_scan(run[:, 1:2 * NT], ones[:, 0:2 * NT - 1], ps_w[:, 1, 0:2 * NT - 1], 0.0, ALU.mult, ALU.add))
                ch.step(dve.tensor_tensor(order[:, :], run[:, :], ps_w[:, 0, :], ALU.add))
                ch.step(dve.scalar_tensor_tensor(held[:, :], order[:, :], float(ROUTED), chosen[:, :], ALU.is_lt, ALU.mult))
                ch.step(dve.scalar_tensor_tensor(held[:, :], order[:, :], 1.0, held[:, :], ALU.add, ALU.mult))
                ch.step(dve.scalar_tensor_tensor(place[:, :], held[:, 0:NT], -1.0, held[:, NT:2 * NT], ALU.add, ALU.add))
                dve.sem_inc(facts_ready, 1)
                dve.sem_inc(hot_used, HOT)
                with dve.Fori(0, NT // HOT) as i:
                    for h in range(HOT):
                        dve.wait_ge(hot_used, i * HOT + (h + 1))
                        dve.tensor_scalar(hot[:, h], slots[:, :], place[:, bass.ds(i * HOT + h, 1)], None, ALU.is_equal
                                          ).then_inc(hot_ready, 1)
                dve.wait_ge(found_ready, 1)
                ch.step(dve.tensor_copy(found[:, :, :], ps_f[:, :, :]))
                ch.step(dve.scalar_tensor_tensor(token_f[:, :], found[:, :, 1], float(P), found[:, :, 0], ALU.mult, ALU.add))
                dve.tensor_tensor(gains[:, :], found[:, :, 2], found[:, :, 3], ALU.add)
                dve.tensor_copy(token[:, :], token_f[:, :]).then_inc(token_ready, 1)
                def routed_statistics(b):
                    dve.wait_ge(rows_in[b], 16)
                    ch.step(dve.bn_stats(stats_r[:, b], y_rt[:, b]))
                    ch.step(dve.bn_aggr(mv_r[:, b], stats_r[:, b]))
                    dve.tensor_scalar(var_r[:, b, 0:1], mv_r[:, b, 1:2], 1.0 / (YS * YS), None, ALU.mult)
                    ch.step(dve.tensor_scalar(var_r[:, b, 1:2], mv_r[:, b, 1:2], EPS_LN, 1.0 / (YS * YS), ALU.add, ALU.mult))
                    dve.sem_inc(var_rt_ready, 1)

                def routed_norm(b):
                    dve.wait_ge(pow_rt_done, b + 1)
                    ch.step(dve.scalar_tensor_tensor(alpha_r[:, b:b + 1], rstd_r[:, b, 1:2], float(np.sqrt(D)) * 1e12,
                                                     rstd_r[:, b, 0:1], ALU.mult, ALU.min))
                    dve.tensor_scalar(y_rt[:, b], y_rt[:, b], mv_r[:, b, 0:1], alpha_r[:, b:b + 1], ALU.subtract,
                                      ALU.mult).then_inc(y_rt_ready, 1)

                for b in range(B):
                    routed_statistics(b)
                    if b > 0:
                        routed_norm(b - 1)
                routed_norm(B - 1)
                for b in range(B):
                    dve.wait_ge(r_high, b + 1)
                    dve.tensor_tensor(y_rt_t[:, :, 1, b * P:(b + 1) * P], ps_r[b % 2][:, :, :],
                                      y_rt_t[:, :, 0, b * P:(b + 1) * P], ALU.subtract).then_inc(r_low, 1)
                for c in range(HC):
                    dve.wait_ge(u_act, c + 1)
                    dve.tensor_scalar(g_hl[:, c, 0, :], g32[:, c % 2], YS, None, ALU.mult).then_inc(u_high, 1)
                    dve.wait_ge(u_high, c + 1)
                    dve.scalar_tensor_tensor(g_hl[:, c, 1, :], g32[:, c % 2], YS, g_hl[:, c, 0, :], ALU.mult,
                                             ALU.subtract).then_inc(u_low, 1)
                dve.wait_ge(base_in, 16 * B)
                for b in range(B):
                    dve.wait_ge(d_full, b + 1)
                    dve.scalar_tensor_tensor(fin[:, b], ps_u[b][:, :], 1.0 / ZS, b2h_row[:, :], ALU.mult, ALU.add
                                             ).then_inc(d_read, 1)
                    dve.wait_ge(d_read, b + 1)
                    dve.scalar_tensor_tensor(fin[:, b], fin[:, b], gains[:, b:b + 1], base[:, b], ALU.mult, ALU.add
                                             ).then_inc(fin_ready, 1)

            @block.scalar
            def _(act):
                for b in range(B):
                    act.wait_ge(r_full, b + 1)
                    act.activation(y_rt_t[:, :, 0, b * P:(b + 1) * P], ps_r[b % 2][:, :, :], ACT.Copy).then_inc(r_high, 1)
                for c in range(HC):
                    act.wait_ge(u_full, c + 1)
                    if c >= 2:
                        act.wait_ge(u_low, c - 1)
                    act.activation(g32[:, c % 2], ps_u[c % 4][:, :], ACT.Gelu, bias=b1h_sb[:, c:c + 1], scale=1.0 / ZS
                                   ).then_inc(u_act, 1)

            @block.tensor
            def _(pe):
                pe.wait_ge(sel_ready, 1)
                pe.matmul(ps_w[:, 0, :], before[:, :], chosen[:, :], start=True, stop=True)
                pe.matmul(ps_w[:, 1, :], ones[:, :], chosen[:, :], start=True, stop=True).then_inc(prefix_ready, 1)
                pe.wait_ge(facts_ready, 1)
                pe.matmul(ps_f[:, :, :].rearrange("p b n -> p (b n)"), keep["ones16"][:, :], keep["zeros"][:, 0:4 * B],
                          start=True, stop=False, skip_group_check=True)
                with pe.Fori(0, NT // HOT) as i:
                    for h in range(HOT):
                        pe.wait_ge(hot_ready, i * HOT + (h + 1))
                        for b in range(B):
                            last = pe.matmul(ps_f[:, b, :], hot[:, h, b * P:(b + 1) * P],
                                             facts[:, bass.ds(i * HOT + h, 1), :].rearrange("p a n -> p (a n)"),
                                             start=False, stop=False, skip_group_check=True)
                        last.then_inc(hot_used, 1)
                pe.matmul(ps_f[:, 0, 0:1], keep["ones16"][:, :], keep["zeros"][:, 0:1], start=False, stop=True,
                          skip_group_check=True).then_inc(found_ready, 1)
                for b in range(B):
                    pe.wait_ge(y_rt_ready, b + 1)
                    if b >= 2:
                        pe.wait_ge(r_low, b - 1)
                    for k in range(KC):
                        last = pe.transpose(ps_r[b % 2][:, k, :], y_rt[:, b, k * P:(k + 1) * P], keep["ident"][:, :])
                    last.then_inc(r_full, 1)
                pe.wait_ge(r_low, B)
                for c in range(HC):
                    if c >= 4:
                        pe.wait_ge(u_act, c - 3)
                    for k in range(KC):
                        for e, f in PASSES:
                            last = pe.matmul(ps_u[c % 4][:, :], w1h_sb[:, k, e, c * P:(c + 1) * P], y_rt_t[:, k, f, :],
                                             start=(k == 0 and e + f == 0), stop=(k == KC - 1 and e == 1))
                    last.then_inc(u_full, 1)
                pe.wait_ge(u_low, HC)
                pe.wait_ge(u_act, HC)
                for b in range(B):
                    for c in range(HC):
                        for e, f in PASSES:
                            last = pe.matmul(ps_u[b][:, :], g_hl[:, c, e, b * P:(b + 1) * P], w2h_sb[:, c // 4, f, c % 4, :],
                                             start=(c == 0 and e + f == 0), stop=(c == HC - 1 and e == 1))
                    last.then_inc(d_full, 1)


_INS = ["x", "adj", "adj_t", "L0_gnn_W_q", "L0_gnn_b_q", "L0_gnn_W_k", "L0_gnn_b_k", "L0_gnn_W_v_t", "L0_gnn_b_v",
        "L0_ffn_routing_token", "L0_ffn_gamma_light", "L0_ffn_w1_light", "L0_ffn_b1_light", "L0_ffn_w2_light",
        "L0_ffn_b2_light", "L0_ffn_gamma_heavy", "L0_ffn_w1_heavy", "L0_ffn_b1_heavy", "L0_ffn_w2_heavy",
        "L0_ffn_b2_heavy"]


def build(nc, shapes):
    args = [nc.dram_tensor(f"in_{n}", tuple(shapes[n]), F32, kind="ExternalInput").ap() for n in _INS]
    args.append(nc.dram_tensor("out_0", (N, D), F32, kind="ExternalOutput").ap())
    gnn_ffn_kernel(nc, *args)


def kernel(**inputs):
    import concourse.bacc as _bacc
    from concourse.bass_utils import run_bass_kernel_spmd as _run

    inputs = {k: np.asarray(v) for k, v in inputs.items()}
    inputs["adj_t"] = inputs["adj"].T
    inputs["L0_gnn_W_v_t"] = inputs["L0_gnn_W_v"].T
    arrays = {f"in_{n}": np.ascontiguousarray(inputs[n]) for n in _INS}
    nc = _bacc.Bacc("TRN2", target_bir_lowering=False, num_devices=1)
    build(nc, {n: inputs[n].shape for n in _INS})
    r = _run(nc, [arrays], core_ids=[0])
    return r.results[0]["out_0"]
```
